# Optimizing a Trainium2 kernel written in Bass

```python
import numpy as np
import jax
import jax.numpy as jnp

def _softmax(x, axis=-1):
    return jax.nn.softmax(x, axis=axis)

def _gelu(x):
    return jax.nn.gelu(x, approximate=True)

def _silu(x):
    return jax.nn.silu(x)

def _sigmoid(x):
    return jax.nn.sigmoid(x)

def _layernorm(x, axis=-1, eps=1e-05):
    m = jnp.mean(x, axis=axis, keepdims=True)
    v = jnp.var(x, axis=axis, keepdims=True)
    return (x - m) / jnp.sqrt(v + eps)

def _scatter_add(tgt, idx, src, axis=0):
    return tgt.at[idx].add(src)

def _segment_sum(src, seg, n):
    return jax.ops.segment_sum(src, seg, n)
kernel_name = 'mk_prb_d1_jaxref_r4_d99979'

def setup_inputs(seed: int=0):
    np.random.seed(seed)
    _w = jnp.asarray

    def _L0_attn_setup():
        import math
        import jax, jax.numpy as jnp
        import numpy as np
        N_EMBD = 256
        N_HEAD = 16
        HEAD_DIM = N_EMBD // N_HEAD

        def alibi_slopes(n_heads):
            start = 2.0 ** (-2.0 ** (-(math.log2(n_heads) - 3)))
            return np.array([start * start ** i for i in range(n_heads)], dtype=np.float32)
        key = jax.random.key(seed)
        k1, k2, k3 = jax.random.split(key, 3)
        B, T, C = (2, 512, N_EMBD)
        x = jax.random.normal(k1, (B, T, C), dtype=jnp.float32)
        w_attn = jax.random.normal(k2, (3 * C, C), dtype=jnp.float32) * (1.0 / math.sqrt(C))
        w_proj = jax.random.normal(k3, (C, C), dtype=jnp.float32) * (1.0 / math.sqrt(C))
        return {'x': x, 'w_attn': w_attn, 'w_proj': w_proj}
    _L0_attn_in = _L0_attn_setup()

    def _L0_ffn_setup():
        import jax, jax.numpy as jnp
        import numpy as np
        K = 2
        CAP_FACTOR = 1.25
        key = jax.random.key(seed)
        ks = jax.random.split(key, 6)
        B, T, C, H, E = (8, 512, 256, 1024, 8)
        return {'x': jax.random.normal(ks[0], (B, T, C), dtype=jnp.float32), 'Wr': jax.random.normal(ks[1], (C, E), dtype=jnp.float32) * 0.02, 'W1': jax.random.normal(ks[2], (E, C, H), dtype=jnp.float32) * 0.02, 'b1': jax.random.normal(ks[3], (E, H), dtype=jnp.float32) * 0.02, 'W2': jax.random.normal(ks[4], (E, H, C), dtype=jnp.float32) * 0.02, 'b2': jax.random.normal(ks[5], (E, C), dtype=jnp.float32) * 0.02}
    _L0_ffn_in = _L0_ffn_setup()
    _d = {'L0_attn_x': _L0_attn_in['x'], 'L0_attn_w_attn': _L0_attn_in['w_attn'], 'L0_attn_w_proj': _L0_attn_in['w_proj'], 'L0_ffn_Wr': _L0_ffn_in['Wr'], 'L0_ffn_W1': _L0_ffn_in['W1'], 'L0_ffn_b1': _L0_ffn_in['b1'], 'L0_ffn_W2': _L0_ffn_in['W2'], 'L0_ffn_b2': _L0_ffn_in['b2']}
    _x0 = _d['L0_attn_x']
    _d['L0_attn_x'] = jax.random.normal(jax.random.fold_in(jax.random.key(seed), 1), (32, 512, 256), dtype=_x0.dtype)
    del _x0
    return _d

def reference(L0_attn_x, L0_attn_w_attn, L0_attn_w_proj, L0_ffn_Wr, L0_ffn_W1, L0_ffn_b1, L0_ffn_W2, L0_ffn_b2):

    def _L0_attn_ref(x, w_attn, w_proj):
        import math
        import jax, jax.numpy as jnp
        import numpy as np
        N_EMBD = 256
        N_HEAD = 16
        HEAD_DIM = N_EMBD // N_HEAD

        def alibi_slopes(n_heads):
            start = 2.0 ** (-2.0 ** (-(math.log2(n_heads) - 3)))
            return np.array([start * start ** i for i in range(n_heads)], dtype=np.float32)
        B, T, C = x.shape
        H, D = (N_HEAD, HEAD_DIM)
        qkv = x @ w_attn.T
        q, k, v = jnp.split(qkv, 3, axis=-1)
        q = q.reshape(B, T, H, D).transpose(0, 2, 1, 3)
        k = k.reshape(B, T, H, D).transpose(0, 2, 1, 3)
        v = v.reshape(B, T, H, D).transpose(0, 2, 1, 3)
        att = jnp.einsum('bhqd,bhkd->bhqk', q, k) * (1.0 / math.sqrt(D))
        pos = jnp.arange(T)
        rel = pos[None, :] - pos[:, None]
        slopes = jnp.asarray(alibi_slopes(H))[:, None, None]
        causal = rel <= 0
        bias = jnp.where(causal, slopes * rel, -jnp.inf)
        att = att + bias[None]
        att = jax.nn.softmax(att, axis=-1)
        y = jnp.einsum('bhqk,bhkd->bhqd', att, v)
        y = y.transpose(0, 2, 1, 3).reshape(B, T, C)
        return y @ w_proj.T

    def _L0_ffn_ref(x, Wr, W1, b1, W2, b2):
        import jax, jax.numpy as jnp
        import numpy as np
        K = 2
        CAP_FACTOR = 1.25
        B, T, C = x.shape
        E = Wr.shape[1]
        capacity = int(T / E * CAP_FACTOR)
        probs = jax.nn.softmax(x @ Wr, axis=-1)
        topk_probs, topk_experts = jax.lax.top_k(probs, K)
        S = T * K
        e_flat = topk_experts.reshape(B, S)
        p_flat = topk_probs.reshape(B, S)
        x_rep = jnp.repeat(x, K, axis=1)
        onehot = jax.nn.one_hot(e_flat, E, dtype=jnp.int32)
        pos_all = jnp.cumsum(onehot, axis=1) - onehot
        pos = jnp.take_along_axis(pos_all, e_flat[..., None], axis=-1)[..., 0]
        keep = pos < capacity
        pos_c = jnp.minimum(pos, capacity - 1)
        b_idx = jnp.broadcast_to(jnp.arange(B)[:, None], (B, S))
        buf = jnp.zeros((E, B, capacity, C), dtype=x.dtype)
        buf = buf.at[e_flat, b_idx, pos_c].add(x_rep * keep[..., None].astype(x.dtype))
        h = jax.nn.relu(jnp.einsum('ebnc,ech->ebnh', buf, W1) + b1[:, None, None, :])
        y = jnp.einsum('ebnh,ehc->ebnc', h, W2) + b2[:, None, None, :]
        y_tok = y[e_flat, b_idx, pos_c]
        y_tok = y_tok * keep[..., None].astype(x.dtype) * p_flat[..., None]
        out = y_tok.reshape(B, T, K, C).sum(axis=2)
        return out
    x = L0_attn_x
    xn = _layernorm(x, axis=-1)
    x = x + _L0_attn_ref(xn, L0_attn_w_attn, L0_attn_w_proj) + _L0_ffn_ref(xn, L0_ffn_Wr, L0_ffn_W1, L0_ffn_b1, L0_ffn_W2, L0_ffn_b2)
    return x

_drawn_inputs = setup_inputs


def setup_inputs(seed=0):
    import zlib

    import numpy as np

    out = dict(_drawn_inputs(seed))
    spreads = {}
    factors = {'L0_ffn_b1': 34.903, 'L0_ffn_b2': 8.0}
    for name, (base, spread) in spreads.items():
        noise = np.random.default_rng([zlib.crc32(name.encode()), seed]).standard_normal(out[name].shape)
        drawn = base * np.exp(spread * noise) if base else spread * noise
        out[name] = jnp.asarray(drawn.astype(out[name].dtype))
    for name, factor in factors.items():
        out[name] = (out[name] * factor).astype(out[name].dtype)
    return out
```

```python
from contextlib import ExitStack

import concourse.bass as bass
from concourse import mybir

F32 = mybir.dt.float32
F16 = mybir.dt.float16
BF16 = mybir.dt.bfloat16
U32 = mybir.dt.uint32
U16 = mybir.dt.uint16
I32 = mybir.dt.int32
ALU = mybir.AluOpType
ACT = mybir.ActivationFunctionType
AX = mybir.AxisListType
RMAX = bass.bass_isa.ReduceOp.max

P = 128
T, C = 512, 256
NT = T // P
NC = C // P
NH, HD = 16, 16
E, HF = 8, 1024
CAP = int(T / E * 1.25)
NM = HF // P
GB = 4
GS = GB * CAP
H_BANKS = 2
SLOTS = E * CAP
EPS = 1e-5
X_SCALE = 1024.0
ALIBI_UP = 32.0
ROW_UP = 32768.0
HPG = 4
NG = NH // HPG
HALF = NH // 2
P_OFF = {0: 0, 1: 512, 3: 896, 2: 1024}
P_LEN = 1280
SCORE_UNITS = ((0,), (1, 3), (2,))
NU = len(SCORE_UNITS)
ROW_ALIBI, ROW_MAX = 64, 96
K_MAXIMA, K_SCORES = 96, 98
BIG = 2.0 ** 100

(M_A, M_P, M_R, V_A, V_P, V_R, A_POW, P_POW, R_POW, A_INV, SQ, QS, KS, S2, S_INV, QROW, Y_SC, ACC_DIV, ACC_SC,
 R_DIV, R_INV, M_1, M_2, M_B, V_1, V_2, V_B, W1_POW, W2_POW, H_POW, UP_DIV, UP_INV, UP_SC, DOWN_DIV, DOWN_SC,
 BOUND) = range(36)


def first_batch(b):
    return isinstance(b, int) and b == 0


def apart(eng):
    eng.nop(nofuse=True)


class Count:

    def __init__(self, before):
        self.before, self.n = before, 0

    def next(self):
        self.n += 1
        return self.before + self.n


def attention_phase(nc, top, x, waT, wpT, wr, c_mask, c_kbias, c_ident, c_maskT, xhl_dram, acc_dram, qk_dram,
                    logits, scales):
    NB = x.shape[0]
    x_v = x.rearrange("b (j p) c -> b p j c", p=P)
    with ExitStack() as ctx:
        def sb(name, shape, dt):
            return ctx.enter_context(nc.sbuf_tensor(name, shape, dt))

        def ps(name, shape, dt):
            return ctx.enter_context(nc.psum_tensor(name, shape, dt))

        def sem(name):
            return top.enter_context(nc.semaphore(name))

        def sc(n, lo=0, hi=P):
            return scales[lo:hi, n:n + 1]

        wa32 = sb("wa32", [P, NC, 3 * C], F32)
        wp32 = sb("wp32", [P, NC, C], F32)
        wr32 = sb("wr32", [P, NC, E], F32)
        wa = sb("wa", [P, 2, NC, 3 * C], F16)
        wp = sb("wp", [P, 2, NC, C], F16)
        wrs = sb("wrs", [P, NC, 2, E], F16)
        mask_q = sb("mask_q", [P, T], F32)
        ident = sb("ident", [P, P], F16)
        identb = sb("identb", [P, P], BF16)
        mask_k = sb("mask_k", [P, P], BF16)
        xin = sb("xin", [P, NT, C], F32)
        stats = sb("stats", [P, NT, 6], F32)
        mv = sb("mv", [P, NT, 2], F32)
        rstd = sb("rstd", [P, 4, NT], F32)
        xs = sb("xs", [P, NT, C], F32)
        xhl = sb("xhl", [P, NT, 2, C], F16)
        xT = sb("xT", [P, 2, NC, T], F16)
        qk_rows = sb("qk_rows", [P, 2, 2, 2, T], F16)
        q_st = sb("q_st", [P, NH, T], F16)
        k_st = sb("k_st", [P, NH, T], F16)
        v_ones = sb("v_ones", [P, NT, NH, 2 * HD], F32)
        maxima = sb("maxima", [P, 2, HPG * NT], F32)
        c_hl = sb("c_hl", [P, 2, 2, HPG * NT], F16)
        c_rows = sb("c_rows", [2 * HPG * NT, 2, P], F16)
        probs = sb("probs", [P, 2, HPG, P_LEN], F32)
        y_sums = sb("y_sums", [P, 2, T], F32)
        y_in = sb("y_in", [P, 2, T], F32)
        r_in = sb("r_in", [P, 2, T], F32)
        y_nrm = sb("y_nrm", [P, 2, T], F32)
        y_hl = sb("y_hl", [P, 2, 2, T], F16)
        x_res = sb("x_res", [P, NT, C], F32)
        acc = sb("acc", [P, NT, C], F32)

        ps_max = ps("ps_max", [P, 2, T], F32)
        ps_st = ps("ps_st", [P, 2, T], F32)
        ps_y = ps("ps_y", [P, T], F32)
        ps_c = ps("ps_c", [P, T], F32)
        ps_m = ps("ps_m", [P, 2, T], F32)

        s_w = sem("s_w")
        s_amax = sem("s_amax")
        s_all = sem("s_all")
        s_sc = sem("s_sc")
        s_whi = sem("s_whi")
        s_fill = sem("s_fill")
        s_kb = sem("s_kb")

        with nc.Block() as block:
            @block.sync
            def _(sp):
                for dst, src in ((wa32[:], waT.rearrange("(c p) n -> p c n", p=P)),
                                 (wp32[:], wpT.rearrange("(c p) n -> p c n", p=P)),
                                 (wr32[:], wr.rearrange("(c p) n -> p c n", p=P)),
                                 (mask_q[:], c_mask), (ident[:], c_ident[0]), (mask_k[:].bitcast(U16), c_maskT[0]),
                                 (identb[:].bitcast(U16), c_maskT[1])):
                    sp.dma_start(dst, src).then_inc(s_w, 16)
                sp.wait_ge(s_fill, 3)
                sp.dma_start(k_st[ROW_ALIBI:ROW_ALIBI + 3, :, :], c_kbias).then_inc(s_kb, 16)
                sp.wait_ge(s_kb, 16)
                sp.wait_ge(s_w, 7 * 16)

            @block.vector
            def _(dve):
                dve.wait_ge(s_w, 7 * 16)
                for n, w in ((M_A, wa32), (M_P, wp32), (M_R, wr32)):
                    dve.tensor_reduce(sc(n), w[:], AX.XY, ALU.max, apply_absolute_value=True).then_inc(s_amax, 1)
                dve.wait_ge(s_all, 1)
                own = Count(0)
                v3, p3 = scales[:, V_A:V_R + 1], scales[:, A_POW:R_POW + 1]
                dve.tensor_scalar(v3, v3, 1e-18, None, ALU.max).then_inc(s_sc, 1)
                dve.wait_ge(s_sc, own.next())
                dve.reciprocal(p3, v3).then_inc(s_sc, 1)
                dve.wait_ge(s_sc, own.next())
                dve.tensor_scalar(p3.bitcast(U32), p3.bitcast(U32), 0x7F800000, None,
                                  ALU.bitwise_and).then_inc(s_sc, 1)
                dve.wait_ge(s_sc, own.next())
                dve.tensor_scalar(sc(SQ), sc(A_POW), 2.0 ** 6, 1024.0, ALU.mult, ALU.min).then_inc(s_sc, 1)
                dve.wait_ge(s_sc, own.next())
                dve.tensor_scalar(sc(Y_SC), sc(A_POW), 2.0 ** 7, None, ALU.mult).then_inc(s_sc, 1)
                dve.wait_ge(s_sc, own.next())
                dve.tensor_scalar(p3, p3, 2.0 ** 15, None, ALU.mult).then_inc(s_sc, 1)
                dve.wait_ge(s_sc, own.next())
                dve.tensor_scalar(sc(ACC_DIV), sc(Y_SC), sc(P_POW), None, ALU.mult).then_inc(s_sc, 1)
                dve.wait_ge(s_sc, own.next())
                dve.tensor_scalar(sc(R_DIV), sc(R_POW), X_SCALE, None, ALU.mult).then_inc(s_sc, 1)
                dve.wait_ge(s_sc, own.next())
                dve.tensor_scalar(sc(A_INV), sc(A_POW), X_SCALE, None, ALU.mult).then_inc(s_sc, 1)
                dve.wait_ge(s_sc, own.next())
                dve.tensor_scalar(sc(S2), sc(SQ), sc(SQ), None, ALU.mult).then_inc(s_sc, 1)
                dve.wait_ge(s_sc, own.next())
                for dst, src in ((ACC_SC, ACC_DIV), (R_INV, R_DIV), (A_INV, A_INV), (S_INV, S2)):
                    dve.reciprocal(sc(dst), sc(src)).then_inc(s_sc, 1)
                    dve.wait_ge(s_sc, own.next())
                dve.tensor_scalar(sc(QROW), sc(S2), 1.0 / ALIBI_UP, None, ALU.mult).then_inc(s_sc, 1)
                dve.wait_ge(s_sc, own.next())
                dve.tensor_scalar(sc(KS), sc(SQ), sc(A_INV), None, ALU.mult).then_inc(s_sc, 1)
                dve.wait_ge(s_sc, own.next())
                dve.tensor_scalar(sc(QS), sc(KS), HD ** -0.5, None, ALU.mult).then_inc(s_sc, 1)
                dve.wait_ge(s_sc, own.next())
                dve.wait_ge(s_whi, 4)
                dve.scalar_tensor_tensor(wa[:, 1], wa32[:], sc(A_POW), wa[:, 0], ALU.mult,
                                         ALU.subtract).then_inc(s_sc, 1)
                dve.scalar_tensor_tensor(wp[:, 1], wp32[:], sc(P_POW), wp[:, 0], ALU.mult,
                                         ALU.subtract).then_inc(s_sc, 1)
                dve.scalar_tensor_tensor(wrs[:, :, 1, :], wr32[:], sc(R_POW), wrs[:, :, 0, :], ALU.mult,
                                         ALU.subtract).then_inc(s_sc, 1)
                dve.wait_ge(s_fill, 3)
                rows = slice(ROW_ALIBI, ROW_ALIBI + 3)
                dve.tensor_scalar(q_st[rows], q_st[rows], sc(QROW, ROW_ALIBI, ROW_ALIBI + 3), None,
                                  ALU.add).then_inc(s_sc, 1)

            @block.gpsimd
            def _(pool):
                pool.memset(q_st[:], 0.0).then_inc(s_fill, 1)
                pool.memset(k_st[:], 0.0).then_inc(s_fill, 1)
                pool.wait_ge(s_fill, 2)
                pool.memset(k_st[ROW_MAX:ROW_MAX + 2], ROW_UP).then_inc(s_fill, 1)
                pool.wait_ge(s_fill, 3)
                pool.memset(v_ones[:], 1.0).then_inc(s_fill, 1)
                pool.wait_ge(s_amax, 3)
                pool.partition_all_reduce(scales[:, V_A:V_R + 1], scales[:, M_A:M_R + 1], P, RMAX).then_inc(s_all, 1)

            @block.scalar
            def _(act):
                act.wait_ge(s_sc, 17)
                act.activation(wa[:, 0], wa32[:], ACT.Copy, scale=sc(A_POW)).then_inc(s_whi, 1)
                act.activation(wp[:, 0], wp32[:], ACT.Copy, scale=sc(P_POW)).then_inc(s_whi, 1)
                for c in range(NC):
                    act.activation(wrs[:, c, 0, :], wr32[:, c, :], ACT.Copy, scale=sc(R_POW)).then_inc(s_whi, 1)

        x_landed = sem("x_landed")
        xs_made = sem("xs_made")
        ln_own = sem("ln_own")
        guess_made = sem("guess_made")
        root_made = sem("root_made")
        xhl_split = sem("xhl_split")
        xhl_stored = sem("xhl_stored")
        t_ready = sem("t_ready")
        xt_hi = sem("xt_hi")
        xt_lo = sem("xt_lo")
        r_ready = sem("r_ready")
        r_kept = sem("r_kept")
        qk_ready = sem("qk_ready")
        qk_hi = sem("qk_hi")
        qk_lo = sem("qk_lo")
        v_ready = sem("v_ready")
        v_kept = sem("v_kept")
        qk_stored = [sem(f"qk_stored{h}") for h in range(2)]
        qk_stacked = [sem(f"qk_stacked{h}") for h in range(2)]
        m_ready = sem("m_ready")
        m_done = sem("m_done")
        c_own = sem("c_own")
        c_turned = sem("c_turned")
        c_kept = sem("c_kept")
        c_in = [sem(f"c_in{g}") for g in range(NG)]
        st_ready = sem("st_ready")
        exp_done = sem("exp_done")
        pv_ready = sem("pv_ready")
        y_kept = sem("y_kept")
        y_moved = [sem(f"y_moved{n}") for n in range(2)]
        y_own = sem("y_own")
        y_split = sem("y_split")
        xr_landed = sem("xr_landed")
        p_ready = sem("p_ready")
        p_kept = sem("p_kept")
        acc_stored = sem("acc_stored")

        UNITS = NH * NT
        STU = NH * NU
        ROOT_STEPS = 16

        with nc.Block() as block:
            @block.sync
            def _(sp):
                def load_x(b):
                    sp.wait_ge(xs_made, b)
                    sp.dma_start(xin[:], x_v[b]).then_inc(x_landed, 16)

                def store_xhl(b):
                    sp.wait_ge(xhl_split, 2 * b + 2)
                    sp.dma_start(xhl_dram[b], xhl[:]).then_inc(xhl_stored, 16)

                def store_qk(b, h):
                    sp.wait_ge(qk_lo, 4 * b + 2 * h + 2)
                    sp.dma_start(qk_dram[b, h].rearrange("q l p t -> p q l t"), qk_rows[:, h]).then_inc(qk_stored[h], 16)

                def stack_qk(b, h):
                    if not first_batch(b):
                        sp.wait_ge(st_ready, STU * (b - 1) + (h + 1) * STU // 2)
                    sp.wait_ge(qk_stored[h], 16 * (b + 1))
                    hs = slice(h * HALF, (h + 1) * HALF)
                    for qk, stack, parts in ((0, q_st, (0, 1, 0)), (1, k_st, (0, 0, 1))):
                        for n, part in enumerate(parts):
                            sp.dma_start(stack[n * HD:(n + 1) * HD, hs, :],
                                         qk_dram[b, h, qk, part].rearrange("(h d) t -> d h t", d=HD)
                                         ).then_inc(qk_stacked[h], 16)

                def rows_c(b, g):
                    sp.wait_ge(c_kept, 4 * b + g + 1)
                    for part in range(2):
                        n = HPG * NT
                        sp.dma_start(q_st[ROW_MAX + part:ROW_MAX + part + 1, g * HPG:(g + 1) * HPG, :]
                                     .rearrange("o h (t q) -> o (h t) q", q=P),
                                     c_rows[part * n:(part + 1) * n, g % 2, :]).then_inc(c_in[g], 16)

                def move_y(b, g):
                    sp.wait_ge(y_kept, 4 * b + g + 1)
                    apart(sp)
                    if not first_batch(b):
                        sp.wait_ge(y_own, 2 * (2 * (b - 1) + g // 2 + 1))
                    for j in range(HPG):
                        at = (g % 2 * HPG + j) * HD
                        for dst, off in ((y_in, 0), (r_in, HD)):
                            sp.dma_start(dst[at:at + HD, g // 2, :],
                                         y_sums[32 * j + off:32 * j + off + HD, g % 2, :]).then_inc(y_moved[g % 2], 16)

                def load_res(b):
                    if not first_batch(b):
                        sp.wait_ge(p_kept, 2 * b)
                    sp.dma_start(x_res[:], x_v[b]).then_inc(xr_landed, 16)

                def store_acc(b):
                    for n in range(2):
                        sp.wait_ge(p_kept, 2 * b + n + 1)
                        sp.dma_start(acc_dram[b, :, 2 * n:2 * n + 2], acc[:, 2 * n:2 * n + 2]).then_inc(acc_stored, 16)

                def turn(i, first=False, last=False):
                    if not last:
                        load_x(i + 1)
                    if not first:
                        move_y(i - 1, 3)
                        load_res(i - 1)
                    rows_c(i, 0)
                    if not last:
                        store_xhl(i + 1)
                    rows_c(i, 1)
                    if not first:
                        store_acc(i - 1)
                    if not last:
                        store_qk(i + 1, 0)
                    move_y(i, 0)
                    rows_c(i, 2)
                    if not last:
                        store_qk(i + 1, 1)
                        stack_qk(i + 1, 0)
                    rows_c(i, 3)
                    move_y(i, 1)
                    move_y(i, 2)
                    if not last:
                        stack_qk(i + 1, 1)

                sp.dma_start(xin[:], x_v[0]).then_inc(x_landed, 16)
                store_xhl(0)
                for h in range(2):
                    store_qk(0, h)
                    stack_qk(0, h)
                turn(0, first=True)
                with sp.Fori(1, NB - 1) as i:
                    turn(i)
                turn(NB - 1, last=True)
                move_y(NB - 1, 3)
                load_res(NB - 1)
                store_acc(NB - 1)
                sp.wait_ge(xhl_stored, 16 * NB)
                sp.wait_ge(acc_stored, 32 * NB)

            @block.gpsimd
            def _(pool):
                def split_x(b):
                    v, r, a, d = rstd[:, 0, :], rstd[:, 2, :], rstd[:, 1, :], rstd[:, 3, :]
                    own = Count(ROOT_STEPS * b)
                    pool.wait_ge(guess_made, b + 1)
                    for step in range(4):
                        up = X_SCALE if step == 3 else 1.0
                        pool.tensor_tensor(a, r, r, ALU.mult).then_inc(root_made, 1)
                        pool.wait_ge(root_made, own.next())
                        pool.tensor_tensor(d, a, v, ALU.mult).then_inc(root_made, 1)
                        pool.wait_ge(root_made, own.next())
                        apart(pool)
                        pool.tensor_scalar(a, d, -0.5 * up, 1.5 * up, ALU.mult, ALU.add).then_inc(root_made, 1)
                        pool.wait_ge(root_made, own.next())
                        pool.tensor_tensor(r, a, r, ALU.mult).then_inc(root_made, 1)
                        pool.wait_ge(root_made, own.next())
                    assert own.n == ROOT_STEPS
                    pool.wait_ge(xs_made, b + 1)
                    if not first_batch(b):
                        pool.wait_ge(t_ready, 2 * b)
                        pool.wait_ge(xhl_stored, 16 * b)
                    apart(pool)
                    pool.tensor_copy(xhl[:, :, 0, :], xs[:]).then_inc(xhl_split, 1)
                    pool.wait_ge(xhl_split, 2 * b + 1)
                    pool.tensor_tensor(xhl[:, :, 1, :], xs[:], xhl[:, :, 0, :], ALU.subtract).then_inc(xhl_split, 1)

                def split_y(b, n):
                    if not first_batch(b):
                        pool.wait_ge(p_ready, 2 * b)
                    pool.wait_ge(y_own, 4 * b + 2 * n + 2)
                    apart(pool)
                    pool.tensor_copy(y_hl[:, 0, n], y_nrm[:, n]).then_inc(y_split, 1)
                    pool.wait_ge(y_split, 4 * b + 2 * n + 1)
                    pool.tensor_tensor(y_hl[:, 1, n], y_nrm[:, n], y_hl[:, 0, n], ALU.subtract).then_inc(y_split, 1)

                def turn(i, first=False, last=False):
                    if not first:
                        split_y(i - 1, 1)
                    if not last:
                        split_x(i + 1)
                    split_y(i, 0)

                split_x(0)
                turn(0, first=True)
                with pool.Fori(1, NB - 1) as i:
                    turn(i)
                turn(NB - 1, last=True)
                split_y(NB - 1, 1)

            @block.vector
            def _(dve):
                LN_STEPS = 2 * NT + 2

                def layer_norm(b):
                    own = Count(LN_STEPS * b)
                    dve.wait_ge(x_landed, 16 * (b + 1))
                    for j in range(NT):
                        dve.bn_stats(stats[:, j, :], xin[:, j, :]).then_inc(ln_own, 1)
                        own.next()
                    dve.wait_ge(ln_own, own.before + NT)
                    apart(dve)
                    for j in range(NT):
                        dve.bn_aggr(mv[:, j, :], stats[:, j, :]).then_inc(ln_own, 1)
                        done = own.next()
                    dve.wait_ge(ln_own, done)
                    var = mv[:, :, 1]
                    r0, r1 = rstd[:, 0, :], rstd[:, 1, :]
                    dve.tensor_scalar(r0, var, EPS, None, ALU.add).then_inc(ln_own, 1)
                    dve.wait_ge(ln_own, own.next())
                    bits = r1.bitcast(U32)
                    dve.tensor_scalar(bits, r0.bitcast(U32), 1, None, ALU.logical_shift_right).then_inc(ln_own, 1)
                    dve.wait_ge(ln_own, own.next())
                    dve.tensor_scalar(rstd[:, 2, :].bitcast(I32), r1.bitcast(I32), -1.0, float(0x5F3759DF), ALU.mult, ALU.add
                                      ).then_inc(guess_made, 1)
                    assert own.n == LN_STEPS

                def scale_x(b):
                    dve.wait_ge(root_made, ROOT_STEPS * (b + 1))
                    if not first_batch(b):
                        dve.wait_ge(xhl_split, 2 * b)
                    for j in range(NT):
                        last = dve.tensor_scalar(xs[:, j, :], xin[:, j, :], mv[:, j, 0:1], rstd[:, 2, j:j + 1],
                                                 ALU.subtract, ALU.mult)
                    last.then_inc(xs_made, 1)

                def keep_xt(b):
                    dve.wait_ge(t_ready, 2 * b + 2)
                    dve.tensor_copy(xT[:, 1], ps_m[:, 1, :].bitcast(F16).rearrange("p (c t) -> p c t", c=NC)
                                    ).then_inc(xt_lo, 1)

                def keep_logits(b):
                    dve.wait_ge(r_ready, b + 1)
                    dve.tensor_reduce(logits[:, b], ps_m[:, 0, 0:NT * 2 * E].rearrange("p (j l e) -> p j e l", j=NT, l=2),
                                      AX.X, ALU.add).then_inc(r_kept, 1)

                def low_qk(b, n):
                    h, qk = n // 2, n % 2
                    dve.wait_ge(qk_hi, 4 * b + n + 1)
                    dve.scalar_tensor_tensor(qk_rows[:, h, qk, 1, :], ps_m[:, 1 - qk, :], sc(KS if qk else QS),
                                             qk_rows[:, h, qk, 0, :], ALU.mult, ALU.subtract).then_inc(qk_lo, 1)

                def maxima_of(b, g, j):
                    for qt in range(NT):
                        u = (g * HPG + j) * NT + qt
                        dve.wait_ge(m_ready, UNITS * b + u + 1)
                        apart(dve)
                        n = (qt + 1) * P
                        dve.tensor_tensor_reduce(out=ps_max[:, u % 2, 0:n], in0=ps_max[:, u % 2, 0:n], in1=mask_q[:, T - n:T],
                                                 scale=1.0, scalar=-3e38, op0=ALU.add, op1=ALU.max,
                                                 accum_out=maxima[:, g % 2, j * NT + qt:j * NT + qt + 1]
                                                 ).then_inc(m_done, 1)

                def negate(b, g):
                    dve.wait_ge(m_done, UNITS * b + (g + 1) * HPG * NT)
                    if g >= 2 or not first_batch(b):
                        dve.wait_ge(c_turned, 4 * b + g - 1)
                    dve.tensor_scalar(c_hl[:, g % 2, 0], maxima[:, g % 2], -1.0 / ROW_UP, None, ALU.mult
                                      ).then_inc(c_own, 1)
                    dve.wait_ge(c_own, 2 * (4 * b + g) + 1)
                    dve.scalar_tensor_tensor(c_hl[:, g % 2, 1], maxima[:, g % 2], -1.0 / ROW_UP, c_hl[:, g % 2, 0],
                                             ALU.mult, ALU.subtract).then_inc(c_own, 1)

                def normalise(b, n):
                    for s in range(2):
                        dve.wait_ge(y_moved[s], 256 * b + 128 * (n + 1))
                    if not first_batch(b):
                        dve.wait_ge(y_split, 4 * (b - 1) + 2 * n + 2)
                    dve.reciprocal(r_in[:, n], r_in[:, n]).then_inc(y_own, 1)
                    dve.wait_ge(y_own, 4 * b + 2 * n + 1)
                    dve.scalar_tensor_tensor(y_nrm[:, n], y_in[:, n], sc(Y_SC), r_in[:, n], ALU.mult, ALU.mult
                                             ).then_inc(y_own, 1)

                def add_input(b, n):
                    if n == 0:
                        dve.wait_ge(xr_landed, 16 * (b + 1))
                        if not first_batch(b):
                            dve.wait_ge(acc_stored, 32 * b)
                    dve.wait_ge(p_ready, 2 * b + n + 1)
                    dve.scalar_tensor_tensor(acc[:, 2 * n:2 * n + 2], ps_m[:, 1 - n, :].rearrange("p (j c) -> p j c", c=C),
                                             sc(ACC_SC), x_res[:, 2 * n:2 * n + 2], ALU.mult, ALU.add
                                             ).then_inc(p_kept, 1)

                def turn(i, first=False, last=False):
                    prev = i - 1
                    for j in range(HPG):
                        maxima_of(i, 0, j)
                    negate(i, 0)
                    if not first:
                        normalise(prev, 1)
                    if not last:
                        layer_norm(i + 1)
                    for j in range(3):
                        maxima_of(i, 1, j)
                        if j == 0 and not last:
                            scale_x(i + 1)
                    if not last:
                        keep_xt(i + 1)
                    maxima_of(i, 1, 3)
                    negate(i, 1)
                    if not last:
                        keep_logits(i + 1)
                    for j in range(HPG):
                        maxima_of(i, 2, j)
                        if j < 2 and not first:
                            add_input(prev, j)
                        if j in (1, 2) and not last:
                            low_qk(i + 1, j - 1)
                    negate(i, 2)
                    for j in range(HPG):
                        maxima_of(i, 3, j)
                        if j in (0, 2) and not last:
                            low_qk(i + 1, 2 + j // 2)
                    negate(i, 3)
                    normalise(i, 0)

                layer_norm(0)
                scale_x(0)
                keep_xt(0)
                keep_logits(0)
                for n in range(4):
                    low_qk(0, n)
                turn(0, first=True)
                with dve.Fori(1, NB - 1) as i:
                    turn(i)
                turn(NB - 1, last=True)
                normalise(NB - 1, 1)
                add_input(NB - 1, 0)
                add_input(NB - 1, 1)

            @block.scalar
            def _(act):
                def keep_xt(b):
                    act.wait_ge(t_ready, 2 * b + 1)
                    act.activation(xT[:, 0], ps_m[:, 0, :].bitcast(F16).rearrange("p (c t) -> p c t", c=NC), ACT.Copy
                                   ).then_inc(xt_hi, 1)

                def high_qk(b, n):
                    h, qk = n // 2, n % 2
                    act.wait_ge(qk_ready, 4 * b + n + 1)
                    if not first_batch(b):
                        act.wait_ge(qk_stored[h], 16 * b)
                    act.activation(qk_rows[:, h, qk, 0, :], ps_m[:, 1 - qk, :], ACT.Copy, scale=sc(KS if qk else QS)
                                   ).then_inc(qk_hi, 1)

                def keep_v(b, n):
                    act.wait_ge(v_ready, 2 * b + n + 1)
                    if not first_batch(b):
                        act.wait_ge(pv_ready, 4 * b)
                    act.activation(v_ones[:, 2 * n:2 * n + 2, :, 0:HD].rearrange("p j h d -> p (j h) d"),
                                   ps_m[:, 1 - n, :].rearrange("p (jh d) -> p jh d", d=HD), ACT.Copy, scale=sc(A_INV)
                                   ).then_inc(v_kept, 1)

                def keep_c(b, g):
                    act.wait_ge(c_turned, 4 * b + g + 1)
                    if g >= 2:
                        act.wait_ge(c_in[g - 2], 32 * (b + 1))
                    elif not first_batch(b):
                        act.wait_ge(c_in[g + 2], 32 * b)
                    act.activation(c_rows[:, g % 2, :], ps_c[0:2 * HPG * NT, 0:P // 2].bitcast(F16), ACT.Copy
                                   ).then_inc(c_kept, 1)

                def exps(b, g, j):
                    h = g * HPG + j
                    if j == 0 and (g >= 2 or not first_batch(b)):
                        act.wait_ge(pv_ready, 4 * b + g - 1)
                    for u in range(NU):
                        n = h * NU + u
                        act.wait_ge(st_ready, STU * b + n + 1)
                        size = min(T, P_LEN - u * T)
                        act.activation(probs[:, g % 2, j, u * T:u * T + size], ps_st[:, n % 2, 0:size], ACT.Exp,
                                       scale=sc(S_INV)).then_inc(exp_done, 1)

                def keep_y(b, g):
                    act.wait_ge(pv_ready, 4 * b + g + 1)
                    if g >= 2:
                        act.wait_ge(y_moved[g % 2], 256 * b + 128)
                    elif not first_batch(b):
                        act.wait_ge(y_moved[g % 2], 256 * b)
                    act.activation(y_sums[:, g % 2, :], ps_y[:], ACT.Copy).then_inc(y_kept, 1)

                def turn(i, first=False, last=False):
                    keep_c(i, 0)
                    if not last:
                        keep_xt(i + 1)
                    exps(i, 0, 0)
                    keep_c(i, 1)
                    exps(i, 0, 1)
                    if not last:
                        high_qk(i + 1, 0)
                    exps(i, 0, 2)
                    if not last:
                        high_qk(i + 1, 1)
                    exps(i, 0, 3)
                    exps(i, 1, 0)
                    keep_c(i, 2)
                    keep_y(i, 0)
                    if not last:
                        high_qk(i + 1, 2)
                    exps(i, 1, 1)
                    exps(i, 1, 2)
                    if not last:
                        high_qk(i + 1, 3)
                    exps(i, 1, 3)
                    exps(i, 2, 0)
                    keep_c(i, 3)
                    keep_y(i, 1)
                    for j in range(1, HPG):
                        exps(i, 2, j)
                    exps(i, 3, 0)
                    keep_y(i, 2)
                    for j in range(1, HPG):
                        exps(i, 3, j)
                    keep_y(i, 3)
                    if not last:
                        keep_v(i + 1, 0)
                        keep_v(i + 1, 1)

                act.wait_ge(s_fill, 4)
                keep_xt(0)
                for n in range(4):
                    high_qk(0, n)
                keep_v(0, 0)
                keep_v(0, 1)
                turn(0, first=True)
                with act.Fori(1, NB - 1) as i:
                    turn(i)
                turn(NB - 1, last=True)

            @block.tensor
            def _(pe):
                def products(out, left, right):
                    terms = [(l, r, c) for c in range(NC) for l, r in ((0, 0), (1, 0), (0, 1))]
                    for n, (l, r, c) in enumerate(terms):
                        last = pe.matmul(out, left(l, c), right(r, c), start=(n == 0), stop=(n == len(terms) - 1),
                                         skip_group_check=True)
                    return last

                def transpose_x(b):
                    for part in range(2):
                        pe.wait_ge(xhl_split, 2 * b + part + 1)
                        if part == 0 and not first_batch(b):
                            pe.wait_ge(v_kept, 2 * b)
                        bank = ps_m[:, part, :].bitcast(F16).rearrange("p (c t) -> p c t", c=NC)
                        for c in range(NC):
                            for j in range(NT):
                                last = pe.transpose(bank[:, c, j * P:(j + 1) * P], xhl[:, j, part, c * P:(c + 1) * P],
                                                    ident[:])
                        last.then_inc(t_ready, 1)

                def router(b):
                    pe.wait_ge(xt_hi, b + 1)
                    pe.wait_ge(xt_lo, b + 1)
                    for j in range(NT):
                        for n in range(2 * NC):
                            part, c = n // NC, n % NC
                            last = pe.matmul(ps_m[:, 0, j * 2 * E:(j + 1) * 2 * E], xT[:, part, c, j * P:(j + 1) * P],
                                             wrs[:, c].rearrange("p l e -> p (l e)"), start=(n == 0),
                                             stop=(n == 2 * NC - 1), skip_group_check=True)
                    last.then_inc(r_ready, 1)

                def qk(b, n, after_proj):
                    h, is_k = n // 2, n % 2
                    if n >= 2:
                        pe.wait_ge(qk_lo, 4 * b + n - 1)
                    elif after_proj is not None:
                        pe.wait_ge(p_kept, 2 * after_proj + n + 1)
                    elif n == 1:
                        pe.wait_ge(r_kept, b + 1)
                    at = is_k * C + h * P
                    products(ps_m[:, 1 - is_k, :], lambda l, c: wa[:, l, c, at:at + P], lambda r, c: xT[:, r, c, :]
                             ).then_inc(qk_ready, 1)

                def values(b, n):
                    pe.wait_ge(qk_lo, 4 * b + 3 + n)
                    for j in (2 * n, 2 * n + 1):
                        last = products(ps_m[:, 1 - n, (j % 2) * C:(j % 2 + 1) * C],
                                        lambda l, c: xT[:, l, c, j * P:(j + 1) * P],
                                        lambda r, c: wa[:, r, c, 2 * C:3 * C])
                    last.then_inc(v_ready, 1)

                def project(b, n, bank_free):
                    pe.wait_ge(y_split, 4 * b + 4)
                    pe.wait_ge(*bank_free)
                    for j in (2 * n, 2 * n + 1):
                        last = products(ps_m[:, 1 - n, (j % 2) * C:(j % 2 + 1) * C],
                                        lambda l, c: y_hl[:, l, c, j * P:(j + 1) * P], lambda r, c: wp[:, r, c, :])
                    last.then_inc(p_ready, 1)

                def score_maxima(b, g, j):
                    h = g * HPG + j
                    if j == 0:
                        pe.wait_ge(qk_stacked[g // 2], 96 * (b + 1))
                    for qt in range(NT):
                        u = h * NT + qt
                        if u >= 2 or not first_batch(b):
                            pe.wait_ge(m_done, UNITS * b + u - 1)
                        n = (qt + 1) * P
                        pe.matmul(ps_max[:, u % 2, 0:n], q_st[0:K_MAXIMA, h, qt * P:n], k_st[0:K_MAXIMA, h, 0:n],
                                  start=True, stop=True).then_inc(m_ready, 1)

                def turn_c(b, g):
                    pe.wait_ge(c_own, 2 * (4 * b + g) + 2)
                    if g >= 1 or not first_batch(b):
                        pe.wait_ge(c_kept, 4 * b + g)
                    pe.transpose(ps_c[0:2 * HPG * NT, 0:P // 2].bitcast(F16),
                                 c_hl[:, g % 2].rearrange("p l n -> p (l n)"), ident[:]).then_inc(c_turned, 1)

                def scores(b, g, j):
                    h = g * HPG + j
                    if j == 0:
                        pe.wait_ge(c_in[g], 32 * (b + 1))
                    for u, tiles in enumerate(SCORE_UNITS):
                        n = h * NU + u
                        if n >= 2 or not first_batch(b):
                            pe.wait_ge(exp_done, STU * b + n - 1)
                        for kt in tiles:
                            at, size = P_OFF[kt] - u * T, T - kt * P
                            pe.matmul(ps_st[:, n % 2, at:at + size], k_st[0:K_SCORES, h, kt * P:(kt + 1) * P],
                                      q_st[0:K_SCORES, h, kt * P:T], start=True, stop=False, skip_group_check=True)
                            last = pe.matmul(ps_st[:, n % 2, at:at + P], identb[:], mask_k[:], start=False, stop=True,
                                             skip_group_check=True)
                        last.then_inc(st_ready, 1)

                def weighted_sums(b, g):
                    pe.wait_ge(exp_done, STU * b + (g + 1) * HPG * NU)
                    if g == 0:
                        pe.wait_ge(v_kept, 2 * (b + 1))
                    if g >= 1 or not first_batch(b):
                        pe.wait_ge(y_kept, 4 * b + g)
                    for kt in range(NT):
                        for j in range(HPG):
                            last = pe.matmul(ps_y[32 * j:32 * j + 32, kt * P:T], v_ones[:, kt, g * HPG + j, :],
                                             probs[:, g % 2, j, P_OFF[kt]:P_OFF[kt] + T - kt * P],
                                             start=(kt == 0), stop=(kt == NT - 1), skip_group_check=True)
                    last.then_inc(pv_ready, 1)

                def turn(i, first=False, last=False):
                    prev = None if first else i - 1
                    for j in range(HPG):
                        score_maxima(i, 0, j)
                    for j in range(HPG):
                        score_maxima(i, 1, j)
                        if j == 0:
                            turn_c(i, 0)
                        if j == 2 and not last:
                            transpose_x(i + 1)
                    if not last:
                        router(i + 1)
                    for j in range(HPG):
                        score_maxima(i, 2, j)
                        scores(i, 0, j)
                        if j == 0:
                            turn_c(i, 1)
                        if j < 2 and not first:
                            project(prev, j, (v_kept, 2 * NB) if last else (xt_lo, i + 2) if j == 0 else (r_kept, i + 2))
                        if j in (1, 2) and not last:
                            qk(i + 1, j - 1, prev)
                    for j in range(HPG):
                        score_maxima(i, 3, j)
                        scores(i, 1, j)
                        if j == 0:
                            turn_c(i, 2)
                            weighted_sums(i, 0)
                        if j in (0, 2) and not last:
                            qk(i + 1, 2 + j // 2, None)
                    scores(i, 2, 0)
                    turn_c(i, 3)
                    weighted_sums(i, 1)
                    for j in range(1, HPG):
                        scores(i, 2, j)
                        if j < 3 and not last:
                            values(i + 1, j - 1)
                    scores(i, 3, 0)
                    weighted_sums(i, 2)
                    for j in range(1, HPG):
                        scores(i, 3, j)
                    weighted_sums(i, 3)

                transpose_x(0)
                router(0)
                for n in range(4):
                    qk(0, n, None)
                values(0, 0)
                values(0, 1)
                turn(0, first=True)
                with pe.Fori(1, NB - 1) as i:
                    turn(i)
                turn(NB - 1, last=True)
                project(NB - 1, 0, (p_kept, 2 * NB - 2))
                project(NB - 1, 1, (p_kept, 2 * NB - 2))



def routing_phase(nc, top, w1, b1T, w2, b2, c_tri, c_erank, c_erow, c_brow, logits, scales, pos_slot, weight, row_of,
                  w1s, w2s, b1s, b2b):
    NB = logits.shape[1]
    N = NB * NT
    with ExitStack() as ctx:
        def sb(name, shape, dt):
            return ctx.enter_context(nc.sbuf_tensor(name, shape, dt))

        def sem(name):
            return top.enter_context(nc.semaphore(name))

        def sc(n):
            return scales[:, n:n + 1]

        stage = w2s[:].rearrange("p l k e n -> p (l k e n)").bitcast(F32).rearrange("p (e n) -> p e n", e=E)
        RING = 4
        ring = sb("ring", [P, RING, NC * HF], F32)
        amax = sb("amax", [P, 2, E], F32)
        tri = sb("tri", [P, 2, P], BF16)
        erank = sb("erank", [P, E], F32)
        erow = sb("erow", [P, E], F32)
        brow = sb("brow", [P, NB], F32)
        one = sb("one", [P, 4, N], F32)
        pk = sb("pk", [P, 2, N], F32)
        t0 = sb("t0", [P, N, E], F32)
        t1 = sb("t1", [P, N, E], F32)
        oh = sb("oh", [P, 2, N, E], F32)
        taken = sb("taken", [P, NB, NT, E], BF16)
        before = sb("before", [P, NB, NT, E], BF16)
        ps_pos = ctx.enter_context(nc.psum_tensor("ps_pos", [P, N * E], F32))

        s_c = sem("r_const")
        s_w1 = [sem(f"w1_landed{e}") for e in range(E)]
        s_w2 = [sem(f"w2_landed{n}") for n in range(RING)]
        s_amax = sem("w_amax")
        s_seen = sem("w2_seen")
        s_top = sem("w_amax_all")
        s_own = sem("r_own")
        s_exp = sem("r_exp")
        s_pos = sem("r_pos")
        s_route = sem("r_route")
        s_pow = sem("w_pow")
        s_hi = sem("w_hi")
        s_lo = sem("w_lo")
        s_b1 = sem("b1_scaled")

        with nc.Block() as block:
            @block.sync
            def _(sp):
                for dst, src in ((tri[:].bitcast(U16), c_tri.rearrange("n p q -> p n q")), (erank[:], c_erank), (erow[:], c_erow),
                                 (brow[:], c_brow), (b1s[:], b1T),
                                 (b2b[:], b2.rearrange("e c -> (e c)").partition_broadcast(P))):
                    sp.dma_start(dst, src).then_inc(s_c, 16)
                for e in range(E):
                    sp.dma_start(stage[:, e].rearrange("p (c h) -> p c h", c=NC),
                                 w1[e].rearrange("(c p) h -> p c h", p=P)).then_inc(s_w1[e], 16)
                for n in range(2 * E):
                    if n >= RING:
                        if n - RING < E:
                            sp.wait_ge(s_seen, n - RING + 1)
                        else:
                            sp.wait_ge(s_lo, n - RING + 1)
                    sp.dma_start(ring[:, n % RING].rearrange("p (k n) -> p k n", k=NM),
                                 w2[n % E].rearrange("(k p) n -> p k n", p=P)).then_inc(s_w2[n % RING], 16)
                for n in range(RING):
                    sp.wait_ge(s_w2[n], 16 * 2 * E // RING)

            @block.gpsimd
            def _(pool):
                pool.wait_ge(s_amax, 1)
                pool.partition_all_reduce(scales[:, V_1:V_1 + 1], scales[:, M_1:M_1 + 1], P, RMAX).then_inc(s_top, 1)
                pool.wait_ge(s_top, 1)
                pool.partition_all_reduce(scales[:, V_B:V_B + 1], scales[:, M_B:M_B + 1], P, RMAX).then_inc(s_top, 1)
                pool.wait_ge(s_amax, 2)
                pool.wait_ge(s_top, 2)
                pool.partition_all_reduce(scales[:, V_2:V_2 + 1], scales[:, M_2:M_2 + 1], P, RMAX).then_inc(s_top, 1)

            @block.scalar
            def _(act):
                act.wait_ge(s_route, 1)
                act.activation(t1[:], t0[:], ACT.Exp, scale=sc(R_INV)).then_inc(s_exp, 1)
                act.wait_ge(s_pow, 1)
                for e in range(E):
                    act.activation(w1s[:, 0, :, e, :], stage[:, e].rearrange("p (c h) -> p c h", c=NC), ACT.Copy,
                                   scale=sc(W1_POW)).then_inc(s_hi, 1)
                act.wait_ge(s_c, 6 * 16)
                act.activation(b1s[:], b1s[:], ACT.Copy, scale=sc(H_POW)).then_inc(s_b1, 1)
                act.wait_ge(s_pow, 2)
                for e in range(E):
                    act.wait_ge(s_w2[e % RING], 16 * ((E + e) // RING + 1))
                    if e == 0:
                        act.wait_ge(s_lo, E)
                    act.activation(w2s[:, 0, :, e, :], ring[:, e % RING].rearrange("p (k n) -> p k n", k=NM), ACT.Copy,
                                   scale=sc(W2_POW)).then_inc(s_hi, 1)

            @block.tensor
            def _(pe):
                pe.wait_ge(s_c, 6 * 16)
                pe.wait_ge(s_route, 2)
                flat_taken = taken[:].rearrange("p b j e -> p (b j e)")
                flat_before = before[:].rearrange("p b j e -> p (b j e)")
                for at in range(0, N * E, 512):
                    to = min(at + 512, N * E)
                    pe.matmul(ps_pos[:, at:to], tri[:, 0], flat_taken[:, at:to], start=True, stop=False)
                    last = pe.matmul(ps_pos[:, at:to], tri[:, 1], flat_before[:, at:to], start=False, stop=True)
                last.then_inc(s_pos, 1)

            @block.vector
            def _(dve):
                own = Count(0)

                def bc(v):
                    return v.rearrange("p (n o) -> p n o", o=1).to_broadcast([P, N, E])

                def row(v):
                    return v.rearrange("p (o e) -> p o e", o=1).to_broadcast([P, N, E])

                lg = logits.rearrange("p b j e -> p (b j) e")
                dve.tensor_reduce(one[:, 0], lg, AX.X, ALU.max).then_inc(s_own, 1)
                dve.wait_ge(s_own, own.next())
                dve.tensor_tensor(t0[:], lg, bc(one[:, 0]), ALU.subtract).then_inc(s_route, 1)
                for e in range(E):
                    dve.wait_ge(s_w1[e], 16)
                    dve.tensor_reduce(amax[:, 0, e:e + 1], stage[:, e], AX.X, ALU.max, apply_absolute_value=True
                                      ).then_inc(s_own, 1)
                    done = own.next()
                dve.wait_ge(s_c, 6 * 16)
                dve.tensor_reduce(sc(M_B), b1s[:], AX.XY, ALU.max, apply_absolute_value=True).then_inc(s_own, 1)
                dve.wait_ge(s_own, own.next())
                dve.tensor_reduce(sc(M_1), amax[:, 0], AX.X, ALU.max).then_inc(s_amax, 1)
                dve.wait_ge(s_exp, 1)
                dve.tensor_reduce(one[:, 1], t1[:], AX.X, ALU.add).then_inc(s_own, 1)
                dve.wait_ge(s_own, own.next())
                dve.reciprocal(one[:, 3], one[:, 1]).then_inc(s_own, 1)
                dve.wait_ge(s_own, own.next())
                dve.tensor_tensor(t0[:], t1[:], bc(one[:, 3]), ALU.mult).then_inc(s_own, 1)
                dve.wait_ge(s_own, own.next())
                for k in range(2):
                    dve.tensor_reduce(pk[:, k], t0[:], AX.X, ALU.max).then_inc(s_own, 1)
                    dve.wait_ge(s_own, own.next())
                    dve.tensor_tensor(t1[:], t0[:], bc(pk[:, k]), ALU.is_equal).then_inc(s_own, 1)
                    dve.wait_ge(s_own, own.next())
                    dve.tensor_tensor(t1[:], t1[:], row(erank[:]), ALU.mult).then_inc(s_own, 1)
                    dve.wait_ge(s_own, own.next())
                    dve.tensor_reduce(one[:, 2], t1[:], AX.X, ALU.max).then_inc(s_own, 1)
                    dve.wait_ge(s_own, own.next())
                    dve.tensor_tensor(oh[:, k], t1[:], bc(one[:, 2]), ALU.is_equal).then_inc(s_own, 1)
                    dve.wait_ge(s_own, own.next())
                    if k == 0:
                        dve.scalar_tensor_tensor(t0[:], oh[:, 0], -2.0, t0[:], ALU.mult, ALU.add).then_inc(s_own, 1)
                        dve.wait_ge(s_own, own.next())
                dve.tensor_tensor(taken[:].rearrange("p b j e -> p (b j) e"), oh[:, 0], oh[:, 1], ALU.add
                                  ).then_inc(s_own, 1)
                dve.memset(before[:, :, 0, :], 0.0).then_inc(s_own, 1)
                own.next()
                dve.wait_ge(s_own, own.next())
                for j in range(1, NT):
                    last = dve.tensor_tensor(before[:, :, j, :], before[:, :, j - 1, :], taken[:, :, j - 1, :], ALU.add)
                    last.then_inc(s_own, 1)
                    dve.wait_ge(s_own, own.next())
                dve.wait_ge(s_route, 1)
                dve.memset(one[:, 3], 0.0).then_inc(s_route, 1)

                def power(dst, src, up):
                    dve.reciprocal(sc(dst), sc(src)).then_inc(s_own, 1)
                    dve.wait_ge(s_own, own.next())
                    dve.tensor_scalar(sc(dst).bitcast(U32), sc(dst).bitcast(U32), 0x7F800000, None, ALU.bitwise_and
                                      ).then_inc(s_own, 1)
                    dve.wait_ge(s_own, own.next())
                    return dve.tensor_scalar(sc(dst), sc(dst), up, None, ALU.mult)

                dve.wait_ge(s_top, 2)
                dve.tensor_scalar(sc(V_1), sc(V_1), 1e-18, None, ALU.max).then_inc(s_own, 1)
                dve.wait_ge(s_own, own.next())
                power(W1_POW, V_1, 2.0 ** 15).then_inc(s_own, 1)
                dve.wait_ge(s_own, own.next())
                dve.scalar_tensor_tensor(sc(BOUND), sc(V_1), float(C), sc(V_B), ALU.mult, ALU.add).then_inc(s_own, 1)
                dve.wait_ge(s_own, own.next())
                power(H_POW, BOUND, 2.0 ** 15).then_inc(s_pow, 1)
                dve.wait_ge(s_pow, 1)
                for e in range(E):
                    dve.wait_ge(s_hi, e + 1)
                    dve.scalar_tensor_tensor(w1s[:, 1, :, e, :], stage[:, e].rearrange("p (c h) -> p c h", c=NC),
                                             sc(W1_POW), w1s[:, 0, :, e, :], ALU.mult, ALU.subtract).then_inc(s_lo, 1)
                dve.wait_ge(s_pos, 1)
                dve.tensor_copy(t0[:], ps_pos[:].rearrange("p (n e) -> p n e", e=E)).then_inc(s_own, 1)
                dve.wait_ge(s_own, own.next())
                dve.tensor_scalar(t1[:], t0[:], CAP - 0.5, None, ALU.is_lt).then_inc(s_own, 1)
                dve.wait_ge(s_own, own.next())
                dve.tensor_tensor(t1[:], t1[:], taken[:].rearrange("p b j e -> p (b j) e"), ALU.mult).then_inc(s_own, 1)
                dve.wait_ge(s_own, own.next())
                ps = pos_slot[:].rearrange("p b j e -> p (b j) e")
                lgf = logits.rearrange("p b j e -> p (b j) e")
                dve.scalar_tensor_tensor(lgf, t0[:], 1.0, t1[:], ALU.add, ALU.mult).then_inc(s_own, 1)
                dve.wait_ge(s_own, own.next())
                dve.tensor_scalar(ps, lgf, -1.0, None, ALU.add).then_inc(s_own, 1)
                own.next()
                dve.tensor_scalar(t0[:], t0[:], float(CAP - 1), None, ALU.min).then_inc(s_own, 1)
                dve.wait_ge(s_own, own.next())
                dve.tensor_tensor(t0[:], t0[:], row(erow[:]), ALU.add).then_inc(s_own, 1)
                dve.wait_ge(s_own, own.next())
                for k in range(2):
                    dve.tensor_tensor(lgf, t0[:], oh[:, k], ALU.mult).then_inc(s_own, 1)
                    dve.wait_ge(s_own, own.next())
                    dve.tensor_reduce(one[:, 0], lgf, AX.X, ALU.add).then_inc(s_own, 1)
                    dve.wait_ge(s_own, own.next())
                    dve.tensor_tensor(row_of[:, k], one[:, 0].rearrange("p (b j) -> p b j", j=NT),
                                      brow[:].rearrange("p (b o) -> p b o", o=1).to_broadcast([P, NB, NT]), ALU.add
                                      ).then_inc(s_own, 1)
                    dve.wait_ge(s_own, own.next())
                    dve.tensor_tensor(lgf, t1[:], oh[:, k], ALU.mult).then_inc(s_own, 1)
                    dve.wait_ge(s_own, own.next())
                    dve.tensor_reduce(one[:, 1], lgf, AX.X, ALU.add).then_inc(s_own, 1)
                    dve.wait_ge(s_own, own.next())
                    dve.tensor_tensor(weight[:, k], pk[:, k].rearrange("p (b j) -> p b j", j=NT),
                                      one[:, 1].rearrange("p (b j) -> p b j", j=NT), ALU.mult).then_inc(s_own, 1)
                    dve.wait_ge(s_own, own.next())
                for e in range(E):
                    dve.wait_ge(s_w2[e % RING], 16 * (e // RING + 1))
                    dve.tensor_reduce(amax[:, 1, e:e + 1], ring[:, e % RING], AX.X, ALU.max, apply_absolute_value=True
                                      ).then_inc(s_seen, 1)
                dve.wait_ge(s_seen, E)
                dve.tensor_reduce(sc(M_2), amax[:, 1], AX.X, ALU.max).then_inc(s_amax, 1)
                dve.wait_ge(s_top, 3)
                dve.tensor_scalar(sc(V_2), sc(V_2), 1e-18, None, ALU.max).then_inc(s_own, 1)
                dve.wait_ge(s_own, own.next())
                power(W2_POW, V_2, 2.0 ** 15).then_inc(s_pow, 1)
                dve.wait_ge(s_pow, 2)
                dve.tensor_scalar(sc(UP_DIV), sc(W1_POW), X_SCALE, None, ALU.mult).then_inc(s_own, 1)
                dve.wait_ge(s_own, own.next())
                dve.reciprocal(sc(UP_INV), sc(UP_DIV)).then_inc(s_own, 1)
                dve.wait_ge(s_own, own.next())
                dve.tensor_tensor(sc(UP_SC), sc(UP_INV), sc(H_POW), ALU.mult).then_inc(s_own, 1)
                own.next()
                dve.tensor_tensor(sc(DOWN_DIV), sc(H_POW), sc(W2_POW), ALU.mult).then_inc(s_own, 1)
                dve.wait_ge(s_own, own.next())
                dve.reciprocal(sc(DOWN_SC), sc(DOWN_DIV)).then_inc(s_own, 1)
                for e in range(E):
                    dve.wait_ge(s_hi, E + e + 1)
                    dve.scalar_tensor_tensor(w2s[:, 1, :, e, :], ring[:, e % RING].rearrange("p (k n) -> p k n", k=NM),
                                             sc(W2_POW), w2s[:, 0, :, e, :], ALU.mult, ALU.subtract).then_inc(s_lo, 1)


def expert_phase(nc, top, c_iota, xhl_dram, acc_dram, y_dram, out, scales, spare, pos_slot, weight,
                 row_of, w1s, w2s, b1s, b2b):
    NB = pos_slot.shape[1]
    NQ = NB // GB
    assert NQ % 2 == 0
    out_v = out.rearrange("b (j p) c -> b p j c", p=P)
    TILES = ((0, P), (P, 2 * P), (2 * P, GS))
    NTI = len(TILES)
    MH = NM // 2
    with ExitStack() as ctx:
        def sb(name, shape, dt):
            return ctx.enter_context(nc.sbuf_tensor(name, shape, dt))

        def ps(name, shape, dt):
            return ctx.enter_context(nc.psum_tensor(name, shape, dt))

        def sem(name):
            return top.enter_context(nc.semaphore(name))

        def sc(n):
            return scales[:, n:n + 1]

        iota = sb("iota", [P, CAP], F16)
        xg = sb("xg", [P, 2, NT, 2, C], F16)
        place = sb("place", [P, 2, NT, E, CAP], F16)
        xb = sb("xb", [P, 2, NC, E, GB, CAP], F16)
        relu = sb("relu", [P, MH, GS], F32)
        hs = sb("hs", [P, 2, 2, MH, GS], F16)
        yo = sb("yo", [P, NTI, C], F32)
        rows_q = sb("rows_q", [P, 2, GB, NT], I32)
        yg = sb("yg", [P, NT, C], F32)
        acc = spare[:, 0:NT * C].rearrange("p (j c) -> p j c", c=C)
        ps_x = ps("ps_x", [P, 2, 512], F32)
        ps_h = ps("ps_h", [P, H_BANKS, 512], F32)
        ps_o = ps("ps_o", [P, 3, 512], F32)

        b_const = sem("b_const")
        xg_landed = [sem(f"xg_landed{n}") for n in range(2)]
        placed = sem("placed")
        d_ready = sem("d_ready")
        xb_hi = sem("xb_hi")
        xb_lo = sem("xb_lo")
        h_ready = sem("h_ready")
        relued = sem("relued")
        h_hi = sem("h_hi")
        h_lo = sem("h_lo")
        o_ready = sem("o_ready")
        o_kept = sem("o_kept")
        o_stored = sem("o_stored")
        rows_made = sem("rows_made")
        halves = sem("halves")
        yg_landed = sem("yg_landed")
        acc_landed = sem("accb_landed")
        summed = sem("summed")
        out_stored = sem("out_stored")

        with nc.Block() as block:
            @block.sync
            def _(sp):
                def load_x(q, bb):
                    n = 4 * q + bb
                    if bb >= 2 or not first_batch(q):
                        sp.wait_ge(d_ready, 8 * (n - 1))
                    sp.dma_start(xg[:, bb % 2], xhl_dram[n]).then_inc(xg_landed[bb % 2], 16)

                def load_acc(q, bb):
                    n = 4 * q + bb
                    if bb or not first_batch(q):
                        sp.wait_ge(out_stored, 16 * n)
                    sp.dma_start(acc, acc_dram[n]).then_inc(acc_landed, 16)

                def store_y(q, odd, e):
                    if e == 0 and not first_batch(q):
                        sp.wait_ge(o_stored, NTI * E * 16 * q)
                    for t, (lo, hi) in enumerate(TILES):
                        sp.wait_ge(o_kept, NTI * (E * q + e) + t + 1)
                        sp.dma_start(y_dram[odd][e * GS + lo:e * GS + hi, :],
                                     yo[0:hi - lo, t]).then_inc(o_stored, 16)

                def store_out(q, bb):
                    sp.wait_ge(summed, 2 * (4 * q + bb + 1))
                    sp.dma_start(out_v[4 * q + bb], acc).then_inc(out_stored, 16)

                def turn(q, odd, first=False, last=False):
                    load_x(q, 2)
                    load_x(q, 3)
                    if not last:
                        load_x(q + 1, 0)
                        load_x(q + 1, 1)
                    if not first:
                        load_acc(q - 1, 0)
                    for e in range(1, E):
                        store_y(q, odd, e - 1)
                        if not first and e % 2 == 0:
                            store_out(q - 1, e // 2 - 1)
                            load_acc(q - 1, e // 2)
                    if not first:
                        store_out(q - 1, GB - 1)
                    store_y(q, odd, E - 1)

                sp.dma_start(iota[:], c_iota).then_inc(b_const, 16)
                load_x(0, 0)
                load_x(0, 1)
                turn(0, 0, first=True)
                if NQ > 2:
                    with sp.Fori(0, NQ // 2 - 1) as pair:
                        turn(2 * pair + 1, 1)
                        turn(2 * pair + 2, 0)
                turn(NQ - 1, 1, last=True)
                for bb in range(GB):
                    load_acc(NQ - 1, bb)
                    store_out(NQ - 1, bb)
                sp.wait_ge(out_stored, 16 * NB)
                sp.wait_ge(o_stored, NTI * E * 16 * NQ)

            @block.gpsimd
            def _(pool):
                def high_h(q, e):
                    for n in range(NM // 2):
                        k = NM // 2 * (E * q + e) + n
                        if n % 2 == 0 and (e or not first_batch(q)):
                            if n == 0:
                                pool.wait_ge(halves, E * q + e)
                            else:
                                pool.wait_ge(o_ready, NTI * (E * q + e))
                        pool.wait_ge(relued, 2 * k + 2)
                        apart(pool)
                        at = n % 2 * 2
                        pool.tensor_copy(hs[:, n // 2, 0, at:at + 2], relu[:, at:at + 2]).then_inc(h_hi, 1)

                def gather(q, odd, n):
                    bb, k = n // 2, n % 2
                    if n == 0:
                        pool.wait_ge(o_stored, NTI * E * 16 * (q + 1))
                        pool.wait_ge(rows_made, q + 1)
                    if n or not first_batch(q):
                        pool.wait_ge(summed, 8 * q + n)
                        apart(pool)
                    for j in range(NT):
                        pool.indirect_dma_start(yg[:, j], None, y_dram[odd],
                                                bass.IndirectOffsetOnAxis(ap=rows_q[:, k, bb, j:j + 1], axis=0)
                                                ).then_inc(yg_landed, 16)

                def turn(q, odd, first=False, last=False):
                    for e in range(E):
                        high_h(q, e)
                        if not first:
                            gather(q - 1, 1 - odd, e)

                turn(0, 0, first=True)
                if NQ > 2:
                    with pool.Fori(0, NQ // 2 - 1) as pair:
                        turn(2 * pair + 1, 1)
                        turn(2 * pair + 2, 0)
                turn(NQ - 1, 1, last=True)
                for n in range(2 * GB):
                    gather(NQ - 1, 1, n)

            @block.scalar
            def _(act):
                def keep_dispatched(q, bb):
                    for c in range(NC):
                        for half in range(2):
                            u = 8 * (4 * q + bb) + 4 * c + half
                            act.wait_ge(d_ready, u + 1)
                            act.activation(xb[:, 0, c, half * 4:half * 4 + 4, bb],
                                           ps_x[:, half, 0:SLOTS // 2].rearrange("p (e s) -> p e s", s=CAP), ACT.Copy
                                           ).then_inc(xb_hi, 1)

                def hidden(q, e):
                    for m in range(NM):
                        u = NM * (E * q + e) + m
                        if m % 2 == 0 and (m >= 4 or e or not first_batch(q)):
                            act.wait_ge(h_lo, NM // 2 * (E * q + e) + m // 2 - 1)
                        act.wait_ge(h_ready, u + 1)
                        act.activation(relu[:, m % 4], ps_h[:, (NM * e + m) % H_BANKS, 0:GS], ACT.Relu,
                                       bias=b1s[:, e, m:m + 1], scale=sc(UP_SC)).then_inc(relued, 1)

                def turn(q, odd, first=False, last=False):
                    for bb in range(GB):
                        keep_dispatched(q, bb)
                    for e in range(E):
                        hidden(q, e)

                turn(0, 0, first=True)
                if NQ > 2:
                    with act.Fori(0, NQ // 2 - 1) as pair:
                        turn(2 * pair + 1, 1)
                        turn(2 * pair + 2, 0)
                turn(NQ - 1, 1, last=True)

            @block.vector
            def _(dve):
                def keep_dispatched(q, bb):
                    for c in range(NC):
                        for half in range(2):
                            u = 8 * (4 * q + bb) + 4 * c + 2 + half
                            dve.wait_ge(d_ready, u + 1)
                            dve.tensor_copy(xb[:, 1, c, half * 4:half * 4 + 4, bb],
                                            ps_x[:, half, 0:SLOTS // 2].rearrange("p (e s) -> p e s", s=CAP)
                                            ).then_inc(xb_lo, 1)

                def fill_slots(q, bb):
                    n = 4 * q + bb
                    if bb >= 2 or not first_batch(q):
                        dve.wait_ge(d_ready, 8 * (n - 1))
                    for j in range(NT):
                        dve.tensor_tensor(place[:, bb % 2, j],
                                           iota[:].rearrange("p (o s) -> p o s", o=1).to_broadcast([P, E, CAP]),
                                           pos_slot[:, n, j].rearrange("p (e o) -> p e o", o=1).to_broadcast([P, E, CAP]),
                                           ALU.is_equal).then_inc(placed, 1)

                def low_h(q, e, half):
                    for n in range(2 * half, 2 * half + 2):
                        dve.wait_ge(h_hi, NM // 2 * (E * q + e) + n + 1)
                        at = n % 2 * 2
                        dve.tensor_tensor(hs[:, half, 1, at:at + 2], relu[:, at:at + 2], hs[:, half, 0, at:at + 2],
                                          ALU.subtract).then_inc(h_lo, 1)

                def keep_y(q, e):
                    for t, (lo, hi) in enumerate(TILES):
                        u = NTI * (E * q + e) + t
                        dve.wait_ge(o_ready, u + 1)
                        if e or not first_batch(q):
                            dve.wait_ge(o_stored, NTI * 16 * (E * q + e))
                        dve.scalar_tensor_tensor(yo[0:hi - lo, t], ps_o[0:hi - lo, t, 0:C],
                                                 scales[0:hi - lo, DOWN_SC:DOWN_SC + 1], b2b[0:hi - lo, e],
                                                 ALU.mult, ALU.add).then_inc(o_kept, 1)

                def add_term(q, n):
                    bb, k = n // 2, n % 2
                    b = 4 * q + bb
                    if k == 0:
                        dve.wait_ge(acc_landed, 16 * (b + 1))
                    else:
                        dve.wait_ge(summed, 8 * q + n)
                    dve.wait_ge(yg_landed, NT * 16 * (8 * q + n + 1))
                    for j in range(NT):
                        last = dve.scalar_tensor_tensor(acc[:, j], yg[:, j], weight[:, k, b, j:j + 1], acc[:, j],
                                                        ALU.mult, ALU.add)
                    last.then_inc(summed, 1)

                def rows_for(q):
                    dve.tensor_copy(rows_q[:], row_of[:, :, bass.ds(4 * q, GB)]).then_inc(rows_made, 1)

                def turn(q, odd, first=False, last=False):
                    if not first:
                        rows_for(q - 1)
                    for bb in range(GB):
                        keep_dispatched(q, bb)
                        if bb + 2 < GB:
                            fill_slots(q, bb + 2)
                    for e in range(E):
                        low_h(q, e, 0)
                        if e > 0:
                            keep_y(q, e - 1)
                        low_h(q, e, 1)
                        if e > 0 and not first:
                            add_term(q - 1, e - 1)
                    if not first:
                        add_term(q - 1, E - 1)
                    if not last:
                        fill_slots(q + 1, 0)
                        fill_slots(q + 1, 1)
                    keep_y(q, E - 1)

                dve.wait_ge(b_const, 16)
                fill_slots(0, 0)
                fill_slots(0, 1)
                turn(0, 0, first=True)
                if NQ > 2:
                    with dve.Fori(0, NQ // 2 - 1) as pair:
                        turn(2 * pair + 1, 1)
                        turn(2 * pair + 2, 0)
                turn(NQ - 1, 1, last=True)
                rows_for(NQ - 1)
                for n in range(2 * GB):
                    add_term(NQ - 1, n)

            @block.tensor
            def _(pe):
                def dispatch(q, bb):
                    n = 4 * q + bb
                    pe.wait_ge(xg_landed[bb % 2], 32 * q + 16 * (bb // 2 + 1))
                    pe.wait_ge(placed, NT * (n + 1))
                    for c in range(NC):
                        for part in range(2):
                            for half in range(2):
                                if c or part or bb or not first_batch(q):
                                    if part:
                                        pe.wait_ge(xb_hi, 4 * n + 2 * c + half + 1)
                                    else:
                                        pe.wait_ge(xb_lo, 4 * n + 2 * c + half - 1)
                                for j in range(NT):
                                    last = pe.matmul(ps_x[:, half, 0:SLOTS // 2],
                                                     xg[:, bb % 2, j, part, c * P:(c + 1) * P],
                                                     place[:, bb % 2, j, half * 4:half * 4 + 4].rearrange("p e s -> p (e s)"),
                                                     start=(j == 0), stop=(j == NT - 1))
                                last.then_inc(d_ready, 1)

                def up(q, e, half):
                    if e == 0 and half == 0:
                        pe.wait_ge(xb_hi, 16 * (q + 1))
                        pe.wait_ge(xb_lo, 16 * (q + 1))
                    for m in range(half * MH, (half + 1) * MH):
                        u = NM * (E * q + e) + m
                        if m >= H_BANKS or e or not first_batch(q):
                            pe.wait_ge(relued, u - H_BANKS + 1)
                        terms = [(l, r, c) for c in range(NC) for l, r in ((0, 0), (1, 0), (0, 1))]
                        for n, (l, r, c) in enumerate(terms):
                            last = pe.matmul(ps_h[:, m % H_BANKS, 0:GS], w1s[:, l, c, e, m * P:(m + 1) * P],
                                             xb[:, r, c, e].rearrange("p b s -> p (b s)"),
                                             start=(n == 0), stop=(n == len(terms) - 1))
                        last.then_inc(h_ready, 1)

                def down(q, e, half):
                    pe.wait_ge(h_lo, NM // 2 * (E * q + e) + 2 * (half + 1))
                    for t, (lo, hi) in enumerate(TILES):
                        u = NTI * (E * q + e) + t
                        if half == 0 and (e or not first_batch(q)):
                            pe.wait_ge(o_kept, u - NTI + 1)
                        terms = [(l, r, k) for k in range(MH) for l, r in ((0, 0), (0, 1), (1, 0))]
                        for n, (l, r, k) in enumerate(terms):
                            last = pe.matmul(ps_o[0:hi - lo, t, 0:C], hs[:, half, l, k, lo:hi],
                                             w2s[:, r, half * MH + k, e],
                                             start=(half == 0 and n == 0), stop=(half == 1 and n == len(terms) - 1))
                            if n == len(terms) - 1 and (half == 1 or t == NTI - 1):
                                last.then_inc(o_ready if half == 1 else halves, 1)

                def turn(q, odd, first=False, last=False):
                    for bb in range(GB):
                        dispatch(q, bb)
                    up(q, 0, 0)
                    for u in range(2 * E):
                        if u + 1 < 2 * E:
                            up(q, (u + 1) // 2, (u + 1) % 2)
                        down(q, u // 2, u % 2)

                turn(0, 0, first=True)
                if NQ > 2:
                    with pe.Fori(0, NQ // 2 - 1) as pair:
                        turn(2 * pair + 1, 1)
                        turn(2 * pair + 2, 0)
                turn(NQ - 1, 1, last=True)


def program(nc, x, waT, wpT, wr, w1, b1T, w2, b2, c_mask, c_kbias, c_ident, c_maskT, c_tri, c_erank, c_erow, c_brow,
            c_iota, out):
    NB = x.shape[0]
    xhl_dram = nc.dram_tensor("xhl_scratch", [NB, P, NT, 2, C], F16, kind="Internal").ap()
    acc_dram = nc.dram_tensor("acc_scratch", [NB, P, NT, C], F32, kind="Internal").ap()
    qk_dram = nc.dram_tensor("qk_scratch", [NB, 2, 2, 2, P, T], F16, kind="Internal").ap()
    y_dram = [nc.dram_tensor(f"y_scratch{n}", [E * GS, C], F32, kind="Internal").ap() for n in range(2)]
    with ExitStack() as top:
        def lasting(name, shape, dt):
            return top.enter_context(nc.sbuf_tensor(name, shape, dt))

        spare = lasting("spare", [P, max(NT * C, NB * NT * E)], F32)
        logits = spare[:, 0:NB * NT * E].rearrange("p (b j e) -> p b j e", b=NB, j=NT)
        scales = lasting("scales", [P, BOUND + 1], F32)
        attention_phase(nc, top, x, waT, wpT, wr, c_mask, c_kbias, c_ident, c_maskT, xhl_dram, acc_dram, qk_dram,
                        logits, scales)
        pos_slot = lasting("pos_slot", [P, NB, NT, E], F16)
        weight = lasting("weight", [P, 2, NB, NT], F32)
        row_of = lasting("row_of", [P, 2, NB, NT], I32)
        w1s = lasting("w1s", [P, 2, NC, E, HF], F16)
        w2s = lasting("w2s", [P, 2, NM, E, C], F16)
        b1s = lasting("b1s", [P, E, NM], F32)
        b2b = lasting("b2b", [P, E, C], F32)
        routing_phase(nc, top, w1, b1T, w2, b2, c_tri, c_erank, c_erow, c_brow, logits, scales, pos_slot, weight,
                      row_of, w1s, w2s, b1s, b2b)
        expert_phase(nc, top, c_iota, xhl_dram, acc_dram, y_dram, out, scales, spare, pos_slot, weight, row_of,
                     w1s, w2s, b1s, b2b)


def constants(nb):
    import numpy as np

    start = 2.0 ** (-0.5)
    slopes = np.array([start * start ** i for i in range(NH)], dtype=np.float32).astype(np.float64)
    keys = np.arange(T)
    rest = slopes[:, None] * keys[None, :] * ALIBI_UP
    parts = []
    for _ in range(3):
        part = rest.astype(np.float16)
        parts.append(part)
        rest = rest - part.astype(np.float64)
    mask_q = np.zeros((P, T), np.float32)
    mask_q[:, T - P:] = np.where(np.arange(P)[None, :] > np.arange(P)[:, None], -BIG, 0.0)
    mask_k = np.where(np.arange(P)[:, None] > np.arange(P)[None, :], -BIG, 0.0)

    def bf16_bits(a):
        return (np.asarray(a, np.float32).view(np.uint32) >> 16).astype(np.uint16)

    return {
        "c_mask": mask_q,
        "c_kbias": np.stack(parts),
        "c_ident": np.eye(P, dtype=np.float16)[None],
        "c_maskT": bf16_bits(np.stack([mask_k, np.eye(P)])),
        "c_tri": bf16_bits(np.stack([np.triu(np.ones((P, P)), 1), np.ones((P, P))])),
        "c_erank": np.tile(np.arange(E, 0, -1, dtype=np.float32), (P, 1)),
        "c_erow": np.tile(np.arange(E, dtype=np.float32) * GS, (P, 1)),
        "c_brow": np.tile(np.array([b % GB * CAP for b in range(nb)], np.float32), (P, 1)),
        "c_iota": np.tile(np.arange(CAP, dtype=np.float16), (P, 1)),
    }


def kernel(L0_attn_x, L0_attn_w_attn, L0_attn_w_proj, L0_ffn_Wr, L0_ffn_W1, L0_ffn_b1, L0_ffn_W2, L0_ffn_b2):
    import numpy as np
    import concourse.bacc as bacc
    from concourse.bass_utils import run_bass_kernel_spmd

    x = np.ascontiguousarray(L0_attn_x)
    arrays = {
        "x": x,
        "waT": np.ascontiguousarray(np.asarray(L0_attn_w_attn).T),
        "wpT": np.ascontiguousarray(np.asarray(L0_attn_w_proj).T),
        "wr": np.ascontiguousarray(L0_ffn_Wr),
        "w1": np.ascontiguousarray(L0_ffn_W1),
        "b1T": np.ascontiguousarray(np.asarray(L0_ffn_b1).reshape(E, NM, P).transpose(2, 0, 1)),
        "w2": np.ascontiguousarray(L0_ffn_W2),
        "b2": np.ascontiguousarray(L0_ffn_b2),
        **constants(x.shape[0]),
    }
    nc = bacc.Bacc("TRN2", target_bir_lowering=False, num_devices=1)
    aps = {name: nc.dram_tensor(name, a.shape, mybir.dt.from_np(a.dtype), kind="ExternalInput").ap()
           for name, a in arrays.items()}
    out = nc.dram_tensor("out", x.shape, mybir.dt.from_np(x.dtype), kind="ExternalOutput").ap()
    program(nc, out=out, **aps)
    r = run_bass_kernel_spmd(nc, [arrays], core_ids=[0])
    return r.results[0]["out"]
```

```python
from contextlib import ExitStack

import concourse.bass as bass
from concourse import mybir

F32 = mybir.dt.float32
F16 = mybir.dt.float16
BF16 = mybir.dt.bfloat16
U32 = mybir.dt.uint32
U16 = mybir.dt.uint16
I32 = mybir.dt.int32
ALU = mybir.AluOpType
ACT = mybir.ActivationFunctionType
AX = mybir.AxisListType
RMAX = bass.bass_isa.ReduceOp.max

P = 128
T, C = 512, 256
NT = T // P
NC = C // P
NH, HD = 16, 16
E, HF = 8, 1024
CAP = int(T / E * 1.25)
NM = HF // P
GB = 4
GS = GB * CAP
H_BANKS = 2
SLOTS = E * CAP
EPS = 1e-5
X_SCALE = 1024.0
ALIBI_UP = 32.0
ROW_UP = 32768.0
HPG = 4
NG = NH // HPG
HALF = NH // 2
LEAD = 6
P_OFF = {0: 0, 1: 512, 3: 896, 2: 1024}
P_LEN = 1280
SCORE_UNITS = ((0,), (1, 3), (2,))
NU = len(SCORE_UNITS)
ROW_ALIBI, ROW_MAX = 64, 96
K_MAXIMA, K_SCORES = 96, 98
BIG = 2.0 ** 100

(M_A, M_P, M_R, V_A, V_P, V_R, A_POW, P_POW, R_POW, A_INV, SQ, QS, KS, S2, S_INV, QROW, Y_SC, ACC_DIV, ACC_SC,
 R_DIV, R_INV, M_1, M_2, M_B, V_1, V_2, V_B, W1_POW, W2_POW, H_POW, UP_DIV, UP_INV, UP_SC, DOWN_DIV, DOWN_SC,
 BOUND) = range(36)


def first_batch(b):
    return isinstance(b, int) and b == 0


def apart(eng):
    eng.nop(nofuse=True)


class Count:

    def __init__(self, before):
        self.before, self.n = before, 0

    def next(self):
        self.n += 1
        return self.before + self.n


def attention_phase(nc, top, x, waT, wpT, wr, c_mask, c_kbias, c_ident, c_ident32, c_maskT, xhl_dram, acc_dram,
                    qk_dram, logits, scales):
    NB = x.shape[0]
    x_v = x.rearrange("b (j p) c -> b p j c", p=P)
    with ExitStack() as ctx:
        def sb(name, shape, dt):
            return ctx.enter_context(nc.sbuf_tensor(name, shape, dt))

        def ps(name, shape, dt):
            return ctx.enter_context(nc.psum_tensor(name, shape, dt))

        def sem(name):
            return top.enter_context(nc.semaphore(name))

        def sc(n, lo=0, hi=P):
            return scales[lo:hi, n:n + 1]

        wa32 = sb("wa32", [P, NC, 3 * C], F32)
        wp32 = sb("wp32", [P, NC, C], F32)
        wr32 = sb("wr32", [P, NC, E], F32)
        wa = sb("wa", [P, 2, NC, 3 * C], F16)
        wp = sb("wp", [P, 2, NC, C], F16)
        wrs = sb("wrs", [P, NC, 2, E], F16)
        mask_q = sb("mask_q", [P, T], F32)
        ident = sb("ident", [P, P], F16)
        ident32 = sb("ident32", [P, P], F32)
        identb = sb("identb", [P, P], BF16)
        mask_k = sb("mask_k", [P, P], BF16)
        xin = sb("xin", [P, NT, C], F32)
        stats = sb("stats", [P, NT, 6], F32)
        mv = sb("mv", [P, NT, 2], F32)
        rstd = sb("rstd", [P, 4, NT], F32)
        xs = sb("xs", [P, NT, C], F32)
        xhl = sb("xhl", [P, NT, 2, C], F16)
        xT = sb("xT", [P, 2, NC, T], F16)
        qk_rows = sb("qk_rows", [P, 2, 2, 2, T], F16)
        q_st = sb("q_st", [P, NH, T], F16)
        k_st = sb("k_st", [P, NH, T], F16)
        v_ones = sb("v_ones", [P, NT, NH, 2 * HD], F32)
        maxima = sb("maxima", [P, 2, HPG * NT], F32)
        c_hl = sb("c_hl", [P, 2, 2, HPG * NT], F16)
        c_rows = sb("c_rows", [2 * HPG * NT, 2, P], F16)
        probs = sb("probs", [P, 2, HPG, P_LEN], F32)
        y_sums = sb("y_sums", [P, T], F32)
        y_rec = sb("y_rec", [P, NT, HPG], F32)
        y_nrm = sb("y_nrm", [P, NT, C], F32)
        y_hl = sb("y_hl", [P, 2, NT, C], F16)
        yT = sb("yT", [P, 2, NC, T], F16)
        x_res = sb("x_res", [P, NT, C], F32)
        acc = sb("acc", [P, NT, C], F32)

        ps_max = ps("ps_max", [P, 2, T], F32)
        ps_st = ps("ps_st", [P, 2, T], F32)
        ps_y = ps("ps_y", [P, T], F32)
        ps_c = ps("ps_c", [P, T], F32)
        ps_m = ps("ps_m", [P, 2, T], F32)

        s_w = sem("s_w")
        s_amax = sem("s_amax")
        s_all = sem("s_all")
        s_sc = sem("s_sc")
        s_whi = sem("s_whi")
        s_fill = sem("s_fill")
        s_kb = sem("s_kb")

        with nc.Block() as block:
            @block.sync
            def _(sp):
                for dst, src in ((wa32[:], waT.rearrange("(c p) n -> p c n", p=P)),
                                 (wp32[:], wpT.rearrange("(c p) n -> p c n", p=P)),
                                 (wr32[:], wr.rearrange("(c p) n -> p c n", p=P)),
                                 (mask_q[:], c_mask), (ident[:], c_ident), (ident32[:], c_ident32), (mask_k[:].bitcast(U16), c_maskT[0]),
                                 (identb[:].bitcast(U16), c_maskT[1])):
                    sp.dma_start(dst, src).then_inc(s_w, 16)
                sp.wait_ge(s_fill, 3)
                sp.dma_start(k_st[ROW_ALIBI:ROW_ALIBI + 3, :, :], c_kbias).then_inc(s_kb, 16)
                sp.wait_ge(s_kb, 16)
                sp.wait_ge(s_w, 8 * 16)

            @block.vector
            def _(dve):
                dve.wait_ge(s_w, 8 * 16)
                for n, w in ((M_A, wa32), (M_P, wp32), (M_R, wr32)):
                    dve.tensor_reduce(sc(n), w[:], AX.XY, ALU.max, apply_absolute_value=True).then_inc(s_amax, 1)
                dve.wait_ge(s_all, 1)
                own = Count(0)
                v3, p3 = scales[:, V_A:V_R + 1], scales[:, A_POW:R_POW + 1]
                dve.tensor_scalar(v3, v3, 1e-18, None, ALU.max).then_inc(s_sc, 1)
                dve.wait_ge(s_sc, own.next())
                dve.reciprocal(p3, v3).then_inc(s_sc, 1)
                dve.wait_ge(s_sc, own.next())
                dve.tensor_scalar(p3.bitcast(U32), p3.bitcast(U32), 0x7F800000, None,
                                  ALU.bitwise_and).then_inc(s_sc, 1)
                dve.wait_ge(s_sc, own.next())
                dve.tensor_scalar(sc(SQ), sc(A_POW), 2.0 ** 6, 1024.0, ALU.mult, ALU.min).then_inc(s_sc, 1)
                dve.wait_ge(s_sc, own.next())
                dve.tensor_scalar(sc(Y_SC), sc(A_POW), 2.0 ** 7, None, ALU.mult).then_inc(s_sc, 1)
                dve.wait_ge(s_sc, own.next())
                dve.tensor_scalar(p3, p3, 2.0 ** 15, None, ALU.mult).then_inc(s_sc, 1)
                dve.wait_ge(s_sc, own.next())
                dve.tensor_scalar(sc(ACC_DIV), sc(Y_SC), sc(P_POW), None, ALU.mult).then_inc(s_sc, 1)
                dve.wait_ge(s_sc, own.next())
                dve.tensor_scalar(sc(R_DIV), sc(R_POW), X_SCALE, None, ALU.mult).then_inc(s_sc, 1)
                dve.wait_ge(s_sc, own.next())
                dve.tensor_scalar(sc(A_INV), sc(A_POW), X_SCALE, None, ALU.mult).then_inc(s_sc, 1)
                dve.wait_ge(s_sc, own.next())
                dve.tensor_scalar(sc(S2), sc(SQ), sc(SQ), None, ALU.mult).then_inc(s_sc, 1)
                dve.wait_ge(s_sc, own.next())
                for dst, src in ((ACC_SC, ACC_DIV), (R_INV, R_DIV), (A_INV, A_INV), (S_INV, S2)):
                    dve.reciprocal(sc(dst), sc(src)).then_inc(s_sc, 1)
                    dve.wait_ge(s_sc, own.next())
                dve.tensor_scalar(sc(QROW), sc(S2), 1.0 / ALIBI_UP, None, ALU.mult).then_inc(s_sc, 1)
                dve.wait_ge(s_sc, own.next())
                dve.tensor_scalar(sc(KS), sc(SQ), sc(A_INV), None, ALU.mult).then_inc(s_sc, 1)
                dve.wait_ge(s_sc, own.next())
                dve.tensor_scalar(sc(QS), sc(KS), HD ** -0.5, None, ALU.mult).then_inc(s_sc, 1)
                dve.wait_ge(s_sc, own.next())
                dve.wait_ge(s_whi, 4)
                dve.scalar_tensor_tensor(wa[:, 1], wa32[:], sc(A_POW), wa[:, 0], ALU.mult,
                                         ALU.subtract).then_inc(s_sc, 1)
                dve.scalar_tensor_tensor(wp[:, 1], wp32[:], sc(P_POW), wp[:, 0], ALU.mult,
                                         ALU.subtract).then_inc(s_sc, 1)
                dve.scalar_tensor_tensor(wrs[:, :, 1, :], wr32[:], sc(R_POW), wrs[:, :, 0, :], ALU.mult,
                                         ALU.subtract).then_inc(s_sc, 1)
                dve.wait_ge(s_fill, 3)
                rows = slice(ROW_ALIBI, ROW_ALIBI + 3)
                dve.tensor_scalar(q_st[rows], q_st[rows], sc(QROW, ROW_ALIBI, ROW_ALIBI + 3), None,
                                  ALU.add).then_inc(s_sc, 1)

            @block.gpsimd
            def _(pool):
                pool.memset(q_st[:], 0.0).then_inc(s_fill, 1)
                pool.memset(k_st[:], 0.0).then_inc(s_fill, 1)
                pool.wait_ge(s_fill, 2)
                pool.memset(k_st[ROW_MAX:ROW_MAX + 2], ROW_UP).then_inc(s_fill, 1)
                pool.wait_ge(s_fill, 3)
                pool.memset(v_ones[:], 1.0).then_inc(s_fill, 1)
                pool.wait_ge(s_amax, 3)
                pool.partition_all_reduce(scales[:, V_A:V_R + 1], scales[:, M_A:M_R + 1], P, RMAX).then_inc(s_all, 1)

            @block.scalar
            def _(act):
                act.wait_ge(s_sc, 17)
                act.activation(wa[:, 0], wa32[:], ACT.Copy, scale=sc(A_POW)).then_inc(s_whi, 1)
                act.activation(wp[:, 0], wp32[:], ACT.Copy, scale=sc(P_POW)).then_inc(s_whi, 1)
                for c in range(NC):
                    act.activation(wrs[:, c, 0, :], wr32[:, c, :], ACT.Copy, scale=sc(R_POW)).then_inc(s_whi, 1)

        x_landed = sem("x_landed")
        xs_made = sem("xs_made")
        ln_own = sem("ln_own")
        guess_made = sem("guess_made")
        root_made = sem("root_made")
        xhl_split = sem("xhl_split")
        xhl_stored = sem("xhl_stored")
        t_ready = sem("t_ready")
        xt_hi = sem("xt_hi")
        xt_lo = sem("xt_lo")
        r_ready = sem("r_ready")
        r_kept = sem("r_kept")
        qk_ready = sem("qk_ready")
        qk_hi = sem("qk_hi")
        qk_lo = sem("qk_lo")
        v_ready = sem("v_ready")
        v_kept = sem("v_kept")
        qk_stored = [sem(f"qk_stored{h}") for h in range(2)]
        qk_stacked = [sem(f"qk_stacked{g}") for g in range(NG)]
        m_ready = sem("m_ready")
        m_done = sem("m_done")
        c_split = sem("c_split")
        c_turned = sem("c_turned")
        c_kept = sem("c_kept")
        c_in = [sem(f"c_in{g}") for g in range(NG)]
        st_ready = sem("st_ready")
        exp_done = sem("exp_done")
        pv_ready = sem("pv_ready")
        y_kept = sem("y_kept")
        y_turned = sem("y_turned")
        y_rec_made = sem("y_rec_made")
        y_normed = sem("y_normed")
        y_split = sem("y_split")
        yt_ready = sem("yt_ready")
        yt_hi = sem("yt_hi")
        yt_lo = sem("yt_lo")
        xr_landed = sem("xr_landed")
        p_ready = sem("p_ready")
        p_kept = sem("p_kept")
        acc_stored = sem("acc_stored")

        UNITS = NH * NT
        STU = NH * NU
        ROOT_STEPS = 16

        def run_turns(eng, turn):
            turn(0, first=True)
            with eng.Fori(1, NB - 2) as i:
                turn(i)
            turn(NB - 2, norm=False)
            turn(NB - 1, norm=False, front=False)

        def ahead(i, h, front):
            if h + LEAD < NH:
                return i, h + LEAD
            return (i + 1, h + LEAD - NH) if front else None

        with nc.Block() as block:
            @block.sync
            def _(sp):
                def load_x(b):
                    if not first_batch(b):
                        sp.wait_ge(xs_made, b)
                    sp.dma_start(xin[:], x_v[b]).then_inc(x_landed, 16)

                def store_xhl(b):
                    sp.wait_ge(xhl_split, 2 * b + 2)
                    sp.dma_start(xhl_dram[b], xhl[:]).then_inc(xhl_stored, 16)

                def store_q(b, h):
                    sp.wait_ge(qk_lo, 4 * b + 2 * h + 1)
                    sp.dma_start(qk_dram[b, h, 0, 0:2].rearrange("n p t -> p n t"), qk_rows[:, h, 0]
                                 ).then_inc(qk_stored[h], 16)
                    sp.dma_start(qk_dram[b, h, 0, 2], qk_rows[:, h, 0, 0]).then_inc(qk_stored[h], 16)

                def store_k(b, h):
                    sp.wait_ge(qk_lo, 4 * b + 2 * h + 2)
                    sp.dma_start(qk_dram[b, h, 1, 0], qk_rows[:, h, 1, 0]).then_inc(qk_stored[h], 16)
                    sp.dma_start(qk_dram[b, h, 1, 1:3].rearrange("n p t -> p n t"), qk_rows[:, h, 1]
                                 ).then_inc(qk_stored[h], 16)

                def stack_qk(b, g):
                    if not first_batch(b):
                        sp.wait_ge(st_ready, STU * (b - 1) + (g + 1) * HPG * NU)
                        apart(sp)
                    sp.wait_ge(qk_stored[g // 2], 64 * (b + 1))
                    heads = slice(g % 2 * HPG, (g % 2 + 1) * HPG)
                    for qk, stack in ((0, q_st), (1, k_st)):
                        rows = qk_dram[b, g // 2, qk].rearrange("n (d h) t -> (n d) h t", h=HALF)
                        sp.dma_start(stack[0:3 * HD, g * HPG:(g + 1) * HPG, :], rows[:, heads, :]
                                     ).then_inc(qk_stacked[g], 16)

                def rows_c(b, g):
                    sp.wait_ge(c_kept, 4 * b + g + 1)
                    for part in range(2):
                        n = HPG * NT
                        sp.dma_start(q_st[ROW_MAX + part:ROW_MAX + part + 1, g * HPG:(g + 1) * HPG, :]
                                     .rearrange("o h (t q) -> o (h t) q", q=P),
                                     c_rows[part * n:(part + 1) * n, g % 2, :]).then_inc(c_in[g], 16)

                def load_res(b):
                    if not first_batch(b):
                        sp.wait_ge(p_kept, 2 * b)
                    sp.dma_start(x_res[:], x_v[b]).then_inc(xr_landed, 16)

                def store_acc(b):
                    for n in range(2):
                        sp.wait_ge(p_kept, 2 * b + n + 1)
                        sp.dma_start(acc_dram[b, :, 2 * n:2 * n + 2], acc[:, 2 * n:2 * n + 2]).then_inc(acc_stored, 16)

                def turn(i, first=False, norm=True, front=True):
                    if not first:
                        stack_qk(i, 3)
                    if front:
                        store_xhl(i + 1)
                    if norm:
                        load_x(i + 2)
                    if not first:
                        load_res(i - 1)
                    rows_c(i, 1)
                    if front:
                        store_q(i + 1, 0)
                        store_k(i + 1, 0)
                        stack_qk(i + 1, 0)
                    rows_c(i, 2)
                    if front:
                        store_q(i + 1, 1)
                        store_k(i + 1, 1)
                        stack_qk(i + 1, 1)
                    rows_c(i, 3)
                    if not first:
                        store_acc(i - 1)
                    if front:
                        stack_qk(i + 1, 2)
                        rows_c(i + 1, 0)

                load_x(0)
                load_x(1)
                store_xhl(0)
                for h in range(2):
                    store_q(0, h)
                    store_k(0, h)
                    stack_qk(0, 2 * h)
                    stack_qk(0, 2 * h + 1)
                rows_c(0, 0)
                run_turns(sp, turn)
                load_res(NB - 1)
                store_acc(NB - 1)
                sp.wait_ge(xhl_stored, 16 * NB)
                sp.wait_ge(acc_stored, 32 * NB)

            @block.gpsimd
            def _(pool):
                def root(b):
                    v, r, a, d = rstd[:, 0, :], rstd[:, 2, :], rstd[:, 1, :], rstd[:, 3, :]
                    own = Count(ROOT_STEPS * b)
                    pool.wait_ge(guess_made, b + 1)
                    for step in range(4):
                        up = X_SCALE if step == 3 else 1.0
                        pool.tensor_tensor(a, r, r, ALU.mult).then_inc(root_made, 1)
                        pool.wait_ge(root_made, own.next())
                        pool.tensor_tensor(d, a, v, ALU.mult).then_inc(root_made, 1)
                        pool.wait_ge(root_made, own.next())
                        apart(pool)
                        pool.tensor_scalar(a, d, -0.5 * up, 1.5 * up, ALU.mult, ALU.add).then_inc(root_made, 1)
                        pool.wait_ge(root_made, own.next())
                        pool.tensor_tensor(r, a, r, ALU.mult).then_inc(root_made, 1)
                        pool.wait_ge(root_made, own.next())
                    assert own.n == ROOT_STEPS

                def split_x(b):
                    pool.wait_ge(xs_made, b + 1)
                    if not first_batch(b):
                        pool.wait_ge(t_ready, 2 * b)
                        pool.wait_ge(xhl_stored, 16 * b)
                    apart(pool)
                    pool.tensor_copy(xhl[:, :, 0, :], xs[:]).then_inc(xhl_split, 1)
                    pool.wait_ge(xhl_split, 2 * b + 1)
                    pool.tensor_tensor(xhl[:, :, 1, :], xs[:], xhl[:, :, 0, :], ALU.subtract).then_inc(xhl_split, 1)

                def split_y(b):
                    if not first_batch(b):
                        pool.wait_ge(yt_ready, 2 * b)
                    pool.wait_ge(y_normed, 4 * b + 4)
                    apart(pool)
                    pool.tensor_copy(y_hl[:, 0], y_nrm[:]).then_inc(y_split, 1)
                    pool.wait_ge(y_split, 2 * b + 1)
                    pool.tensor_tensor(y_hl[:, 1], y_nrm[:], y_hl[:, 0], ALU.subtract).then_inc(y_split, 1)

                def turn(i, first=False, norm=True, front=True):
                    if not first:
                        split_y(i - 1)
                    if norm:
                        root(i + 2)
                        split_x(i + 2)

                for b in range(2):
                    root(b)
                    split_x(b)
                run_turns(pool, turn)
                split_y(NB - 1)

            @block.vector
            def _(dve):
                LN_STEPS = 2 * NT + 2

                def statistics(b):
                    dve.wait_ge(x_landed, 16 * (b + 1))
                    for j in range(NT):
                        dve.bn_stats(stats[:, j, :], xin[:, j, :]).then_inc(ln_own, 1)

                def guess(b):
                    own = Count(LN_STEPS * b + NT)
                    dve.wait_ge(ln_own, own.before)
                    apart(dve)
                    for j in range(NT):
                        dve.bn_aggr(mv[:, j, :], stats[:, j, :]).then_inc(ln_own, 1)
                        made = own.next()
                    dve.wait_ge(ln_own, made)
                    var = mv[:, :, 1]
                    r0, r1 = rstd[:, 0, :], rstd[:, 1, :]
                    dve.tensor_scalar(r0, var, EPS, None, ALU.add).then_inc(ln_own, 1)
                    dve.wait_ge(ln_own, own.next())
                    bits = r1.bitcast(U32)
                    dve.tensor_scalar(bits, r0.bitcast(U32), 1, None, ALU.logical_shift_right).then_inc(ln_own, 1)
                    dve.wait_ge(ln_own, own.next())
                    dve.tensor_scalar(rstd[:, 2, :].bitcast(I32), r1.bitcast(I32), -1.0, float(0x5F3759DF), ALU.mult,
                                      ALU.add).then_inc(guess_made, 1)
                    assert own.n == LN_STEPS - NT

                def scale_x(b):
                    dve.wait_ge(root_made, ROOT_STEPS * (b + 1))
                    if not first_batch(b):
                        dve.wait_ge(xhl_split, 2 * b)
                    for j in range(NT):
                        last = dve.tensor_scalar(xs[:, j, :], xin[:, j, :], mv[:, j, 0:1], rstd[:, 2, j:j + 1],
                                                 ALU.subtract, ALU.mult)
                    last.then_inc(xs_made, 1)

                def keep_xt(b):
                    dve.wait_ge(t_ready, 2 * b + 2)
                    dve.tensor_copy(xT[:, 1], ps_m[:, 1, :].bitcast(F16).rearrange("p (c t) -> p c t", c=NC)
                                    ).then_inc(xt_lo, 1)

                def keep_logits(b):
                    dve.wait_ge(r_ready, b + 1)
                    dve.tensor_reduce(logits[:, b], ps_m[:, 0, 0:NT * 2 * E].rearrange("p (j l e) -> p j e l", j=NT, l=2),
                                      AX.X, ALU.add).then_inc(r_kept, 1)

                def low_qk(b, n):
                    h, qk = n // 2, n % 2
                    dve.wait_ge(qk_hi, 4 * b + n + 1)
                    dve.scalar_tensor_tensor(qk_rows[:, h, qk, 1, :], ps_m[:, 1 - qk, :], sc(KS if qk else QS),
                                             qk_rows[:, h, qk, 0, :], ALU.mult, ALU.subtract).then_inc(qk_lo, 1)

                def maximum(b, h, qt):
                    g, j = h // HPG, h % HPG
                    dve.wait_ge(m_ready, UNITS * b + h * NT + qt + 1)
                    apart(dve)
                    n = (qt + 1) * P
                    dve.tensor_tensor_reduce(out=ps_max[:, qt % 2, 0:n], in0=ps_max[:, qt % 2, 0:n],
                                             in1=mask_q[:, T - n:T], scale=1.0, scalar=-3e38, op0=ALU.add, op1=ALU.max,
                                             accum_out=maxima[:, g % 2, j * NT + qt:j * NT + qt + 1]
                                             ).then_inc(m_done, 1)

                def negate(b, g):
                    dve.wait_ge(m_done, UNITS * b + (g + 1) * HPG * NT)
                    if g >= 2 or not first_batch(b):
                        dve.wait_ge(c_turned, 4 * b + g - 1)
                    dve.tensor_scalar(c_hl[:, g % 2, 0], maxima[:, g % 2], -1.0 / ROW_UP, None, ALU.mult
                                      ).then_inc(c_split, 1)
                    dve.wait_ge(c_split, 2 * (4 * b + g) + 1)
                    dve.scalar_tensor_tensor(c_hl[:, g % 2, 1], maxima[:, g % 2], -1.0 / ROW_UP, c_hl[:, g % 2, 0],
                                             ALU.mult, ALU.subtract).then_inc(c_split, 1)

                def normalise(b, g):
                    if g == 0 and not first_batch(b):
                        dve.wait_ge(y_split, 2 * b)
                    dve.wait_ge(y_turned, 4 * b + g + 1)
                    rows = ps_y[:].rearrange("p (t j s d) -> p t j s d", t=NT, j=HPG, s=2)
                    dve.reciprocal(y_rec[:], rows[:, :, :, 1, 0]).then_inc(y_rec_made, 1)
                    dve.wait_ge(y_rec_made, 4 * b + g + 1)
                    dve.scalar_tensor_tensor(
                        y_nrm[:, :, g * HPG * HD:(g + 1) * HPG * HD].rearrange("p t (j d) -> p t j d", j=HPG),
                        rows[:, :, :, 0, :], sc(Y_SC),
                        y_rec[:].rearrange("p t (j o) -> p t j o", o=1).to_broadcast([P, NT, HPG, HD]),
                        ALU.mult, ALU.mult).then_inc(y_normed, 1)

                def keep_yt(b):
                    dve.wait_ge(yt_ready, 2 * b + 2)
                    dve.tensor_copy(yT[:, 1], ps_m[:, 1, :].bitcast(F16).rearrange("p (c t) -> p c t", c=NC)
                                    ).then_inc(yt_lo, 1)

                def add_input(b, n):
                    if n == 0:
                        dve.wait_ge(xr_landed, 16 * (b + 1))
                        if not first_batch(b):
                            dve.wait_ge(acc_stored, 32 * b)
                    dve.wait_ge(p_ready, 2 * b + n + 1)
                    dve.scalar_tensor_tensor(acc[:, 2 * n:2 * n + 2], ps_m[:, 1 - n, :].rearrange("p (j c) -> p j c", c=C),
                                             sc(ACC_SC), x_res[:, 2 * n:2 * n + 2], ALU.mult, ALU.add
                                             ).then_inc(p_kept, 1)

                def between(i, h, first, norm, front):
                    if not first:
                        if h == 2:
                            normalise(i - 1, 3)
                        if h == 8:
                            keep_yt(i - 1)
                        if h in (10, 11):
                            add_input(i - 1, h - 10)
                    if front:
                        if h == 3:
                            keep_xt(i + 1)
                        if h == 4:
                            keep_logits(i + 1)
                        if h in (4, 5, 6, 7):
                            low_qk(i + 1, h - 4)
                    if h in (6, 10, 14):
                        normalise(i, (h - 6) // 4)
                    if norm:
                        if h == 9:
                            statistics(i + 2)
                        if h == 11:
                            guess(i + 2)
                        if h == 13:
                            scale_x(i + 2)

                def turn(i, first=False, norm=True, front=True):
                    for h in range(NH):
                        head = ahead(i, h, front)
                        for qt in range(NT):
                            if qt == 2:
                                between(i, h, first, norm, front)
                            if head:
                                maximum(*head, qt)
                        if head and head[1] % HPG == HPG - 1:
                            negate(head[0], head[1] // HPG)

                statistics(0)
                guess(0)
                scale_x(0)
                statistics(1)
                guess(1)
                keep_xt(0)
                scale_x(1)
                keep_logits(0)
                for n in range(4):
                    low_qk(0, n)
                for h in range(LEAD):
                    for qt in range(NT):
                        maximum(0, h, qt)
                    if h == HPG - 1:
                        negate(0, 0)
                run_turns(dve, turn)
                normalise(NB - 1, 3)
                keep_yt(NB - 1)
                add_input(NB - 1, 0)
                add_input(NB - 1, 1)

            @block.scalar
            def _(act):
                def keep_xt(b):
                    act.wait_ge(t_ready, 2 * b + 1)
                    act.activation(xT[:, 0], ps_m[:, 0, :].bitcast(F16).rearrange("p (c t) -> p c t", c=NC), ACT.Copy
                                   ).then_inc(xt_hi, 1)

                def keep_yt(b):
                    act.wait_ge(yt_ready, 2 * b + 1)
                    act.activation(yT[:, 0], ps_m[:, 0, :].bitcast(F16).rearrange("p (c t) -> p c t", c=NC), ACT.Copy
                                   ).then_inc(yt_hi, 1)

                def high_qk(b, n):
                    h, qk = n // 2, n % 2
                    act.wait_ge(qk_ready, 4 * b + n + 1)
                    if not first_batch(b):
                        act.wait_ge(qk_stored[h], 64 * b)
                    act.activation(qk_rows[:, h, qk, 0, :], ps_m[:, 1 - qk, :], ACT.Copy, scale=sc(KS if qk else QS)
                                   ).then_inc(qk_hi, 1)

                def keep_v(b, n):
                    act.wait_ge(v_ready, 2 * b + n + 1)
                    if not first_batch(b):
                        act.wait_ge(pv_ready, 4 * b)
                    act.activation(v_ones[:, 2 * n:2 * n + 2, :, 0:HD].rearrange("p j h d -> p (j h) d"),
                                   ps_m[:, 1 - n, :].rearrange("p (jh d) -> p jh d", d=HD), ACT.Copy, scale=sc(A_INV)
                                   ).then_inc(v_kept, 1)

                def keep_c(b, g):
                    act.wait_ge(c_turned, 4 * b + g + 1)
                    if g >= 2:
                        act.wait_ge(c_in[g - 2], 32 * (b + 1))
                    elif not first_batch(b):
                        act.wait_ge(c_in[g + 2], 32 * b)
                    act.activation(c_rows[:, g % 2, :], ps_c[0:2 * HPG * NT, 0:P // 2].bitcast(F16), ACT.Copy
                                   ).then_inc(c_kept, 1)

                def exps(b, h):
                    g, j = h // HPG, h % HPG
                    if j == 0 and (g >= 2 or not first_batch(b)):
                        act.wait_ge(pv_ready, 4 * b + g - 1)
                    for u in range(NU):
                        n = h * NU + u
                        act.wait_ge(st_ready, STU * b + n + 1)
                        size = min(T, P_LEN - u * T)
                        act.activation(probs[:, g % 2, j, u * T:u * T + size], ps_st[:, n % 2, 0:size], ACT.Exp,
                                       scale=sc(S_INV)).then_inc(exp_done, 1)

                def keep_y(b, g):
                    act.wait_ge(pv_ready, 4 * b + g + 1)
                    if g or not first_batch(b):
                        act.wait_ge(y_turned, 4 * b + g)
                    act.activation(y_sums[:], ps_y[:], ACT.Copy).then_inc(y_kept, 1)

                def turn(i, first=False, norm=True, front=True):
                    for h in range(NH):
                        head = ahead(i, h - 1, front)
                        if head and head[1] % HPG == HPG - 1:
                            keep_c(head[0], head[1] // HPG)
                        exps(i, h)
                        if h == 0 and not first:
                            keep_y(i - 1, 3)
                        if h in (0, 1):
                            keep_v(i, h)
                        if front:
                            if h == 2:
                                keep_xt(i + 1)
                            if h in (3, 4, 5, 6):
                                if h == 4:
                                    keep_y(i, 0)
                                high_qk(i + 1, h - 3)
                        elif h == 4:
                            keep_y(i, 0)
                        if h == 7 and not first:
                            keep_yt(i - 1)
                        if h in (8, 12):
                            keep_y(i, h // 4 - 1)

                act.wait_ge(s_fill, 4)
                keep_xt(0)
                for n in range(4):
                    high_qk(0, n)
                keep_c(0, 0)
                run_turns(act, turn)
                keep_y(NB - 1, 3)
                keep_yt(NB - 1)

            @block.tensor
            def _(pe):
                def products(out, left, right):
                    terms = [(l, r, c) for c in range(NC) for l, r in ((0, 0), (1, 0), (0, 1))]
                    for n, (l, r, c) in enumerate(terms):
                        last = pe.matmul(out, left(l, c), right(r, c), start=(n == 0), stop=(n == len(terms) - 1),
                                         skip_group_check=True)
                    return last

                def transpose_rows(rows, part):
                    bank = ps_m[:, part, :].bitcast(F16).rearrange("p (c t) -> p c t", c=NC)
                    for c in range(NC):
                        for j in range(NT):
                            last = pe.transpose(bank[:, c, j * P:(j + 1) * P], rows[:, j, c * P:(c + 1) * P], ident[:])
                    return last

                def transpose_x(b):
                    if not first_batch(b):
                        pe.wait_ge(v_kept, 2 * b)
                    for part in range(2):
                        pe.wait_ge(xhl_split, 2 * b + part + 1)
                        transpose_rows(xhl[:, :, part], part).then_inc(t_ready, 1)

                def router(b):
                    pe.wait_ge(xt_hi, b + 1)
                    pe.wait_ge(xt_lo, b + 1)
                    for j in range(NT):
                        for n in range(2 * NC):
                            part, c = n // NC, n % NC
                            last = pe.matmul(ps_m[:, 0, j * 2 * E:(j + 1) * 2 * E], xT[:, part, c, j * P:(j + 1) * P],
                                             wrs[:, c].rearrange("p l e -> p (l e)"), start=(n == 0),
                                             stop=(n == 2 * NC - 1), skip_group_check=True)
                    last.then_inc(r_ready, 1)

                def qk(b, n):
                    h, is_k = n // 2, n % 2
                    if n >= 2:
                        pe.wait_ge(qk_lo, 4 * b + n - 1)
                    elif n == 1:
                        pe.wait_ge(r_kept, b + 1)
                    at = is_k * C + h * P
                    products(ps_m[:, 1 - is_k, :], lambda l, c: wa[:, l, c, at:at + P], lambda r, c: xT[:, r, c, :]
                             ).then_inc(qk_ready, 1)

                def values(b, n):
                    for j in (2 * n, 2 * n + 1):
                        last = products(ps_m[:, 1 - n, (j % 2) * C:(j % 2 + 1) * C],
                                        lambda l, c: xT[:, l, c, j * P:(j + 1) * P],
                                        lambda r, c: wa[:, r, c, 2 * C:3 * C])
                    last.then_inc(v_ready, 1)

                def transpose_y(b, banks_free):
                    pe.wait_ge(*banks_free)
                    for part in range(2):
                        pe.wait_ge(y_split, 2 * b + part + 1)
                        transpose_rows(y_hl[:, part], part).then_inc(yt_ready, 1)

                def project(b, n):
                    pe.wait_ge(yt_hi, b + 1)
                    pe.wait_ge(yt_lo, b + 1)
                    for j in (2 * n, 2 * n + 1):
                        last = products(ps_m[:, 1 - n, (j % 2) * C:(j % 2 + 1) * C],
                                        lambda l, c: yT[:, l, c, j * P:(j + 1) * P], lambda r, c: wp[:, r, c, :])
                    last.then_inc(p_ready, 1)

                def score_maxima(b, h):
                    if h % HPG == 0:
                        pe.wait_ge(qk_stacked[h // HPG], 32 * (b + 1))
                    for qt in range(NT):
                        u = h * NT + qt
                        if u >= 2 or not first_batch(b):
                            pe.wait_ge(m_done, UNITS * b + u - 1)
                        n = (qt + 1) * P
                        pe.matmul(ps_max[:, qt % 2, 0:n], q_st[0:K_MAXIMA, h, qt * P:n], k_st[0:K_MAXIMA, h, 0:n],
                                  start=True, stop=True).then_inc(m_ready, 1)

                def turn_c(b, g):
                    pe.wait_ge(c_split, 2 * (4 * b + g) + 2)
                    if g >= 1 or not first_batch(b):
                        pe.wait_ge(c_kept, 4 * b + g)
                    pe.transpose(ps_c[0:2 * HPG * NT, 0:P // 2].bitcast(F16),
                                 c_hl[:, g % 2].rearrange("p l n -> p (l n)"), ident[:]).then_inc(c_turned, 1)

                def scores(b, h):
                    if h % HPG == 0:
                        pe.wait_ge(c_in[h // HPG], 32 * (b + 1))
                    for u, tiles in enumerate(SCORE_UNITS):
                        n = h * NU + u
                        if n >= 2 or not first_batch(b):
                            pe.wait_ge(exp_done, STU * b + n - 1)
                        for kt in tiles:
                            at, size = P_OFF[kt] - u * T, T - kt * P
                            pe.matmul(ps_st[:, n % 2, at:at + size], k_st[0:K_SCORES, h, kt * P:(kt + 1) * P],
                                      q_st[0:K_SCORES, h, kt * P:T], start=True, stop=False, skip_group_check=True)
                            last = pe.matmul(ps_st[:, n % 2, at:at + P], identb[:], mask_k[:], start=False, stop=True,
                                             skip_group_check=True)
                        last.then_inc(st_ready, 1)

                def weighted_sums(b, g):
                    pe.wait_ge(exp_done, STU * b + (g + 1) * HPG * NU)
                    if g == 0:
                        pe.wait_ge(v_kept, 2 * (b + 1))
                    if g >= 1 or not first_batch(b):
                        pe.wait_ge(y_normed, 4 * b + g)
                    for kt in range(NT):
                        for j in range(HPG):
                            last = pe.matmul(ps_y[32 * j:32 * j + 32, kt * P:T], v_ones[:, kt, g * HPG + j, :],
                                             probs[:, g % 2, j, P_OFF[kt]:P_OFF[kt] + T - kt * P],
                                             start=(kt == 0), stop=(kt == NT - 1), skip_group_check=True)
                    last.then_inc(pv_ready, 1)

                def turn_y(b, g):
                    pe.wait_ge(y_kept, 4 * b + g + 1)
                    for j in range(NT):
                        last = pe.transpose(ps_y[:, j * P:(j + 1) * P], y_sums[:, j * P:(j + 1) * P], ident32[:])
                    last.then_inc(y_turned, 1)

                def turn(i, first=False, norm=True, front=True):
                    for h in range(NH):
                        head = ahead(i, h, front)
                        if head:
                            score_maxima(*head)
                        head = ahead(i, h - 1, front)
                        if head and head[1] % HPG == HPG - 1:
                            turn_c(head[0], head[1] // HPG)
                        scores(i, h)
                        if h == 0 and not first:
                            weighted_sums(i - 1, 3)
                        if h == 1 and not first:
                            turn_y(i - 1, 3)
                        if h in (0, 1):
                            values(i, h)
                        if h in (4, 8, 12):
                            weighted_sums(i, h // 4 - 1)
                        if h in (5, 9, 13):
                            turn_y(i, h // 4 - 1)
                        if front:
                            if h == 2:
                                transpose_x(i + 1)
                            if h == 3:
                                router(i + 1)
                            if h in (3, 4, 5, 6):
                                qk(i + 1, h - 3)
                        if not first:
                            if h == 7:
                                transpose_y(i - 1, (qk_lo, 4 * (i + 1) + 4) if front else (v_kept, 2 * (i + 1)))
                            if h in (9, 10):
                                project(i - 1, h - 9)
                    if first:
                        pe.wait_ge(qk_lo, 8)
                    else:
                        pe.wait_ge(p_kept, 2 * i)

                transpose_x(0)
                router(0)
                for n in range(4):
                    qk(0, n)
                for h in range(HPG):
                    score_maxima(0, h)
                score_maxima(0, HPG)
                turn_c(0, 0)
                score_maxima(0, HPG + 1)
                pe.wait_ge(qk_lo, 4)
                run_turns(pe, turn)
                weighted_sums(NB - 1, 3)
                turn_y(NB - 1, 3)
                transpose_y(NB - 1, (p_kept, 2 * NB - 2))
                project(NB - 1, 0)
                project(NB - 1, 1)


def routing_phase(nc, top, w1, b1T, w2, b2, c_tri, c_erank, c_erow, c_brow, logits, scales, pos_slot, weight, row_of,
                  w1s, w2s, b1s, b2b):
    NB = logits.shape[1]
    N = NB * NT
    with ExitStack() as ctx:
        def sb(name, shape, dt):
            return ctx.enter_context(nc.sbuf_tensor(name, shape, dt))

        def sem(name):
            return top.enter_context(nc.semaphore(name))

        def sc(n):
            return scales[:, n:n + 1]

        stage = w2s[:].rearrange("p l k e n -> p (l k e n)").bitcast(F32).rearrange("p (e n) -> p e n", e=E)
        RING = 4
        ring = sb("ring", [P, RING, NC * HF], F32)
        amax = sb("amax", [P, 2, E], F32)
        tri = sb("tri", [P, 2, P], BF16)
        erank = sb("erank", [P, E], F32)
        erow = sb("erow", [P, E], F32)
        brow = sb("brow", [P, NB], F32)
        one = sb("one", [P, 4, N], F32)
        pk = sb("pk", [P, 2, N], F32)
        t0 = sb("t0", [P, N, E], F32)
        t1 = sb("t1", [P, N, E], F32)
        oh = sb("oh", [P, 2, N, E], F32)
        taken = sb("taken", [P, NB, NT, E], BF16)
        before = sb("before", [P, NB, NT, E], BF16)
        ps_pos = ctx.enter_context(nc.psum_tensor("ps_pos", [P, N * E], F32))

        s_c = sem("r_const")
        s_w1 = [sem(f"w1_landed{e}") for e in range(E)]
        s_w2 = [sem(f"w2_landed{n}") for n in range(RING)]
        s_amax = sem("w_amax")
        s_seen = sem("w2_seen")
        s_top = sem("w_amax_all")
        s_own = sem("r_own")
        s_exp = sem("r_exp")
        s_pos = sem("r_pos")
        s_route = sem("r_route")
        s_pow = sem("w_pow")
        s_hi = sem("w_hi")
        s_lo = sem("w_lo")
        s_b1 = sem("b1_scaled")

        with nc.Block() as block:
            @block.sync
            def _(sp):
                for dst, src in ((tri[:].bitcast(U16), c_tri.rearrange("n p q -> p n q")), (erank[:], c_erank), (erow[:], c_erow),
                                 (brow[:], c_brow), (b1s[:], b1T),
                                 (b2b[:], b2.rearrange("e c -> (e c)").partition_broadcast(P))):
                    sp.dma_start(dst, src).then_inc(s_c, 16)
                for e in range(E):
                    sp.dma_start(stage[:, e].rearrange("p (c h) -> p c h", c=NC),
                                 w1[e].rearrange("(c p) h -> p c h", p=P)).then_inc(s_w1[e], 16)
                for n in range(2 * E):
                    if n >= RING:
                        if n - RING < E:
                            sp.wait_ge(s_seen, n - RING + 1)
                        else:
                            sp.wait_ge(s_lo, n - RING + 1)
                    sp.dma_start(ring[:, n % RING].rearrange("p (k n) -> p k n", k=NM),
                                 w2[n % E].rearrange("(k p) n -> p k n", p=P)).then_inc(s_w2[n % RING], 16)
                for n in range(RING):
                    sp.wait_ge(s_w2[n], 16 * 2 * E // RING)

            @block.gpsimd
            def _(pool):
                pool.wait_ge(s_amax, 1)
                pool.partition_all_reduce(scales[:, V_1:V_1 + 1], scales[:, M_1:M_1 + 1], P, RMAX).then_inc(s_top, 1)
                pool.wait_ge(s_top, 1)
                pool.partition_all_reduce(scales[:, V_B:V_B + 1], scales[:, M_B:M_B + 1], P, RMAX).then_inc(s_top, 1)
                pool.wait_ge(s_amax, 2)
                pool.wait_ge(s_top, 2)
                pool.partition_all_reduce(scales[:, V_2:V_2 + 1], scales[:, M_2:M_2 + 1], P, RMAX).then_inc(s_top, 1)

            @block.scalar
            def _(act):
                act.wait_ge(s_route, 1)
                act.activation(t1[:], t0[:], ACT.Exp, scale=sc(R_INV)).then_inc(s_exp, 1)
                act.wait_ge(s_pow, 1)
                for e in range(E):
                    act.activation(w1s[:, 0, :, e, :], stage[:, e].rearrange("p (c h) -> p c h", c=NC), ACT.Copy,
                                   scale=sc(W1_POW)).then_inc(s_hi, 1)
                act.wait_ge(s_c, 6 * 16)
                act.activation(b1s[:], b1s[:], ACT.Copy, scale=sc(H_POW)).then_inc(s_b1, 1)
                act.wait_ge(s_pow, 2)
                for e in range(E):
                    act.wait_ge(s_w2[e % RING], 16 * ((E + e) // RING + 1))
                    if e == 0:
                        act.wait_ge(s_lo, E)
                    act.activation(w2s[:, 0, :, e, :], ring[:, e % RING].rearrange("p (k n) -> p k n", k=NM), ACT.Copy,
                                   scale=sc(W2_POW)).then_inc(s_hi, 1)

            @block.tensor
            def _(pe):
                pe.wait_ge(s_c, 6 * 16)
                pe.wait_ge(s_route, 2)
                flat_taken = taken[:].rearrange("p b j e -> p (b j e)")
                flat_before = before[:].rearrange("p b j e -> p (b j e)")
                for at in range(0, N * E, 512):
                    to = min(at + 512, N * E)
                    pe.matmul(ps_pos[:, at:to], tri[:, 0], flat_taken[:, at:to], start=True, stop=False)
                    last = pe.matmul(ps_pos[:, at:to], tri[:, 1], flat_before[:, at:to], start=False, stop=True)
                last.then_inc(s_pos, 1)

            @block.vector
            def _(dve):
                own = Count(0)

                def bc(v):
                    return v.rearrange("p (n o) -> p n o", o=1).to_broadcast([P, N, E])

                def row(v):
                    return v.rearrange("p (o e) -> p o e", o=1).to_broadcast([P, N, E])

                lg = logits.rearrange("p b j e -> p (b j) e")
                dve.tensor_reduce(one[:, 0], lg, AX.X, ALU.max).then_inc(s_own, 1)
                dve.wait_ge(s_own, own.next())
                dve.tensor_tensor(t0[:], lg, bc(one[:, 0]), ALU.subtract).then_inc(s_route, 1)
                for e in range(E):
                    dve.wait_ge(s_w1[e], 16)
                    dve.tensor_reduce(amax[:, 0, e:e + 1], stage[:, e], AX.X, ALU.max, apply_absolute_value=True
                                      ).then_inc(s_own, 1)
                    done = own.next()
                dve.wait_ge(s_c, 6 * 16)
                dve.tensor_reduce(sc(M_B), b1s[:], AX.XY, ALU.max, apply_absolute_value=True).then_inc(s_own, 1)
                dve.wait_ge(s_own, own.next())
                dve.tensor_reduce(sc(M_1), amax[:, 0], AX.X, ALU.max).then_inc(s_amax, 1)
                dve.wait_ge(s_exp, 1)
                dve.tensor_reduce(one[:, 1], t1[:], AX.X, ALU.add).then_inc(s_own, 1)
                dve.wait_ge(s_own, own.next())
                dve.reciprocal(one[:, 3], one[:, 1]).then_inc(s_own, 1)
                dve.wait_ge(s_own, own.next())
                dve.tensor_tensor(t0[:], t1[:], bc(one[:, 3]), ALU.mult).then_inc(s_own, 1)
                dve.wait_ge(s_own, own.next())
                for k in range(2):
                    dve.tensor_reduce(pk[:, k], t0[:], AX.X, ALU.max).then_inc(s_own, 1)
                    dve.wait_ge(s_own, own.next())
                    dve.tensor_tensor(t1[:], t0[:], bc(pk[:, k]), ALU.is_equal).then_inc(s_own, 1)
                    dve.wait_ge(s_own, own.next())
                    dve.tensor_tensor(t1[:], t1[:], row(erank[:]), ALU.mult).then_inc(s_own, 1)
                    dve.wait_ge(s_own, own.next())
                    dve.tensor_reduce(one[:, 2], t1[:], AX.X, ALU.max).then_inc(s_own, 1)
                    dve.wait_ge(s_own, own.next())
                    dve.tensor_tensor(oh[:, k], t1[:], bc(one[:, 2]), ALU.is_equal).then_inc(s_own, 1)
                    dve.wait_ge(s_own, own.next())
                    if k == 0:
                        dve.scalar_tensor_tensor(t0[:], oh[:, 0], -2.0, t0[:], ALU.mult, ALU.add).then_inc(s_own, 1)
                        dve.wait_ge(s_own, own.next())
                dve.tensor_tensor(taken[:].rearrange("p b j e -> p (b j) e"), oh[:, 0], oh[:, 1], ALU.add
                                  ).then_inc(s_own, 1)
                dve.memset(before[:, :, 0, :], 0.0).then_inc(s_own, 1)
                own.next()
                dve.wait_ge(s_own, own.next())
                for j in range(1, NT):
                    last = dve.tensor_tensor(before[:, :, j, :], before[:, :, j - 1, :], taken[:, :, j - 1, :], ALU.add)
                    last.then_inc(s_own, 1)
                    dve.wait_ge(s_own, own.next())
                dve.wait_ge(s_route, 1)
                dve.memset(one[:, 3], 0.0).then_inc(s_route, 1)

                def power(dst, src, up):
                    dve.reciprocal(sc(dst), sc(src)).then_inc(s_own, 1)
                    dve.wait_ge(s_own, own.next())
                    dve.tensor_scalar(sc(dst).bitcast(U32), sc(dst).bitcast(U32), 0x7F800000, None, ALU.bitwise_and
                                      ).then_inc(s_own, 1)
                    dve.wait_ge(s_own, own.next())
                    return dve.tensor_scalar(sc(dst), sc(dst), up, None, ALU.mult)

                dve.wait_ge(s_top, 2)
                dve.tensor_scalar(sc(V_1), sc(V_1), 1e-18, None, ALU.max).then_inc(s_own, 1)
                dve.wait_ge(s_own, own.next())
                power(W1_POW, V_1, 2.0 ** 15).then_inc(s_own, 1)
                dve.wait_ge(s_own, own.next())
                dve.scalar_tensor_tensor(sc(BOUND), sc(V_1), float(C), sc(V_B), ALU.mult, ALU.add).then_inc(s_own, 1)
                dve.wait_ge(s_own, own.next())
                power(H_POW, BOUND, 2.0 ** 15).then_inc(s_pow, 1)
                dve.wait_ge(s_pow, 1)
                for e in range(E):
                    dve.wait_ge(s_hi, e + 1)
                    dve.scalar_tensor_tensor(w1s[:, 1, :, e, :], stage[:, e].rearrange("p (c h) -> p c h", c=NC),
                                             sc(W1_POW), w1s[:, 0, :, e, :], ALU.mult, ALU.subtract).then_inc(s_lo, 1)
                dve.wait_ge(s_pos, 1)
                dve.tensor_copy(t0[:], ps_pos[:].rearrange("p (n e) -> p n e", e=E)).then_inc(s_own, 1)
                dve.wait_ge(s_own, own.next())
                dve.tensor_scalar(t1[:], t0[:], CAP - 0.5, None, ALU.is_lt).then_inc(s_own, 1)
                dve.wait_ge(s_own, own.next())
                dve.tensor_tensor(t1[:], t1[:], taken[:].rearrange("p b j e -> p (b j) e"), ALU.mult).then_inc(s_own, 1)
                dve.wait_ge(s_own, own.next())
                ps = pos_slot[:].rearrange("p b j e -> p (b j) e")
                lgf = logits.rearrange("p b j e -> p (b j) e")
                dve.scalar_tensor_tensor(lgf, t0[:], 1.0, t1[:], ALU.add, ALU.mult).then_inc(s_own, 1)
                dve.wait_ge(s_own, own.next())
                dve.tensor_scalar(ps, lgf, -1.0, None, ALU.add).then_inc(s_own, 1)
                own.next()
                dve.tensor_scalar(t0[:], t0[:], float(CAP - 1), None, ALU.min).then_inc(s_own, 1)
                dve.wait_ge(s_own, own.next())
                dve.tensor_tensor(t0[:], t0[:], row(erow[:]), ALU.add).then_inc(s_own, 1)
                dve.wait_ge(s_own, own.next())
                for k in range(2):
                    dve.tensor_tensor(lgf, t0[:], oh[:, k], ALU.mult).then_inc(s_own, 1)
                    dve.wait_ge(s_own, own.next())
                    dve.tensor_reduce(one[:, 0], lgf, AX.X, ALU.add).then_inc(s_own, 1)
                    dve.wait_ge(s_own, own.next())
                    dve.tensor_tensor(row_of[:, k], one[:, 0].rearrange("p (b j) -> p b j", j=NT),
                                      brow[:].rearrange("p (b o) -> p b o", o=1).to_broadcast([P, NB, NT]), ALU.add
                                      ).then_inc(s_own, 1)
                    dve.wait_ge(s_own, own.next())
                    dve.tensor_tensor(lgf, t1[:], oh[:, k], ALU.mult).then_inc(s_own, 1)
                    dve.wait_ge(s_own, own.next())
                    dve.tensor_reduce(one[:, 1], lgf, AX.X, ALU.add).then_inc(s_own, 1)
                    dve.wait_ge(s_own, own.next())
                    dve.tensor_tensor(weight[:, k], pk[:, k].rearrange("p (b j) -> p b j", j=NT),
                                      one[:, 1].rearrange("p (b j) -> p b j", j=NT), ALU.mult).then_inc(s_own, 1)
                    dve.wait_ge(s_own, own.next())
                for e in range(E):
                    dve.wait_ge(s_w2[e % RING], 16 * (e // RING + 1))
                    dve.tensor_reduce(amax[:, 1, e:e + 1], ring[:, e % RING], AX.X, ALU.max, apply_absolute_value=True
                                      ).then_inc(s_seen, 1)
                dve.wait_ge(s_seen, E)
                dve.tensor_reduce(sc(M_2), amax[:, 1], AX.X, ALU.max).then_inc(s_amax, 1)
                dve.wait_ge(s_top, 3)
                dve.tensor_scalar(sc(V_2), sc(V_2), 1e-18, None, ALU.max).then_inc(s_own, 1)
                dve.wait_ge(s_own, own.next())
                power(W2_POW, V_2, 2.0 ** 15).then_inc(s_pow, 1)
                dve.wait_ge(s_pow, 2)
                dve.tensor_scalar(sc(UP_DIV), sc(W1_POW), X_SCALE, None, ALU.mult).then_inc(s_own, 1)
                dve.wait_ge(s_own, own.next())
                dve.reciprocal(sc(UP_INV), sc(UP_DIV)).then_inc(s_own, 1)
                dve.wait_ge(s_own, own.next())
                dve.tensor_tensor(sc(UP_SC), sc(UP_INV), sc(H_POW), ALU.mult).then_inc(s_own, 1)
                own.next()
                dve.tensor_tensor(sc(DOWN_DIV), sc(H_POW), sc(W2_POW), ALU.mult).then_inc(s_own, 1)
                dve.wait_ge(s_own, own.next())
                dve.reciprocal(sc(DOWN_SC), sc(DOWN_DIV)).then_inc(s_own, 1)
                for e in range(E):
                    dve.wait_ge(s_hi, E + e + 1)
                    dve.scalar_tensor_tensor(w2s[:, 1, :, e, :], ring[:, e % RING].rearrange("p (k n) -> p k n", k=NM),
                                             sc(W2_POW), w2s[:, 0, :, e, :], ALU.mult, ALU.subtract).then_inc(s_lo, 1)


def expert_phase(nc, top, c_iota, xhl_dram, acc_dram, y_dram, out, scales, spare, pos_slot, weight,
                 row_of, w1s, w2s, b1s, b2b):
    NB = pos_slot.shape[1]
    NQ = NB // GB
    assert NQ % 2 == 0
    out_v = out.rearrange("b (j p) c -> b p j c", p=P)
    TILES = ((0, P), (P, 2 * P), (2 * P, GS))
    NTI = len(TILES)
    MH = NM // 2
    with ExitStack() as ctx:
        def sb(name, shape, dt):
            return ctx.enter_context(nc.sbuf_tensor(name, shape, dt))

        def ps(name, shape, dt):
            return ctx.enter_context(nc.psum_tensor(name, shape, dt))

        def sem(name):
            return top.enter_context(nc.semaphore(name))

        def sc(n):
            return scales[:, n:n + 1]

        iota = sb("iota", [P, CAP], F16)
        xg = sb("xg", [P, 2, NT, 2, C], F16)
        place = sb("place", [P, 2, NT, E, CAP], F16)
        xb = sb("xb", [P, 2, NC, E, GB, CAP], F16)
        relu = sb("relu", [P, MH, GS], F32)
        hs = sb("hs", [P, 2, 2, MH, GS], F16)
        yo = sb("yo", [P, NTI, C], F32)
        rows_q = sb("rows_q", [P, 2, GB, NT], I32)
        yg = sb("yg", [P, NT, C], F32)
        acc = spare[:, 0:NT * C].rearrange("p (j c) -> p j c", c=C)
        ps_x = ps("ps_x", [P, 2, 512], F32)
        ps_h = ps("ps_h", [P, H_BANKS, 512], F32)
        ps_o = ps("ps_o", [P, 3, 512], F32)

        b_const = sem("b_const")
        xg_landed = [sem(f"xg_landed{n}") for n in range(2)]
        placed = sem("placed")
        d_ready = sem("d_ready")
        xb_hi = sem("xb_hi")
        xb_lo = sem("xb_lo")
        h_ready = sem("h_ready")
        relued = sem("relued")
        h_hi = sem("h_hi")
        h_lo = sem("h_lo")
        o_ready = sem("o_ready")
        o_kept = sem("o_kept")
        o_stored = sem("o_stored")
        rows_made = sem("rows_made")
        halves = sem("halves")
        yg_landed = sem("yg_landed")
        acc_landed = sem("accb_landed")
        summed = sem("summed")
        out_stored = sem("out_stored")

        with nc.Block() as block:
            @block.sync
            def _(sp):
                def load_x(q, bb):
                    n = 4 * q + bb
                    if bb >= 2 or not first_batch(q):
                        sp.wait_ge(d_ready, 8 * (n - 1))
                    sp.dma_start(xg[:, bb % 2], xhl_dram[n]).then_inc(xg_landed[bb % 2], 16)

                def load_acc(q, bb):
                    n = 4 * q + bb
                    if bb or not first_batch(q):
                        sp.wait_ge(out_stored, 16 * n)
                    sp.dma_start(acc, acc_dram[n]).then_inc(acc_landed, 16)

                def store_y(q, odd, e):
                    if e == 0 and not first_batch(q):
                        sp.wait_ge(o_stored, NTI * E * 16 * q)
                    for t, (lo, hi) in enumerate(TILES):
                        sp.wait_ge(o_kept, NTI * (E * q + e) + t + 1)
                        sp.dma_start(y_dram[odd][e * GS + lo:e * GS + hi, :],
                                     yo[0:hi - lo, t]).then_inc(o_stored, 16)

                def store_out(q, bb):
                    sp.wait_ge(summed, 2 * (4 * q + bb + 1))
                    sp.dma_start(out_v[4 * q + bb], acc).then_inc(out_stored, 16)

                def turn(q, odd, first=False, last=False):
                    load_x(q, 2)
                    load_x(q, 3)
                    if not last:
                        load_x(q + 1, 0)
                        load_x(q + 1, 1)
                    if not first:
                        load_acc(q - 1, 0)
                    for e in range(1, E):
                        store_y(q, odd, e - 1)
                        if not first and e % 2 == 0:
                            store_out(q - 1, e // 2 - 1)
                            load_acc(q - 1, e // 2)
                    if not first:
                        store_out(q - 1, GB - 1)
                    store_y(q, odd, E - 1)

                sp.dma_start(iota[:], c_iota).then_inc(b_const, 16)
                load_x(0, 0)
                load_x(0, 1)
                turn(0, 0, first=True)
                if NQ > 2:
                    with sp.Fori(0, NQ // 2 - 1) as pair:
                        turn(2 * pair + 1, 1)
                        turn(2 * pair + 2, 0)
                turn(NQ - 1, 1, last=True)
                for bb in range(GB):
                    load_acc(NQ - 1, bb)
                    store_out(NQ - 1, bb)
                sp.wait_ge(out_stored, 16 * NB)
                sp.wait_ge(o_stored, NTI * E * 16 * NQ)

            @block.gpsimd
            def _(pool):
                def high_h(q, e):
                    for n in range(NM // 2):
                        k = NM // 2 * (E * q + e) + n
                        if n % 2 == 0 and (e or not first_batch(q)):
                            if n == 0:
                                pool.wait_ge(halves, E * q + e)
                            else:
                                pool.wait_ge(o_ready, NTI * (E * q + e))
                        pool.wait_ge(relued, 2 * k + 2)
                        apart(pool)
                        at = n % 2 * 2
                        pool.tensor_copy(hs[:, n // 2, 0, at:at + 2], relu[:, at:at + 2]).then_inc(h_hi, 1)

                def gather(q, odd, n):
                    bb, k = n // 2, n % 2
                    if n == 0:
                        pool.wait_ge(o_stored, NTI * E * 16 * (q + 1))
                        pool.wait_ge(rows_made, q + 1)
                    if n or not first_batch(q):
                        pool.wait_ge(summed, 8 * q + n)
                        apart(pool)
                    for j in range(NT):
                        pool.indirect_dma_start(yg[:, j], None, y_dram[odd],
                                                bass.IndirectOffsetOnAxis(ap=rows_q[:, k, bb, j:j + 1], axis=0)
                                                ).then_inc(yg_landed, 16)

                def turn(q, odd, first=False, last=False):
                    for e in range(E):
                        high_h(q, e)
                        if not first:
                            gather(q - 1, 1 - odd, e)

                turn(0, 0, first=True)
                if NQ > 2:
                    with pool.Fori(0, NQ // 2 - 1) as pair:
                        turn(2 * pair + 1, 1)
                        turn(2 * pair + 2, 0)
                turn(NQ - 1, 1, last=True)
                for n in range(2 * GB):
                    gather(NQ - 1, 1, n)

            @block.scalar
            def _(act):
                def keep_dispatched(q, bb):
                    for c in range(NC):
                        for half in range(2):
                            u = 8 * (4 * q + bb) + 4 * c + half
                            act.wait_ge(d_ready, u + 1)
                            act.activation(xb[:, 0, c, half * 4:half * 4 + 4, bb],
                                           ps_x[:, half, 0:SLOTS // 2].rearrange("p (e s) -> p e s", s=CAP), ACT.Copy
                                           ).then_inc(xb_hi, 1)

                def hidden(q, e):
                    for m in range(NM):
                        u = NM * (E * q + e) + m
                        if m % 2 == 0 and (m >= 4 or e or not first_batch(q)):
                            act.wait_ge(h_lo, NM // 2 * (E * q + e) + m // 2 - 1)
                        act.wait_ge(h_ready, u + 1)
                        act.activation(relu[:, m % 4], ps_h[:, (NM * e + m) % H_BANKS, 0:GS], ACT.Relu,
                                       bias=b1s[:, e, m:m + 1], scale=sc(UP_SC)).then_inc(relued, 1)

                def turn(q, odd, first=False, last=False):
                    for bb in range(GB):
                        keep_dispatched(q, bb)
                    for e in range(E):
                        hidden(q, e)

                turn(0, 0, first=True)
                if NQ > 2:
                    with act.Fori(0, NQ // 2 - 1) as pair:
                        turn(2 * pair + 1, 1)
                        turn(2 * pair + 2, 0)
                turn(NQ - 1, 1, last=True)

            @block.vector
            def _(dve):
                def keep_dispatched(q, bb):
                    for c in range(NC):
                        for half in range(2):
                            u = 8 * (4 * q + bb) + 4 * c + 2 + half
                            dve.wait_ge(d_ready, u + 1)
                            dve.tensor_copy(xb[:, 1, c, half * 4:half * 4 + 4, bb],
                                            ps_x[:, half, 0:SLOTS // 2].rearrange("p (e s) -> p e s", s=CAP)
                                            ).then_inc(xb_lo, 1)

                def fill_slots(q, bb):
                    n = 4 * q + bb
                    if bb >= 2 or not first_batch(q):
                        dve.wait_ge(d_ready, 8 * (n - 1))
                    for j in range(NT):
                        dve.tensor_tensor(place[:, bb % 2, j],
                                           iota[:].rearrange("p (o s) -> p o s", o=1).to_broadcast([P, E, CAP]),
                                           pos_slot[:, n, j].rearrange("p (e o) -> p e o", o=1).to_broadcast([P, E, CAP]),
                                           ALU.is_equal).then_inc(placed, 1)

                def low_h(q, e, half):
                    for n in range(2 * half, 2 * half + 2):
                        dve.wait_ge(h_hi, NM // 2 * (E * q + e) + n + 1)
                        at = n % 2 * 2
                        dve.tensor_tensor(hs[:, half, 1, at:at + 2], relu[:, at:at + 2], hs[:, half, 0, at:at + 2],
                                          ALU.subtract).then_inc(h_lo, 1)

                def keep_y(q, e):
                    for t, (lo, hi) in enumerate(TILES):
                        u = NTI * (E * q + e) + t
                        dve.wait_ge(o_ready, u + 1)
                        if e or not first_batch(q):
                            dve.wait_ge(o_stored, NTI * 16 * (E * q + e))
                        dve.scalar_tensor_tensor(yo[0:hi - lo, t], ps_o[0:hi - lo, t, 0:C],
                                                 scales[0:hi - lo, DOWN_SC:DOWN_SC + 1], b2b[0:hi - lo, e],
                                                 ALU.mult, ALU.add).then_inc(o_kept, 1)

                def add_term(q, n):
                    bb, k = n // 2, n % 2
                    b = 4 * q + bb
                    if k == 0:
                        dve.wait_ge(acc_landed, 16 * (b + 1))
                    else:
                        dve.wait_ge(summed, 8 * q + n)
                    dve.wait_ge(yg_landed, NT * 16 * (8 * q + n + 1))
                    for j in range(NT):
                        last = dve.scalar_tensor_tensor(acc[:, j], yg[:, j], weight[:, k, b, j:j + 1], acc[:, j],
                                                        ALU.mult, ALU.add)
                    last.then_inc(summed, 1)

                def rows_for(q):
                    dve.tensor_copy(rows_q[:], row_of[:, :, bass.ds(4 * q, GB)]).then_inc(rows_made, 1)

                def turn(q, odd, first=False, last=False):
                    if not first:
                        rows_for(q - 1)
                    for bb in range(GB):
                        keep_dispatched(q, bb)
                        if bb + 2 < GB:
                            fill_slots(q, bb + 2)
                    for e in range(E):
                        low_h(q, e, 0)
                        if e > 0:
                            keep_y(q, e - 1)
                        low_h(q, e, 1)
                        if e > 0 and not first:
                            add_term(q - 1, e - 1)
                    if not first:
                        add_term(q - 1, E - 1)
                    if not last:
                        fill_slots(q + 1, 0)
                        fill_slots(q + 1, 1)
                    keep_y(q, E - 1)

                dve.wait_ge(b_const, 16)
                fill_slots(0, 0)
                fill_slots(0, 1)
                turn(0, 0, first=True)
                if NQ > 2:
                    with dve.Fori(0, NQ // 2 - 1) as pair:
                        turn(2 * pair + 1, 1)
                        turn(2 * pair + 2, 0)
                turn(NQ - 1, 1, last=True)
                rows_for(NQ - 1)
                for n in range(2 * GB):
                    add_term(NQ - 1, n)

            @block.tensor
            def _(pe):
                def dispatch(q, bb):
                    n = 4 * q + bb
                    pe.wait_ge(xg_landed[bb % 2], 32 * q + 16 * (bb // 2 + 1))
                    pe.wait_ge(placed, NT * (n + 1))
                    for c in range(NC):
                        for part in range(2):
                            for half in range(2):
                                if c or part or bb or not first_batch(q):
                                    if part:
                                        pe.wait_ge(xb_hi, 4 * n + 2 * c + half + 1)
                                    else:
                                        pe.wait_ge(xb_lo, 4 * n + 2 * c + half - 1)
                                for j in range(NT):
                                    last = pe.matmul(ps_x[:, half, 0:SLOTS // 2],
                                                     xg[:, bb % 2, j, part, c * P:(c + 1) * P],
                                                     place[:, bb % 2, j, half * 4:half * 4 + 4].rearrange("p e s -> p (e s)"),
                                                     start=(j == 0), stop=(j == NT - 1))
                                last.then_inc(d_ready, 1)

                def up(q, e, half):
                    if e == 0 and half == 0:
                        pe.wait_ge(xb_hi, 16 * (q + 1))
                        pe.wait_ge(xb_lo, 16 * (q + 1))
                    for m in range(half * MH, (half + 1) * MH):
                        u = NM * (E * q + e) + m
                        if m >= H_BANKS or e or not first_batch(q):
                            pe.wait_ge(relued, u - H_BANKS + 1)
                        terms = [(l, r, c) for c in range(NC) for l, r in ((0, 0), (1, 0), (0, 1))]
                        for n, (l, r, c) in enumerate(terms):
                            last = pe.matmul(ps_h[:, m % H_BANKS, 0:GS], w1s[:, l, c, e, m * P:(m + 1) * P],
                                             xb[:, r, c, e].rearrange("p b s -> p (b s)"),
                                             start=(n == 0), stop=(n == len(terms) - 1))
                        last.then_inc(h_ready, 1)

                def down(q, e, half):
                    pe.wait_ge(h_lo, NM // 2 * (E * q + e) + 2 * (half + 1))
                    for t, (lo, hi) in enumerate(TILES):
                        u = NTI * (E * q + e) + t
                        if half == 0 and (e or not first_batch(q)):
                            pe.wait_ge(o_kept, u - NTI + 1)
                        terms = [(l, r, k) for k in range(MH) for l, r in ((0, 0), (0, 1), (1, 0))]
                        for n, (l, r, k) in enumerate(terms):
                            last = pe.matmul(ps_o[0:hi - lo, t, 0:C], hs[:, half, l, k, lo:hi],
                                             w2s[:, r, half * MH + k, e],
                                             start=(half == 0 and n == 0), stop=(half == 1 and n == len(terms) - 1))
                            if n == len(terms) - 1 and (half == 1 or t == NTI - 1):
                                last.then_inc(o_ready if half == 1 else halves, 1)

                def turn(q, odd, first=False, last=False):
                    for bb in range(GB):
                        dispatch(q, bb)
                    up(q, 0, 0)
                    for u in range(2 * E):
                        if u + 1 < 2 * E:
                            up(q, (u + 1) // 2, (u + 1) % 2)
                        down(q, u // 2, u % 2)

                turn(0, 0, first=True)
                if NQ > 2:
                    with pe.Fori(0, NQ // 2 - 1) as pair:
                        turn(2 * pair + 1, 1)
                        turn(2 * pair + 2, 0)
                turn(NQ - 1, 1, last=True)


def program(nc, x, waT, wpT, wr, w1, b1T, w2, b2, c_mask, c_kbias, c_ident, c_ident32, c_maskT, c_tri, c_erank, c_erow, c_brow,
            c_iota, out):
    NB = x.shape[0]
    xhl_dram = nc.dram_tensor("xhl_scratch", [NB, P, NT, 2, C], F16, kind="Internal").ap()
    acc_dram = nc.dram_tensor("acc_scratch", [NB, P, NT, C], F32, kind="Internal").ap()
    qk_dram = nc.dram_tensor("qk_scratch", [NB, 2, 2, 3, P, T], F16, kind="Internal").ap()
    y_dram = [nc.dram_tensor(f"y_scratch{n}", [E * GS, C], F32, kind="Internal").ap() for n in range(2)]
    with ExitStack() as top:
        def lasting(name, shape, dt):
            return top.enter_context(nc.sbuf_tensor(name, shape, dt))

        spare = lasting("spare", [P, max(NT * C, NB * NT * E)], F32)
        logits = spare[:, 0:NB * NT * E].rearrange("p (b j e) -> p b j e", b=NB, j=NT)
        scales = lasting("scales", [P, BOUND + 1], F32)
        attention_phase(nc, top, x, waT, wpT, wr, c_mask, c_kbias, c_ident, c_ident32, c_maskT, xhl_dram, acc_dram,
                        qk_dram, logits, scales)
        pos_slot = lasting("pos_slot", [P, NB, NT, E], F16)
        weight = lasting("weight", [P, 2, NB, NT], F32)
        row_of = lasting("row_of", [P, 2, NB, NT], I32)
        w1s = lasting("w1s", [P, 2, NC, E, HF], F16)
        w2s = lasting("w2s", [P, 2, NM, E, C], F16)
        b1s = lasting("b1s", [P, E, NM], F32)
        b2b = lasting("b2b", [P, E, C], F32)
        routing_phase(nc, top, w1, b1T, w2, b2, c_tri, c_erank, c_erow, c_brow, logits, scales, pos_slot, weight,
                      row_of, w1s, w2s, b1s, b2b)
        expert_phase(nc, top, c_iota, xhl_dram, acc_dram, y_dram, out, scales, spare, pos_slot, weight, row_of,
                     w1s, w2s, b1s, b2b)


def constants(nb):
    import numpy as np

    start = 2.0 ** (-0.5)
    slopes = np.array([start * start ** i for i in range(NH)], dtype=np.float32).astype(np.float64)
    keys = np.arange(T)
    rest = slopes[:, None] * keys[None, :] * ALIBI_UP
    parts = []
    for _ in range(3):
        part = rest.astype(np.float16)
        parts.append(part)
        rest = rest - part.astype(np.float64)
    mask_q = np.zeros((P, T), np.float32)
    mask_q[:, T - P:] = np.where(np.arange(P)[None, :] > np.arange(P)[:, None], -BIG, 0.0)
    mask_k = np.where(np.arange(P)[:, None] > np.arange(P)[None, :], -BIG, 0.0)

    def bf16_bits(a):
        return (np.asarray(a, np.float32).view(np.uint32) >> 16).astype(np.uint16)

    return {
        "c_mask": mask_q,
        "c_kbias": np.stack(parts),
        "c_ident": np.eye(P, dtype=np.float16),
        "c_ident32": np.eye(P, dtype=np.float32),
        "c_maskT": bf16_bits(np.stack([mask_k, np.eye(P)])),
        "c_tri": bf16_bits(np.stack([np.triu(np.ones((P, P)), 1), np.ones((P, P))])),
        "c_erank": np.tile(np.arange(E, 0, -1, dtype=np.float32), (P, 1)),
        "c_erow": np.tile(np.arange(E, dtype=np.float32) * GS, (P, 1)),
        "c_brow": np.tile(np.array([b % GB * CAP for b in range(nb)], np.float32), (P, 1)),
        "c_iota": np.tile(np.arange(CAP, dtype=np.float16), (P, 1)),
    }


def qkv_columns(w):
    import numpy as np

    qk = w[:2 * C].reshape(2, 2, HALF, HD, C).transpose(0, 1, 3, 2, 4).reshape(2 * C, C)
    return np.concatenate([qk, w[2 * C:]]).T


def kernel(L0_attn_x, L0_attn_w_attn, L0_attn_w_proj, L0_ffn_Wr, L0_ffn_W1, L0_ffn_b1, L0_ffn_W2, L0_ffn_b2):
    import numpy as np
    import concourse.bacc as bacc
    from concourse.bass_utils import run_bass_kernel_spmd

    x = np.ascontiguousarray(L0_attn_x)
    arrays = {
        "x": x,
        "waT": np.ascontiguousarray(qkv_columns(np.asarray(L0_attn_w_attn))),
        "wpT": np.ascontiguousarray(np.asarray(L0_attn_w_proj).T),
        "wr": np.ascontiguousarray(L0_ffn_Wr),
        "w1": np.ascontiguousarray(L0_ffn_W1),
        "b1T": np.ascontiguousarray(np.asarray(L0_ffn_b1).reshape(E, NM, P).transpose(2, 0, 1)),
        "w2": np.ascontiguousarray(L0_ffn_W2),
        "b2": np.ascontiguousarray(L0_ffn_b2),
        **constants(x.shape[0]),
    }
    nc = bacc.Bacc("TRN2", target_bir_lowering=False, num_devices=1)
    aps = {name: nc.dram_tensor(name, a.shape, mybir.dt.from_np(a.dtype), kind="ExternalInput").ap()
           for name, a in arrays.items()}
    out = nc.dram_tensor("out", x.shape, mybir.dt.from_np(x.dtype), kind="ExternalOutput").ap()
    program(nc, out=out, **aps)
    r = run_bass_kernel_spmd(nc, [arrays], core_ids=[0])
    return r.results[0]["out"]
```

```python
from contextlib import ExitStack

import concourse.bass as bass
from concourse import mybir

F32 = mybir.dt.float32
F16 = mybir.dt.float16
BF16 = mybir.dt.bfloat16
U32 = mybir.dt.uint32
U16 = mybir.dt.uint16
I32 = mybir.dt.int32
ALU = mybir.AluOpType
ACT = mybir.ActivationFunctionType
AX = mybir.AxisListType
RMAX = bass.bass_isa.ReduceOp.max

P = 128
T, C = 512, 256
NT = T // P
NC = C // P
NH, HD = 16, 16
E, HF = 8, 1024
CAP = int(T / E * 1.25)
NM = HF // P
GB = 4
GS = GB * CAP
H_BANKS = 2
SLOTS = E * CAP
EPS = 1e-5
X_SCALE = 1024.0
ALIBI_UP = 32.0
ROW_UP = 32768.0
HPG = 4
NG = NH // HPG
HALF = NH // 2
LEAD = 6
P_OFF = {0: 0, 1: 512, 3: 896, 2: 1024}
P_LEN = 1280
SCORE_UNITS = ((0,), (1, 3), (2,))
NU = len(SCORE_UNITS)
ROW_ALIBI, ROW_MAX = 64, 96
K_MAXIMA, K_SCORES = 96, 98
BIG = 2.0 ** 100

(M_A, M_P, M_R, V_A, V_P, V_R, A_POW, P_POW, R_POW, A_INV, SQ, QS, KS, S2, S_INV, QROW, Y_SC, ACC_DIV, ACC_SC,
 R_DIV, R_INV, M_1, M_2, M_B, V_1, V_2, V_B, W1_POW, W2_POW, H_POW, UP_DIV, UP_INV, UP_SC, DOWN_DIV, DOWN_SC,
 BOUND) = range(36)


def first_batch(b):
    return isinstance(b, int) and b == 0


def apart(eng):
    eng.nop(nofuse=True)


class Count:

    def __init__(self, before):
        self.before, self.n = before, 0

    def next(self):
        self.n += 1
        return self.before + self.n


def attention_phase(nc, top, x, waT, wpT, wr, w1, w2, c_mask, c_kbias, c_ident, c_ident32, c_maskT, xhl_dram, acc_dram,
                    qk_dram, logits, scales):
    NB = x.shape[0]
    x_v = x.rearrange("b (j p) c -> b p j c", p=P)
    SHARE = E * C * HF // (NB * P)
    w1_v = w1.rearrange("e c h -> (e c h)").rearrange("(b p n) -> b p n", b=NB, p=P)
    w2_v = w2.rearrange("e h c -> (e h c)").rearrange("(b p n) -> b p n", b=NB, p=P)
    with ExitStack() as ctx:
        def sb(name, shape, dt):
            return ctx.enter_context(nc.sbuf_tensor(name, shape, dt))

        def ps(name, shape, dt):
            return ctx.enter_context(nc.psum_tensor(name, shape, dt))

        def sem(name):
            return top.enter_context(nc.semaphore(name))

        def sc(n, lo=0, hi=P):
            return scales[lo:hi, n:n + 1]

        wa32 = sb("wa32", [P, NC, 3 * C], F32)
        wp32 = sb("wp32", [P, NC, C], F32)
        wr32 = sb("wr32", [P, NC, E], F32)
        wa = sb("wa", [P, 2, NC, 3 * C], F16)
        wp = sb("wp", [P, 2, NC, C], F16)
        wrs = sb("wrs", [P, NC, 2, E], F16)
        mask_q = sb("mask_q", [P, T], F32)
        ident = sb("ident", [P, P], F16)
        ident32 = sb("ident32", [P, P], F32)
        identb = sb("identb", [P, P], BF16)
        mask_k = sb("mask_k", [P, P], BF16)
        xin = sb("xin", [P, NT, C], F32)
        stats = sb("stats", [P, NT, 6], F32)
        mv = sb("mv", [P, NT, 2], F32)
        rstd = sb("rstd", [P, 4, NT], F32)
        xs = sb("xs", [P, NT, C], F32)
        xhl = sb("xhl", [P, NT, 2, C], F16)
        xT = sb("xT", [P, 2, NC, T], F16)
        qk_rows = sb("qk_rows", [P, 2, 2, 2, T], F16)
        q_st = sb("q_st", [P, NH, T], F16)
        k_st = sb("k_st", [P, NH, T], F16)
        v_next = sb("v_next", [P, NT, C], F32)
        v_ones = sb("v_ones", [P, NT, NH, 2 * HD], F32)
        maxima = sb("maxima", [P, 2, HPG * NT], F32)
        c_hl = sb("c_hl", [P, 2, 2, HPG * NT], F16)
        c_rows = sb("c_rows", [2 * HPG * NT, 2, P], F16)
        probs = sb("probs", [P, 2, HPG, P_LEN], F32)
        y_sums = sb("y_sums", [P, T], F32)
        y_rec = sb("y_rec", [P, NT, HPG], F32)
        y_nrm = sb("y_nrm", [P, NT, C], F32)
        y_hl = sb("y_hl", [P, 2, NT, C], F16)
        yT = sb("yT", [P, 2, NC, T], F16)
        x_res = sb("x_res", [P, NT, C], F32)
        acc = sb("acc", [P, NT, C], F32)
        w_share = sb("w_share", [P, 2, SHARE], F32)
        w_amax = sb("w_amax", [P, 2], F32)

        ps_max = ps("ps_max", [P, 2, T], F32)
        ps_st = ps("ps_st", [P, 2, T], F32)
        ps_y = ps("ps_y", [P, T], F32)
        ps_c = ps("ps_c", [P, T], F32)
        ps_m = ps("ps_m", [P, 2, T], F32)

        s_w = sem("s_w")
        s_amax = sem("s_amax")
        s_all = sem("s_all")
        s_sc = sem("s_sc")
        s_whi = sem("s_whi")
        s_fill = sem("s_fill")
        s_kb = sem("s_kb")

        x_landed = sem("x_landed")

        with nc.Block() as block:
            @block.sync
            def _(sp):
                sp.dma_start(xin[:], x_v[0]).then_inc(x_landed, 16)
                for dst, src in ((wa32[:], waT.rearrange("(c p) n -> p c n", p=P)),
                                 (wp32[:], wpT.rearrange("(c p) n -> p c n", p=P)),
                                 (wr32[:], wr.rearrange("(c p) n -> p c n", p=P)),
                                 (mask_q[:], c_mask), (ident[:], c_ident), (ident32[:], c_ident32), (mask_k[:].bitcast(U16), c_maskT[0]),
                                 (identb[:].bitcast(U16), c_maskT[1])):
                    sp.dma_start(dst, src).then_inc(s_w, 16)
                sp.wait_ge(s_fill, 3)
                sp.dma_start(k_st[ROW_ALIBI:ROW_ALIBI + 3, :, :], c_kbias).then_inc(s_kb, 16)
                sp.wait_ge(s_kb, 16)
                sp.wait_ge(s_w, 8 * 16)

            @block.vector
            def _(dve):
                dve.memset(q_st[:], 0.0).then_inc(s_fill, 1)
                dve.memset(k_st[:], 0.0).then_inc(s_fill, 1)
                dve.memset(scales[:, M_1:M_2 + 1], 0.0)
                dve.wait_ge(s_w, 8 * 16)
                for n, w in ((M_A, wa32), (M_P, wp32), (M_R, wr32)):
                    dve.tensor_reduce(sc(n), w[:], AX.XY, ALU.max, apply_absolute_value=True).then_inc(s_amax, 1)
                dve.wait_ge(s_all, 1)
                own = Count(0)
                v3, p3 = scales[:, V_A:V_R + 1], scales[:, A_POW:R_POW + 1]
                dve.tensor_scalar(v3, v3, 1e-18, None, ALU.max).then_inc(s_sc, 1)
                dve.wait_ge(s_sc, own.next())
                dve.reciprocal(p3, v3).then_inc(s_sc, 1)
                dve.wait_ge(s_sc, own.next())
                dve.tensor_scalar(p3.bitcast(U32), p3.bitcast(U32), 0x7F800000, None,
                                  ALU.bitwise_and).then_inc(s_sc, 1)
                dve.wait_ge(s_sc, own.next())
                dve.tensor_scalar(sc(SQ), sc(A_POW), 2.0 ** 6, 1024.0, ALU.mult, ALU.min).then_inc(s_sc, 1)
                dve.wait_ge(s_sc, own.next())
                dve.tensor_scalar(sc(Y_SC), sc(A_POW), 2.0 ** 7, None, ALU.mult).then_inc(s_sc, 1)
                dve.wait_ge(s_sc, own.next())
                dve.tensor_scalar(p3, p3, 2.0 ** 15, None, ALU.mult).then_inc(s_sc, 1)
                dve.wait_ge(s_sc, own.next())
                dve.tensor_scalar(sc(ACC_DIV), sc(Y_SC), sc(P_POW), None, ALU.mult).then_inc(s_sc, 1)
                dve.wait_ge(s_sc, own.next())
                dve.tensor_scalar(sc(R_DIV), sc(R_POW), X_SCALE, None, ALU.mult).then_inc(s_sc, 1)
                dve.wait_ge(s_sc, own.next())
                dve.tensor_scalar(sc(A_INV), sc(A_POW), X_SCALE, None, ALU.mult).then_inc(s_sc, 1)
                dve.wait_ge(s_sc, own.next())
                dve.tensor_scalar(sc(S2), sc(SQ), sc(SQ), None, ALU.mult).then_inc(s_sc, 1)
                dve.wait_ge(s_sc, own.next())
                for dst, src in ((ACC_SC, ACC_DIV), (R_INV, R_DIV), (A_INV, A_INV), (S_INV, S2)):
                    dve.reciprocal(sc(dst), sc(src)).then_inc(s_sc, 1)
                    dve.wait_ge(s_sc, own.next())
                dve.tensor_scalar(sc(QROW), sc(S2), 1.0 / ALIBI_UP, None, ALU.mult).then_inc(s_sc, 1)
                dve.wait_ge(s_sc, own.next())
                dve.tensor_scalar(sc(KS), sc(SQ), sc(A_INV), None, ALU.mult).then_inc(s_sc, 1)
                dve.wait_ge(s_sc, own.next())
                dve.tensor_scalar(sc(QS), sc(KS), HD ** -0.5, None, ALU.mult).then_inc(s_sc, 1)
                dve.wait_ge(s_sc, own.next())
                dve.wait_ge(s_whi, 4)
                dve.scalar_tensor_tensor(wa[:, 1], wa32[:], sc(A_POW), wa[:, 0], ALU.mult,
                                         ALU.subtract).then_inc(s_sc, 1)
                dve.scalar_tensor_tensor(wp[:, 1], wp32[:], sc(P_POW), wp[:, 0], ALU.mult,
                                         ALU.subtract).then_inc(s_sc, 1)
                dve.scalar_tensor_tensor(wrs[:, :, 1, :], wr32[:], sc(R_POW), wrs[:, :, 0, :], ALU.mult,
                                         ALU.subtract).then_inc(s_sc, 1)
                dve.wait_ge(s_fill, 3)
                rows = slice(ROW_ALIBI, ROW_ALIBI + 3)
                dve.tensor_scalar(q_st[rows], q_st[rows], sc(QROW, ROW_ALIBI, ROW_ALIBI + 3), None,
                                  ALU.add).then_inc(s_sc, 1)

            @block.gpsimd
            def _(pool):
                pool.wait_ge(s_amax, 3)
                pool.partition_all_reduce(scales[:, V_A:V_R + 1], scales[:, M_A:M_R + 1], P, RMAX).then_inc(s_all, 1)
                pool.wait_ge(s_all, 1)
                pool.wait_ge(s_fill, 2)
                pool.memset(k_st[ROW_MAX:ROW_MAX + 2], ROW_UP).then_inc(s_fill, 1)
                pool.wait_ge(s_fill, 3)
                pool.memset(v_ones[:], 1.0).then_inc(s_fill, 1)

            @block.scalar
            def _(act):
                act.wait_ge(s_sc, 17)
                act.activation(wa[:, 0], wa32[:], ACT.Copy, scale=sc(A_POW)).then_inc(s_whi, 1)
                act.activation(wp[:, 0], wp32[:], ACT.Copy, scale=sc(P_POW)).then_inc(s_whi, 1)
                for c in range(NC):
                    act.activation(wrs[:, c, 0, :], wr32[:, c, :], ACT.Copy, scale=sc(R_POW)).then_inc(s_whi, 1)

        xs_made = sem("xs_made")
        ln_own = sem("ln_own")
        guess_made = sem("guess_made")
        root_made = sem("root_made")
        xhl_split = sem("xhl_split")
        xhl_stored = sem("xhl_stored")
        t_ready = sem("t_ready")
        xt_hi = sem("xt_hi")
        xt_lo = sem("xt_lo")
        r_ready = sem("r_ready")
        r_kept = sem("r_kept")
        qk_ready = sem("qk_ready")
        qk_hi = sem("qk_hi")
        qk_lo = sem("qk_lo")
        v_ready = sem("v_ready")
        v_kept = sem("v_kept")
        v_placed = sem("v_placed")
        qk_stored = [sem(f"qk_stored{h}") for h in range(2)]
        qk_stacked = [sem(f"qk_stacked{g}") for g in range(NG)]
        m_ready = sem("m_ready")
        m_done = sem("m_done")
        c_split = sem("c_split")
        c_turned = sem("c_turned")
        c_kept = sem("c_kept")
        c_in = [sem(f"c_in{g}") for g in range(NG)]
        st_ready = sem("st_ready")
        exp_done = sem("exp_done")
        pv_ready = sem("pv_ready")
        y_kept = sem("y_kept")
        y_turned = sem("y_turned")
        y_rec_made = sem("y_rec_made")
        y_normed = sem("y_normed")
        y_split = sem("y_split")
        yt_ready = sem("yt_ready")
        yt_hi = sem("yt_hi")
        yt_lo = sem("yt_lo")
        xr_landed = sem("xr_landed")
        p_ready = sem("p_ready")
        p_kept = sem("p_kept")
        acc_stored = sem("acc_stored")
        w_landed = sem("w_landed")
        w_seen = sem("w_seen")

        UNITS = NH * NT
        STU = NH * NU
        ROOT_STEPS = 16

        def run_turns(eng, turn):
            turn(0, first=True)
            with eng.Fori(1, NB - 2) as i:
                turn(i)
            turn(NB - 2, norm=False)
            turn(NB - 1, norm=False, front=False)

        def ahead(i, h, front):
            if h + LEAD < NH:
                return i, h + LEAD
            return (i + 1, h + LEAD - NH) if front else None

        with nc.Block() as block:
            @block.sync
            def _(sp):
                def load_x(b):
                    sp.wait_ge(xs_made, b)
                    sp.dma_start(xin[:], x_v[b]).then_inc(x_landed, 16)

                def store_xhl(b):
                    sp.wait_ge(xhl_split, 2 * b + 2)
                    sp.dma_start(xhl_dram[b], xhl[:]).then_inc(xhl_stored, 16)

                def store_q(b, h):
                    sp.wait_ge(qk_lo, 4 * b + 2 * h + 1)
                    sp.dma_start(qk_dram[b, h, 0, 0:2].rearrange("n p t -> p n t"), qk_rows[:, h, 0]
                                 ).then_inc(qk_stored[h], 16)
                    sp.dma_start(qk_dram[b, h, 0, 2], qk_rows[:, h, 0, 0]).then_inc(qk_stored[h], 16)

                def store_k(b, h):
                    sp.wait_ge(qk_lo, 4 * b + 2 * h + 2)
                    sp.dma_start(qk_dram[b, h, 1, 0], qk_rows[:, h, 1, 0]).then_inc(qk_stored[h], 16)
                    sp.dma_start(qk_dram[b, h, 1, 1:3].rearrange("n p t -> p n t"), qk_rows[:, h, 1]
                                 ).then_inc(qk_stored[h], 16)

                def stack_qk(b, g):
                    if not first_batch(b):
                        sp.wait_ge(st_ready, STU * (b - 1) + (g + 1) * HPG * NU)
                        apart(sp)
                    sp.wait_ge(qk_stored[g // 2], 64 * (b + 1))
                    heads = slice(g % 2 * HPG, (g % 2 + 1) * HPG)
                    for qk, stack in ((0, q_st), (1, k_st)):
                        rows = qk_dram[b, g // 2, qk].rearrange("n (d h) t -> (n d) h t", h=HALF)
                        sp.dma_start(stack[0:3 * HD, g * HPG:(g + 1) * HPG, :], rows[:, heads, :]
                                     ).then_inc(qk_stacked[g], 16)

                def rows_c(b, g):
                    sp.wait_ge(c_kept, 4 * b + g + 1)
                    for part in range(2):
                        n = HPG * NT
                        sp.dma_start(q_st[ROW_MAX + part:ROW_MAX + part + 1, g * HPG:(g + 1) * HPG, :]
                                     .rearrange("o h (t q) -> o (h t) q", q=P),
                                     c_rows[part * n:(part + 1) * n, g % 2, :]).then_inc(c_in[g], 16)

                def load_res(b):
                    if not first_batch(b):
                        sp.wait_ge(p_kept, 2 * b)
                    sp.dma_start(x_res[:], x_v[b]).then_inc(xr_landed, 16)

                def load_share(b, first):
                    if not first:
                        sp.wait_ge(w_seen, b)
                        apart(sp)
                    for n, w in enumerate((w1_v, w2_v)):
                        sp.dma_start(w_share[:, n], w[b]).then_inc(w_landed, 16)

                def store_acc(b):
                    for n in range(2):
                        sp.wait_ge(p_kept, 2 * b + n + 1)
                        sp.dma_start(acc_dram[b, :, 2 * n:2 * n + 2], acc[:, 2 * n:2 * n + 2]).then_inc(acc_stored, 16)

                def turn(i, first=False, norm=True, front=True):
                    if not first:
                        stack_qk(i, 3)
                    if front:
                        store_xhl(i + 1)
                    if norm:
                        load_x(i + 2)
                    if not first:
                        load_res(i - 1)
                    load_share(i, first)
                    rows_c(i, 1)
                    if front:
                        store_q(i + 1, 0)
                        store_k(i + 1, 0)
                        stack_qk(i + 1, 0)
                    rows_c(i, 2)
                    if front:
                        store_q(i + 1, 1)
                        store_k(i + 1, 1)
                        stack_qk(i + 1, 1)
                    rows_c(i, 3)
                    if not first:
                        store_acc(i - 1)
                    if front:
                        stack_qk(i + 1, 2)
                        rows_c(i + 1, 0)

                load_x(1)
                store_xhl(0)
                for h in range(2):
                    store_q(0, h)
                    store_k(0, h)
                    stack_qk(0, 2 * h)
                    stack_qk(0, 2 * h + 1)
                rows_c(0, 0)
                run_turns(sp, turn)
                load_res(NB - 1)
                store_acc(NB - 1)
                sp.wait_ge(xhl_stored, 16 * NB)
                sp.wait_ge(acc_stored, 32 * NB)

            @block.gpsimd
            def _(pool):
                def root(b):
                    v, r, a, d = rstd[:, 0, :], rstd[:, 2, :], rstd[:, 1, :], rstd[:, 3, :]
                    own = Count(ROOT_STEPS * b)
                    pool.wait_ge(guess_made, b + 1)
                    for step in range(4):
                        up = X_SCALE if step == 3 else 1.0
                        pool.tensor_tensor(a, r, r, ALU.mult).then_inc(root_made, 1)
                        pool.wait_ge(root_made, own.next())
                        pool.tensor_tensor(d, a, v, ALU.mult).then_inc(root_made, 1)
                        pool.wait_ge(root_made, own.next())
                        apart(pool)
                        pool.tensor_scalar(a, d, -0.5 * up, 1.5 * up, ALU.mult, ALU.add).then_inc(root_made, 1)
                        pool.wait_ge(root_made, own.next())
                        pool.tensor_tensor(r, a, r, ALU.mult).then_inc(root_made, 1)
                        pool.wait_ge(root_made, own.next())
                    assert own.n == ROOT_STEPS

                def split_x(b):
                    pool.wait_ge(xs_made, b + 1)
                    if not first_batch(b):
                        pool.wait_ge(t_ready, 2 * b)
                        pool.wait_ge(xhl_stored, 16 * b)
                    apart(pool)
                    pool.tensor_copy(xhl[:, :, 0, :], xs[:]).then_inc(xhl_split, 1)
                    pool.wait_ge(xhl_split, 2 * b + 1)
                    pool.tensor_tensor(xhl[:, :, 1, :], xs[:], xhl[:, :, 0, :], ALU.subtract).then_inc(xhl_split, 1)

                def split_y(b):
                    if not first_batch(b):
                        pool.wait_ge(yt_ready, 2 * b)
                    pool.wait_ge(y_normed, 4 * b + 4)
                    apart(pool)
                    pool.tensor_copy(y_hl[:, 0], y_nrm[:]).then_inc(y_split, 1)
                    pool.wait_ge(y_split, 2 * b + 1)
                    pool.tensor_tensor(y_hl[:, 1], y_nrm[:], y_hl[:, 0], ALU.subtract).then_inc(y_split, 1)

                def place_v(b):
                    pool.wait_ge(v_kept, 2 * b + 2)
                    if not first_batch(b):
                        pool.wait_ge(pv_ready, 4 * b)
                    apart(pool)
                    pool.tensor_copy(v_ones[:, :, :, 0:HD], v_next[:].rearrange("p j (h d) -> p j h d", d=HD)
                                     ).then_inc(v_placed, 1)

                def turn(i, first=False, norm=True, front=True):
                    place_v(i)
                    if not first:
                        split_y(i - 1)
                    if norm:
                        root(i + 2)
                        split_x(i + 2)

                for b in range(2):
                    root(b)
                    split_x(b)
                run_turns(pool, turn)
                split_y(NB - 1)

            @block.vector
            def _(dve):
                LN_STEPS = 2 * NT + 2

                def statistics(b, j):
                    if j == 0:
                        dve.wait_ge(x_landed, 16 * (b + 1))
                    dve.bn_stats(stats[:, j, :], xin[:, j, :]).then_inc(ln_own, 1)

                def guess(b):
                    own = Count(LN_STEPS * b + NT)
                    dve.wait_ge(ln_own, own.before)
                    apart(dve)
                    for j in range(NT):
                        dve.bn_aggr(mv[:, j, :], stats[:, j, :]).then_inc(ln_own, 1)
                        made = own.next()
                    dve.wait_ge(ln_own, made)
                    var = mv[:, :, 1]
                    r0, r1 = rstd[:, 0, :], rstd[:, 1, :]
                    dve.tensor_scalar(r0, var, EPS, None, ALU.add).then_inc(ln_own, 1)
                    dve.wait_ge(ln_own, own.next())
                    bits = r1.bitcast(U32)
                    dve.tensor_scalar(bits, r0.bitcast(U32), 1, None, ALU.logical_shift_right).then_inc(ln_own, 1)
                    dve.wait_ge(ln_own, own.next())
                    dve.tensor_scalar(rstd[:, 2, :].bitcast(I32), r1.bitcast(I32), -1.0, float(0x5F3759DF), ALU.mult,
                                      ALU.add).then_inc(guess_made, 1)
                    assert own.n == LN_STEPS - NT

                def scale_x(b, j):
                    if j == 0:
                        dve.wait_ge(root_made, ROOT_STEPS * (b + 1))
                        if not first_batch(b):
                            dve.wait_ge(xhl_split, 2 * b)
                    last = dve.tensor_scalar(xs[:, j, :], xin[:, j, :], mv[:, j, 0:1], rstd[:, 2, j:j + 1],
                                             ALU.subtract, ALU.mult)
                    if j == NT - 1:
                        last.then_inc(xs_made, 1)

                def keep_xt(b):
                    dve.wait_ge(t_ready, 2 * b + 2)
                    dve.tensor_copy(xT[:, 1], ps_m[:, 1, :].bitcast(F16).rearrange("p (c t) -> p c t", c=NC)
                                    ).then_inc(xt_lo, 1)

                def keep_logits(b):
                    dve.wait_ge(r_ready, b + 1)
                    dve.tensor_reduce(logits[:, b], ps_m[:, 0, 0:NT * 2 * E].rearrange("p (j l e) -> p j e l", j=NT, l=2),
                                      AX.X, ALU.add).then_inc(r_kept, 1)

                def low_qk(b, n):
                    h, qk = n // 2, n % 2
                    dve.wait_ge(qk_hi, 4 * b + n + 1)
                    dve.scalar_tensor_tensor(qk_rows[:, h, qk, 1, :], ps_m[:, 1 - qk, :], sc(KS if qk else QS),
                                             qk_rows[:, h, qk, 0, :], ALU.mult, ALU.subtract).then_inc(qk_lo, 1)

                def maximum(b, h, qt):
                    g, j = h // HPG, h % HPG
                    dve.wait_ge(m_ready, UNITS * b + h * NT + qt + 1)
                    apart(dve)
                    n = (qt + 1) * P
                    dve.tensor_tensor_reduce(out=ps_max[:, qt % 2, 0:n], in0=ps_max[:, qt % 2, 0:n],
                                             in1=mask_q[:, T - n:T], scale=1.0, scalar=-3e38, op0=ALU.add, op1=ALU.max,
                                             accum_out=maxima[:, g % 2, j * NT + qt:j * NT + qt + 1]
                                             ).then_inc(m_done, 1)

                def negate(b, g):
                    dve.wait_ge(m_done, UNITS * b + (g + 1) * HPG * NT)
                    if g >= 2 or not first_batch(b):
                        dve.wait_ge(c_turned, 4 * b + g - 1)
                    dve.tensor_scalar(c_hl[:, g % 2, 0], maxima[:, g % 2], -1.0 / ROW_UP, None, ALU.mult
                                      ).then_inc(c_split, 1)
                    dve.wait_ge(c_split, 2 * (4 * b + g) + 1)
                    dve.scalar_tensor_tensor(c_hl[:, g % 2, 1], maxima[:, g % 2], -1.0 / ROW_UP, c_hl[:, g % 2, 0],
                                             ALU.mult, ALU.subtract).then_inc(c_split, 1)

                def normalise(b, g):
                    if g == 0 and not first_batch(b):
                        dve.wait_ge(y_split, 2 * b)
                    dve.wait_ge(y_turned, 4 * b + g + 1)
                    rows = ps_y[:].rearrange("p (t j s d) -> p t j s d", t=NT, j=HPG, s=2)
                    dve.reciprocal(y_rec[:], rows[:, :, :, 1, 0]).then_inc(y_rec_made, 1)
                    dve.wait_ge(y_rec_made, 4 * b + g + 1)
                    dve.scalar_tensor_tensor(
                        y_nrm[:, :, g * HPG * HD:(g + 1) * HPG * HD].rearrange("p t (j d) -> p t j d", j=HPG),
                        rows[:, :, :, 0, :], sc(Y_SC),
                        y_rec[:].rearrange("p t (j o) -> p t j o", o=1).to_broadcast([P, NT, HPG, HD]),
                        ALU.mult, ALU.mult).then_inc(y_normed, 1)

                def keep_yt(b):
                    dve.wait_ge(yt_ready, 2 * b + 2)
                    dve.tensor_copy(yT[:, 1], ps_m[:, 1, :].bitcast(F16).rearrange("p (c t) -> p c t", c=NC)
                                    ).then_inc(yt_lo, 1)

                def add_input(b, n):
                    if n == 0:
                        dve.wait_ge(xr_landed, 16 * (b + 1))
                        if not first_batch(b):
                            dve.wait_ge(acc_stored, 32 * b)
                    dve.wait_ge(p_ready, 2 * b + n + 1)
                    dve.scalar_tensor_tensor(acc[:, 2 * n:2 * n + 2], ps_m[:, 1 - n, :].rearrange("p (j c) -> p j c", c=C),
                                             sc(ACC_SC), x_res[:, 2 * n:2 * n + 2], ALU.mult, ALU.add
                                             ).then_inc(p_kept, 1)

                def between(i, h, first, norm, front):
                    if front:
                        if h == 1:
                            keep_xt(i + 1)
                        if h == 3:
                            keep_logits(i + 1)
                        if h in (4, 5, 7, 8):
                            low_qk(i + 1, (4, 5, 7, 8).index(h))
                    if not first:
                        if h == 3:
                            normalise(i - 1, 3)
                        if h == 10:
                            keep_yt(i - 1)
                        if h in (12, 13):
                            add_input(i - 1, h - 12)
                    if h in (7, 12, 15):
                        normalise(i, (7, 12, 15).index(h))
                    if norm and h == 9:
                        guess(i + 2)
                    if h == 14:
                        dve.wait_ge(w_landed, 32 * (i + 1))
                        dve.tensor_reduce(w_amax[:], w_share[:], AX.X, ALU.max, apply_absolute_value=True
                                          ).then_inc(w_seen, 1)
                    if h == 15:
                        dve.wait_ge(w_seen, i + 1)
                        dve.tensor_tensor(scales[:, M_1:M_2 + 1], scales[:, M_1:M_2 + 1], w_amax[:], ALU.max)

                def turn(i, first=False, norm=True, front=True):
                    for h in range(NH):
                        head = ahead(i, h, front)
                        for qt in range(NT):
                            if qt == 2:
                                between(i, h, first, norm, front)
                            if norm and h == 6:
                                statistics(i + 2, qt)
                            if norm and h == 11:
                                scale_x(i + 2, qt)
                            if head:
                                maximum(*head, qt)
                        if head and head[1] % HPG == HPG - 1:
                            negate(head[0], head[1] // HPG)

                for b in range(2):
                    for j in range(NT):
                        statistics(b, j)
                    guess(b)
                    if b == 1:
                        keep_xt(0)
                    for j in range(NT):
                        scale_x(b, j)
                keep_logits(0)
                for n in range(4):
                    low_qk(0, n)
                for h in range(LEAD):
                    for qt in range(NT):
                        maximum(0, h, qt)
                    if h == HPG - 1:
                        negate(0, 0)
                run_turns(dve, turn)
                normalise(NB - 1, 3)
                keep_yt(NB - 1)
                add_input(NB - 1, 0)
                add_input(NB - 1, 1)

            @block.scalar
            def _(act):
                def keep_xt(b):
                    act.wait_ge(t_ready, 2 * b + 1)
                    act.activation(xT[:, 0], ps_m[:, 0, :].bitcast(F16).rearrange("p (c t) -> p c t", c=NC), ACT.Copy
                                   ).then_inc(xt_hi, 1)

                def keep_yt(b):
                    act.wait_ge(yt_ready, 2 * b + 1)
                    act.activation(yT[:, 0], ps_m[:, 0, :].bitcast(F16).rearrange("p (c t) -> p c t", c=NC), ACT.Copy
                                   ).then_inc(yt_hi, 1)

                def high_qk(b, n):
                    h, qk = n // 2, n % 2
                    act.wait_ge(qk_ready, 4 * b + n + 1)
                    if not first_batch(b):
                        act.wait_ge(qk_stored[h], 64 * b)
                    act.activation(qk_rows[:, h, qk, 0, :], ps_m[:, 1 - qk, :], ACT.Copy, scale=sc(KS if qk else QS)
                                   ).then_inc(qk_hi, 1)

                def keep_v(b, n):
                    act.wait_ge(v_ready, 2 * b + n + 1)
                    if not first_batch(b):
                        act.wait_ge(v_placed, b)
                    act.activation(v_next[:, 2 * n:2 * n + 2], ps_m[:, 1 - n, :].rearrange("p (j c) -> p j c", c=C),
                                   ACT.Copy, scale=sc(A_INV)).then_inc(v_kept, 1)

                def keep_c(b, g):
                    act.wait_ge(c_turned, 4 * b + g + 1)
                    if g >= 2:
                        act.wait_ge(c_in[g - 2], 32 * (b + 1))
                    elif not first_batch(b):
                        act.wait_ge(c_in[g + 2], 32 * b)
                    act.activation(c_rows[:, g % 2, :], ps_c[0:2 * HPG * NT, 0:P // 2].bitcast(F16), ACT.Copy
                                   ).then_inc(c_kept, 1)

                def exps(b, h, u):
                    g, j = h // HPG, h % HPG
                    if j == 0 and u == 0 and (g >= 2 or not first_batch(b)):
                        act.wait_ge(pv_ready, 4 * b + g - 1)
                    n = h * NU + u
                    act.wait_ge(st_ready, STU * b + n + 1)
                    size = min(T, P_LEN - u * T)
                    act.activation(probs[:, g % 2, j, u * T:u * T + size], ps_st[:, n % 2, 0:size], ACT.Exp,
                                   scale=sc(S_INV)).then_inc(exp_done, 1)

                def keep_y(b, g):
                    act.wait_ge(pv_ready, 4 * b + g + 1)
                    if g or not first_batch(b):
                        act.wait_ge(y_turned, 4 * b + g)
                    act.activation(y_sums[:], ps_y[:], ACT.Copy).then_inc(y_kept, 1)

                def turn(i, first=False, norm=True, front=True):
                    for h in range(NH):
                        head_before = ahead(i, h - 1, front)
                        for u in range(NU):
                            exps(i, h, u)
                            if u == 1 and head_before and head_before[1] % HPG == HPG - 1:
                                keep_c(head_before[0], head_before[1] // HPG)
                        if front:
                            if h == 0:
                                keep_xt(i + 1)
                            if h in (3, 4, 6, 7):
                                high_qk(i + 1, (3, 4, 6, 7).index(h))
                            if h in (14, 15):
                                keep_v(i + 1, h - 14)
                        if h == 1 and not first:
                            keep_y(i - 1, 3)
                        if h in (5, 10, 13):
                            keep_y(i, (5, 10, 13).index(h))
                        if h == 9 and not first:
                            keep_yt(i - 1)

                keep_xt(0)
                for n in range(4):
                    high_qk(0, n)
                for n in range(2):
                    keep_v(0, n)
                keep_c(0, 0)
                run_turns(act, turn)
                keep_y(NB - 1, 3)
                keep_yt(NB - 1)

            @block.tensor
            def _(pe):
                def products(out, left, right, start, end):
                    terms = [(l, r, c) for c in range(NC) for l, r in ((0, 0), (1, 0), (0, 1))]
                    for n in range(start, end):
                        l, r, c = terms[n]
                        last = pe.matmul(out, left(l, c), right(r, c), start=(n == 0), stop=(n == len(terms) - 1),
                                         skip_group_check=True)
                    return last

                def row_products(bank, left, right, quarter):
                    j, half = quarter // 2, quarter % 2
                    return products(bank[:, j * C:(j + 1) * C], lambda l, c: left(l, c, j), right, 3 * half, 3 * half + 3)

                def transpose_rows(rows, quarter):
                    part, c = quarter // 2, quarter % 2
                    bank = ps_m[:, part, :].bitcast(F16).rearrange("p (c t) -> p c t", c=NC)
                    for j in range(NT):
                        last = pe.transpose(bank[:, c, j * P:(j + 1) * P], rows(part)[:, j, c * P:(c + 1) * P], ident[:])
                    return last

                def transpose_x(b, quarter):
                    if quarter == 0 and not first_batch(b):
                        pe.wait_ge(v_kept, 2 * b)
                    if quarter % 2 == 0:
                        pe.wait_ge(xhl_split, 2 * b + quarter // 2 + 1)
                    last = transpose_rows(lambda part: xhl[:, :, part], quarter)
                    if quarter % 2 == 1:
                        last.then_inc(t_ready, 1)

                def router(b, quarter):
                    if quarter == 0:
                        pe.wait_ge(xt_hi, b + 1)
                        pe.wait_ge(xt_lo, b + 1)
                    j = quarter
                    for n in range(2 * NC):
                        part, c = n // NC, n % NC
                        last = pe.matmul(ps_m[:, 0, j * 2 * E:(j + 1) * 2 * E], xT[:, part, c, j * P:(j + 1) * P],
                                         wrs[:, c].rearrange("p l e -> p (l e)"), start=(n == 0),
                                         stop=(n == 2 * NC - 1), skip_group_check=True)
                    if quarter == 3:
                        last.then_inc(r_ready, 1)

                def qk(b, n, quarter):
                    h, is_k = n // 2, n % 2
                    if quarter == 0 and n >= 2:
                        pe.wait_ge(qk_lo, 4 * b + n - 1)
                    if quarter == 0 and n == 1:
                        pe.wait_ge(r_kept, b + 1)
                    at = is_k * C + h * P
                    last = products(ps_m[:, 1 - is_k, :], lambda l, c: wa[:, l, c, at:at + P], lambda r, c: xT[:, r, c, :],
                                    (0, 2, 3, 5)[quarter], (2, 3, 5, 6)[quarter])
                    if quarter == 3:
                        last.then_inc(qk_ready, 1)

                def values(b, n, quarter, first=False):
                    if quarter == 0:
                        if first:
                            pe.wait_ge(qk_lo, 4 * b + 4)
                        else:
                            pe.wait_ge(p_kept, 2 * (b - 2) + n + 1)
                    last = row_products(ps_m[:, 1 - n], lambda l, c, j: xT[:, l, c, (2 * n + j) * P:(2 * n + j + 1) * P],
                                        lambda r, c: wa[:, r, c, 2 * C:3 * C], quarter)
                    if quarter == 3:
                        last.then_inc(v_ready, 1)

                def transpose_y(b, front, quarter):
                    if quarter == 0:
                        if front:
                            pe.wait_ge(qk_lo, 4 * (b + 2) + 4)
                        elif b == NB - 1:
                            pe.wait_ge(p_kept, 2 * b)
                        else:
                            pe.wait_ge(v_kept, 2 * (b + 2))
                    if quarter % 2 == 0:
                        pe.wait_ge(y_split, 2 * b + quarter // 2 + 1)
                    last = transpose_rows(lambda part: y_hl[:, part], quarter)
                    if quarter % 2 == 1:
                        last.then_inc(yt_ready, 1)

                def project(b, n, quarter):
                    if quarter == 0:
                        pe.wait_ge(yt_hi, b + 1)
                        pe.wait_ge(yt_lo, b + 1)
                    last = row_products(ps_m[:, 1 - n], lambda l, c, j: yT[:, l, c, (2 * n + j) * P:(2 * n + j + 1) * P],
                                        lambda r, c: wp[:, r, c, :], quarter)
                    if quarter == 3:
                        last.then_inc(p_ready, 1)

                def score_maxima(b, h, qt):
                    u = h * NT + qt
                    if u % (HPG * NT) == 0:
                        pe.wait_ge(qk_stacked[h // HPG], 32 * (b + 1))
                    if u >= 2 or not first_batch(b):
                        pe.wait_ge(m_done, UNITS * b + u - 1)
                    n = (qt + 1) * P
                    pe.matmul(ps_max[:, qt % 2, 0:n], q_st[0:K_MAXIMA, h, qt * P:n], k_st[0:K_MAXIMA, h, 0:n],
                              start=True, stop=True).then_inc(m_ready, 1)

                def turn_c(b, g):
                    pe.wait_ge(c_split, 2 * (4 * b + g) + 2)
                    if g >= 1 or not first_batch(b):
                        pe.wait_ge(c_kept, 4 * b + g)
                    pe.transpose(ps_c[0:2 * HPG * NT, 0:P // 2].bitcast(F16),
                                 c_hl[:, g % 2].rearrange("p l n -> p (l n)"), ident[:]).then_inc(c_turned, 1)

                def scores(b, h, u):
                    n = h * NU + u
                    if n % (HPG * NU) == 0:
                        pe.wait_ge(c_in[h // HPG], 32 * (b + 1))
                    if n >= 2 or not first_batch(b):
                        pe.wait_ge(exp_done, STU * b + n - 1)
                    for kt in SCORE_UNITS[u]:
                        at, size = P_OFF[kt] - u * T, T - kt * P
                        pe.matmul(ps_st[:, n % 2, at:at + size], k_st[0:K_SCORES, h, kt * P:(kt + 1) * P],
                                  q_st[0:K_SCORES, h, kt * P:T], start=True, stop=False, skip_group_check=True)
                        last = pe.matmul(ps_st[:, n % 2, at:at + P], identb[:], mask_k[:], start=False, stop=True,
                                         skip_group_check=True)
                    last.then_inc(st_ready, 1)

                def weighted_sums(b, g, quarter):
                    if quarter == 0:
                        pe.wait_ge(exp_done, STU * b + (g + 1) * HPG * NU)
                        if g == 0:
                            pe.wait_ge(v_placed, b + 1)
                        if g >= 1 or not first_batch(b):
                            pe.wait_ge(y_normed, 4 * b + g)
                    kt = quarter
                    for j in range(HPG):
                        last = pe.matmul(ps_y[32 * j:32 * j + 32, kt * P:T], v_ones[:, kt, g * HPG + j, :],
                                         probs[:, g % 2, j, P_OFF[kt]:P_OFF[kt] + T - kt * P],
                                         start=(kt == 0), stop=(kt == NT - 1), skip_group_check=True)
                    if quarter == 3:
                        last.then_inc(pv_ready, 1)

                def turn_y(b, g, quarter):
                    if quarter == 1:
                        pe.wait_ge(y_kept, 4 * b + g + 1)
                    for j in ((), (0,), (1,), (2, 3))[quarter]:
                        last = pe.transpose(ps_y[:, j * P:(j + 1) * P], y_sums[:, j * P:(j + 1) * P], ident32[:])
                    if quarter == 3:
                        last.then_inc(y_turned, 1)

                def between(i, h, quarter, first, front):
                    if front:
                        if h == 0:
                            transpose_x(i + 1, quarter)
                        if h == 2:
                            router(i + 1, quarter)
                        if h in (3, 4, 6, 7):
                            qk(i + 1, (3, 4, 6, 7).index(h), quarter)
                        if h in (14, 15):
                            values(i + 1, h - 14, quarter, first)
                    if not first:
                        if h == 1:
                            weighted_sums(i - 1, 3, quarter)
                        if h == 2:
                            turn_y(i - 1, 3, quarter)
                        if h == 9:
                            transpose_y(i - 1, front, quarter)
                        if h in (11, 12):
                            project(i - 1, h - 11, quarter)
                    if h in (5, 10, 13):
                        weighted_sums(i, (5, 10, 13).index(h), quarter)
                    if h in (6, 11, 14):
                        turn_y(i, (6, 11, 14).index(h), quarter)

                def turn(i, first=False, norm=True, front=True):
                    for h in range(NH):
                        head, head_before = ahead(i, h, front), ahead(i, h - 1, front)
                        for qt in range(NT):
                            if head:
                                score_maxima(*head, qt)
                            if qt == 2 and head_before and head_before[1] % HPG == HPG - 1:
                                turn_c(head_before[0], head_before[1] // HPG)
                            if qt < NU:
                                scores(i, h, qt)
                            between(i, h, qt, first, front)

                for quarter in range(4):
                    transpose_x(0, quarter)
                for quarter in range(4):
                    router(0, quarter)
                for n in range(4):
                    for quarter in range(4):
                        qk(0, n, quarter)
                for n in range(2):
                    for quarter in range(4):
                        values(0, n, quarter, first=True)
                for h in range(LEAD):
                    for qt in range(NT):
                        score_maxima(0, h, qt)
                    if h == HPG:
                        turn_c(0, 0)
                run_turns(pe, turn)
                for quarter in range(4):
                    weighted_sums(NB - 1, 3, quarter)
                for quarter in range(4):
                    turn_y(NB - 1, 3, quarter)
                for quarter in range(4):
                    transpose_y(NB - 1, False, quarter)
                for n in range(2):
                    for quarter in range(4):
                        project(NB - 1, n, quarter)


def routing_phase(nc, top, w1, b1T, w2, b2, c_tri, c_erank, c_erow, c_brow, logits, scales, pos_slot, weight, row_of,
                  w1s, w2s, b1s, b2b):
    NB = logits.shape[1]
    N = NB * NT
    with ExitStack() as ctx:
        def sb(name, shape, dt):
            return ctx.enter_context(nc.sbuf_tensor(name, shape, dt))

        def sem(name):
            return top.enter_context(nc.semaphore(name))

        def sc(n):
            return scales[:, n:n + 1]

        RING = 4
        ring = sb("ring", [P, RING, NC * HF], F32)
        tri = sb("tri", [P, 2, P], BF16)
        erank = sb("erank", [P, E], F32)
        erow = sb("erow", [P, E], F32)
        brow = sb("brow", [P, NB], F32)
        one = sb("one", [P, 4, N], F32)
        pk = sb("pk", [P, 2, N], F32)
        t0 = sb("t0", [P, N, E], F32)
        t1 = sb("t1", [P, N, E], F32)
        oh = sb("oh", [P, 2, N, E], F32)
        taken = sb("taken", [P, NB, NT, E], BF16)
        before = sb("before", [P, NB, NT, E], BF16)
        ps_pos = ctx.enter_context(nc.psum_tensor("ps_pos", [P, N * E], F32))

        s_c = sem("r_const")
        s_w = [sem(f"w_ring{n}") for n in range(RING)]
        s_amax = sem("b1_amax")
        s_top = sem("w_amax_all")
        s_own = sem("r_own")
        s_exp = sem("r_exp")
        s_pos = sem("r_pos")
        s_route = sem("r_route")
        s_pow = sem("w_pow")
        s_hi = sem("w_hi")
        s_lo = sem("w_lo")
        s_b1 = sem("b1_scaled")

        def in_ring(n):
            rows = NC if n < E else NM
            return ring[:, n % RING].rearrange("p (k n) -> p k n", k=rows)

        def part_of(n, part):
            return w1s[:, part, :, n, :] if n < E else w2s[:, part, :, n - E, :]

        with nc.Block() as block:
            @block.sync
            def _(sp):
                for dst, src in ((tri[:].bitcast(U16), c_tri.rearrange("n p q -> p n q")), (erank[:], c_erank), (erow[:], c_erow),
                                 (brow[:], c_brow), (b1s[:], b1T),
                                 (b2b[:], b2.rearrange("e c -> (e c)").partition_broadcast(P))):
                    sp.dma_start(dst, src).then_inc(s_c, 16)
                for n in range(2 * E):
                    if n >= RING:
                        sp.wait_ge(s_lo, n - RING + 1)
                    if n < E:
                        src = w1[n].rearrange("(c p) h -> p c h", p=P)
                    else:
                        src = w2[n - E].rearrange("(k p) n -> p k n", p=P)
                    sp.dma_start(in_ring(n), src).then_inc(s_w[n % RING], 16)

            @block.gpsimd
            def _(pool):
                pool.wait_ge(s_amax, 1)
                pool.partition_all_reduce(scales[:, V_1:V_B + 1], scales[:, M_1:M_B + 1], P, RMAX).then_inc(s_top, 1)

            @block.scalar
            def _(act):
                act.wait_ge(s_route, 1)
                act.activation(t1[:], t0[:], ACT.Exp, scale=sc(R_INV)).then_inc(s_exp, 1)
                act.wait_ge(s_pow, 1)
                act.activation(b1s[:], b1s[:], ACT.Copy, scale=sc(H_POW)).then_inc(s_b1, 1)
                for n in range(2 * E):
                    act.wait_ge(s_w[n % RING], 16 * (n // RING + 1))
                    act.activation(part_of(n, 0), in_ring(n), ACT.Copy, scale=sc(W1_POW if n < E else W2_POW)
                                   ).then_inc(s_hi, 1)

            @block.tensor
            def _(pe):
                pe.wait_ge(s_c, 6 * 16)
                pe.wait_ge(s_route, 2)
                flat_taken = taken[:].rearrange("p b j e -> p (b j e)")
                flat_before = before[:].rearrange("p b j e -> p (b j e)")
                for at in range(0, N * E, 512):
                    to = min(at + 512, N * E)
                    pe.matmul(ps_pos[:, at:to], tri[:, 0], flat_taken[:, at:to], start=True, stop=False)
                    last = pe.matmul(ps_pos[:, at:to], tri[:, 1], flat_before[:, at:to], start=False, stop=True)
                last.then_inc(s_pos, 1)

            @block.vector
            def _(dve):
                own = Count(0)

                def bc(v):
                    return v.rearrange("p (n o) -> p n o", o=1).to_broadcast([P, N, E])

                def row(v):
                    return v.rearrange("p (o e) -> p o e", o=1).to_broadcast([P, N, E])

                lg = logits.rearrange("p b j e -> p (b j) e")
                dve.tensor_reduce(one[:, 0], lg, AX.X, ALU.max).then_inc(s_own, 1)
                dve.wait_ge(s_own, own.next())
                dve.tensor_tensor(t0[:], lg, bc(one[:, 0]), ALU.subtract).then_inc(s_route, 1)
                dve.wait_ge(s_c, 6 * 16)
                dve.tensor_reduce(sc(M_B), b1s[:], AX.XY, ALU.max, apply_absolute_value=True).then_inc(s_amax, 1)

                dve.wait_ge(s_top, 1)
                v2, p2 = scales[:, V_1:V_2 + 1], scales[:, W1_POW:W2_POW + 1]
                dve.tensor_scalar(v2, v2, 1e-18, None, ALU.max).then_inc(s_own, 1)
                dve.wait_ge(s_own, own.next())
                dve.scalar_tensor_tensor(sc(BOUND), sc(V_1), float(C), sc(V_B), ALU.mult, ALU.add).then_inc(s_own, 1)
                dve.wait_ge(s_own, own.next())
                dve.reciprocal(p2, v2).then_inc(s_own, 1)
                dve.wait_ge(s_own, own.next())
                dve.reciprocal(sc(H_POW), sc(BOUND)).then_inc(s_own, 1)
                dve.wait_ge(s_own, own.next())
                p3 = scales[:, W1_POW:H_POW + 1]
                dve.tensor_scalar(p3.bitcast(U32), p3.bitcast(U32), 0x7F800000, None, ALU.bitwise_and
                                  ).then_inc(s_own, 1)
                dve.wait_ge(s_own, own.next())
                dve.tensor_scalar(p3, p3, 2.0 ** 15, None, ALU.mult).then_inc(s_pow, 1)

                def low(*ns):
                    for n in ns:
                        dve.wait_ge(s_hi, n + 1)
                        dve.scalar_tensor_tensor(part_of(n, 1), in_ring(n), sc(W1_POW if n < E else W2_POW),
                                                 part_of(n, 0), ALU.mult, ALU.subtract).then_inc(s_lo, 1)

                dve.wait_ge(s_exp, 1)
                dve.tensor_reduce(one[:, 1], t1[:], AX.X, ALU.add).then_inc(s_own, 1)
                dve.wait_ge(s_own, own.next())
                dve.reciprocal(one[:, 3], one[:, 1]).then_inc(s_own, 1)
                dve.wait_ge(s_own, own.next())
                dve.tensor_tensor(t0[:], t1[:], bc(one[:, 3]), ALU.mult).then_inc(s_own, 1)
                dve.wait_ge(s_own, own.next())
                low(0)
                for k in range(2):
                    dve.tensor_reduce(pk[:, k], t0[:], AX.X, ALU.max).then_inc(s_own, 1)
                    dve.wait_ge(s_own, own.next())
                    dve.tensor_tensor(t1[:], t0[:], bc(pk[:, k]), ALU.is_equal).then_inc(s_own, 1)
                    dve.wait_ge(s_own, own.next())
                    dve.tensor_tensor(t1[:], t1[:], row(erank[:]), ALU.mult).then_inc(s_own, 1)
                    dve.wait_ge(s_own, own.next())
                    low(1 + 2 * k)
                    dve.tensor_reduce(one[:, 2], t1[:], AX.X, ALU.max).then_inc(s_own, 1)
                    dve.wait_ge(s_own, own.next())
                    dve.tensor_tensor(oh[:, k], t1[:], bc(one[:, 2]), ALU.is_equal).then_inc(s_own, 1)
                    dve.wait_ge(s_own, own.next())
                    low(2 + 2 * k)
                    if k == 0:
                        dve.scalar_tensor_tensor(t0[:], oh[:, 0], -2.0, t0[:], ALU.mult, ALU.add).then_inc(s_own, 1)
                        dve.wait_ge(s_own, own.next())
                dve.tensor_tensor(taken[:].rearrange("p b j e -> p (b j) e"), oh[:, 0], oh[:, 1], ALU.add
                                  ).then_inc(s_own, 1)
                dve.memset(before[:, :, 0, :], 0.0).then_inc(s_own, 1)
                own.next()
                dve.wait_ge(s_own, own.next())
                for j in range(1, NT):
                    last = dve.tensor_tensor(before[:, :, j, :], before[:, :, j - 1, :], taken[:, :, j - 1, :], ALU.add)
                    last.then_inc(s_own, 1)
                    dve.wait_ge(s_own, own.next())
                dve.wait_ge(s_route, 1)
                dve.memset(one[:, 3], 0.0).then_inc(s_route, 1)
                low(5)
                dve.wait_ge(s_pos, 1)
                dve.tensor_copy(t0[:], ps_pos[:].rearrange("p (n e) -> p n e", e=E)).then_inc(s_own, 1)
                dve.wait_ge(s_own, own.next())
                dve.tensor_scalar(t1[:], t0[:], CAP - 0.5, None, ALU.is_lt).then_inc(s_own, 1)
                dve.wait_ge(s_own, own.next())
                dve.tensor_tensor(t1[:], t1[:], taken[:].rearrange("p b j e -> p (b j) e"), ALU.mult).then_inc(s_own, 1)
                dve.wait_ge(s_own, own.next())
                low(6)
                ps = pos_slot[:].rearrange("p b j e -> p (b j) e")
                lgf = logits.rearrange("p b j e -> p (b j) e")
                dve.scalar_tensor_tensor(lgf, t0[:], 1.0, t1[:], ALU.add, ALU.mult).then_inc(s_own, 1)
                dve.wait_ge(s_own, own.next())
                dve.tensor_scalar(ps, lgf, -1.0, None, ALU.add).then_inc(s_own, 1)
                own.next()
                dve.tensor_scalar(t0[:], t0[:], float(CAP - 1), None, ALU.min).then_inc(s_own, 1)
                dve.wait_ge(s_own, own.next())
                dve.tensor_tensor(t0[:], t0[:], row(erow[:]), ALU.add).then_inc(s_own, 1)
                dve.wait_ge(s_own, own.next())
                low(7)
                for k in range(2):
                    dve.tensor_tensor(lgf, t0[:], oh[:, k], ALU.mult).then_inc(s_own, 1)
                    dve.wait_ge(s_own, own.next())
                    dve.tensor_reduce(one[:, 0], lgf, AX.X, ALU.add).then_inc(s_own, 1)
                    dve.wait_ge(s_own, own.next())
                    dve.tensor_tensor(row_of[:, k], one[:, 0].rearrange("p (b j) -> p b j", j=NT),
                                      brow[:].rearrange("p (b o) -> p b o", o=1).to_broadcast([P, NB, NT]), ALU.add
                                      ).then_inc(s_own, 1)
                    dve.wait_ge(s_own, own.next())
                    low(8 + k)
                    dve.tensor_tensor(lgf, t1[:], oh[:, k], ALU.mult).then_inc(s_own, 1)
                    dve.wait_ge(s_own, own.next())
                    dve.tensor_reduce(one[:, 1], lgf, AX.X, ALU.add).then_inc(s_own, 1)
                    dve.wait_ge(s_own, own.next())
                    dve.tensor_tensor(weight[:, k], pk[:, k].rearrange("p (b j) -> p b j", j=NT),
                                      one[:, 1].rearrange("p (b j) -> p b j", j=NT), ALU.mult).then_inc(s_own, 1)
                    dve.wait_ge(s_own, own.next())
                dve.wait_ge(s_pow, 1)
                dve.tensor_scalar(sc(UP_DIV), sc(W1_POW), X_SCALE, None, ALU.mult).then_inc(s_own, 1)
                dve.wait_ge(s_own, own.next())
                dve.reciprocal(sc(UP_INV), sc(UP_DIV)).then_inc(s_own, 1)
                dve.wait_ge(s_own, own.next())
                dve.tensor_tensor(sc(UP_SC), sc(UP_INV), sc(H_POW), ALU.mult).then_inc(s_own, 1)
                own.next()
                dve.tensor_tensor(sc(DOWN_DIV), sc(H_POW), sc(W2_POW), ALU.mult).then_inc(s_own, 1)
                dve.wait_ge(s_own, own.next())
                dve.reciprocal(sc(DOWN_SC), sc(DOWN_DIV)).then_inc(s_own, 1)
                low(*range(10, 2 * E))


def expert_phase(nc, top, c_iota, xhl_dram, acc_dram, y_dram, out, scales, spare, pos_slot, weight,
                 row_of, w1s, w2s, b1s, b2b):
    NB = pos_slot.shape[1]
    NQ = NB // GB
    assert NQ % 2 == 0
    out_v = out.rearrange("b (j p) c -> b p j c", p=P)
    TILES = ((0, P), (P, 2 * P), (2 * P, GS))
    NTI = len(TILES)
    MH = NM // 2
    EH = E // 2
    with ExitStack() as ctx:
        def sb(name, shape, dt):
            return ctx.enter_context(nc.sbuf_tensor(name, shape, dt))

        def ps(name, shape, dt):
            return ctx.enter_context(nc.psum_tensor(name, shape, dt))

        def sem(name):
            return top.enter_context(nc.semaphore(name))

        def sc(n):
            return scales[:, n:n + 1]

        iota = sb("iota", [P, CAP], F16)
        xg = sb("xg", [P, 2, NT, 2, C], F16)
        place = sb("place", [P, 2, NT, EH, CAP], F16)
        xb = sb("xb", [P, 2, NC, E, GB, CAP], F16)
        relu = sb("relu", [P, MH, GS], F32)
        hs = sb("hs", [P, 2, 2, MH, GS], F16)
        yo = sb("yo", [P, NTI, C], F32)
        rows_q = sb("rows_q", [P, 2, GB, NT], I32)
        yg = sb("yg", [P, 2, NT, C], F32)
        acc = spare[:, 0:NT * C].rearrange("p (j c) -> p j c", c=C)
        ps_x = ps("ps_x", [P, 2, 512], F32)
        ps_h = ps("ps_h", [P, H_BANKS, 512], F32)
        ps_o = ps("ps_o", [P, 3, 512], F32)

        b_const = sem("b_const")
        xg_landed = [sem(f"xg_landed{n}") for n in range(2)]
        placed = sem("placed")
        d_ready = sem("d_ready")
        xb_hi = sem("xb_hi")
        xb_lo = sem("xb_lo")
        h_ready = sem("h_ready")
        relued = sem("relued")
        h_lo = sem("h_lo")
        o_ready = sem("o_ready")
        o_kept = sem("o_kept")
        o_stored = sem("o_stored")
        rows_made = sem("rows_made")
        halves = sem("halves")
        yg_landed = [sem(f"yg_landed{k}") for k in range(2)]
        acc_landed = sem("accb_landed")
        summed = sem("summed")
        out_stored = sem("out_stored")

        def run_turns(eng, turn):
            turn(0, 0, first=True)
            if NQ > 2:
                with eng.Fori(0, NQ // 2 - 1) as pair:
                    turn(2 * pair + 1, 1)
                    turn(2 * pair + 2, 0)
            turn(NQ - 1, 1, last=True)

        def dispatched(q, e, last):
            if last and e >= EH:
                return None
            half = 1 if e % E < EH else 0
            return 2 * GB * q + GB + e, GB * (q + (e + EH) // E) + e % GB, half

        with nc.Block() as block:
            @block.sync
            def _(sp):
                def load_x(d, batch, half, parity, early=False):
                    if not early:
                        sp.wait_ge(d_ready, 4 * (d - 1))
                    sp.dma_start(xg[:, parity], xhl_dram[batch]).then_inc(xg_landed[parity], 16)

                def load_acc(q, bb):
                    n = GB * q + bb
                    if bb or not first_batch(q):
                        sp.wait_ge(out_stored, 16 * n)
                    sp.dma_start(acc, acc_dram[n]).then_inc(acc_landed, 16)

                def store_y(q, odd, e):
                    if e == 0 and not first_batch(q):
                        sp.wait_ge(o_stored, NTI * E * 16 * q)
                    for t, (lo, hi) in enumerate(TILES):
                        sp.wait_ge(o_kept, NTI * (E * q + e) + t + 1)
                        sp.dma_start(y_dram[odd][e * GS + lo:e * GS + hi, :],
                                     yo[0:hi - lo, t]).then_inc(o_stored, 16)

                def store_out(q, bb):
                    sp.wait_ge(summed, 2 * (GB * q + bb + 1))
                    sp.dma_start(out_v[GB * q + bb], acc).then_inc(out_stored, 16)

                def turn(q, odd, first=False, last=False):
                    for e in range(E):
                        if not first and e == 0:
                            store_y(q - 1, 1 - odd, E - 1)
                            load_acc(q - 1, 0)
                        nxt = dispatched(q, e + 2, last)
                        if nxt:
                            load_x(*nxt, e % 2)
                        if e > 0:
                            store_y(q, odd, e - 1)
                        if not first and e % 2 == 0 and e > 0:
                            store_out(q - 1, e // 2 - 1)
                            load_acc(q - 1, e // 2)
                    if not first:
                        store_out(q - 1, GB - 1)

                sp.dma_start(iota[:], c_iota).then_inc(b_const, 16)
                for d in range(GB + 2):
                    load_x(d, d % GB, d // GB, d % 2, early=d < 2)
                run_turns(sp, turn)
                store_y(NQ - 1, 1, E - 1)
                for bb in range(GB):
                    load_acc(NQ - 1, bb)
                    store_out(NQ - 1, bb)
                sp.wait_ge(out_stored, 16 * NB)
                sp.wait_ge(o_stored, NTI * E * 16 * NQ)

            @block.gpsimd
            def _(pool):
                def gather(q, odd, n):
                    bb, k = n // 2, n % 2
                    if n == 0:
                        pool.wait_ge(o_stored, NTI * E * 16 * (q + 1))
                        pool.wait_ge(rows_made, q + 1)
                    if n > 1:
                        pool.wait_ge(summed, 8 * q + n - 1)
                    apart(pool)
                    for j in range(NT):
                        pool.indirect_dma_start(yg[:, k, j], None, y_dram[odd],
                                                bass.IndirectOffsetOnAxis(ap=rows_q[:, k, bb, j:j + 1], axis=0)
                                                ).then_inc(yg_landed[k], 16)

                def turn(q, odd, first=False, last=False):
                    if not first:
                        for n in range(2 * GB):
                            gather(q - 1, 1 - odd, n)

                run_turns(pool, turn)
                for n in range(2 * GB):
                    gather(NQ - 1, 1, n)

            @block.scalar
            def _(act):
                def keep_high(now, bb, c):
                    d, batch, half = now
                    act.wait_ge(d_ready, 4 * d + 2 * c + 1)
                    act.activation(xb[:, 0, c, half * EH:half * EH + EH, bb],
                                   ps_x[:, 0, 0:SLOTS // 2].rearrange("p (e s) -> p e s", s=CAP), ACT.Copy
                                   ).then_inc(xb_hi, 1)

                def hidden(q, e, half, now=None, bb=0):
                    number = 2 * (E * q + e) + half
                    again = e or half or not first_batch(q)
                    if e or not first_batch(q):
                        if half == 0:
                            act.wait_ge(halves, E * q + e)
                        else:
                            act.wait_ge(o_ready, NTI * (E * q + e))
                    for k in range(MH):
                        if now and k in (0, 1):
                            keep_high(now, bb, k)
                        if k % 2 == 0 and again:
                            act.wait_ge(h_lo, 2 * (number - 1) + k // 2 + 1)
                        act.wait_ge(h_ready, MH * number + k + 1)
                        m = half * MH + k
                        for dst in (relu[:, k], hs[:, half, 0, k]):
                            last = act.activation(dst, ps_h[:, k % H_BANKS, 0:GS], ACT.Relu, bias=b1s[:, e, m:m + 1],
                                                  scale=sc(UP_SC))
                        last.then_inc(relued, 1)

                def turn(q, odd, first=False, last=False):
                    for e in range(E):
                        now = dispatched(q, e, last)
                        hidden(q, e, 1, now, e % GB)
                        if e < E - 1:
                            hidden(q, e + 1, 0)
                        elif not last:
                            hidden(q + 1, 0, 0)

                for bb in range(GB):
                    for c in range(NC):
                        keep_high((bb, bb, 0), bb, c)
                hidden(0, 0, 0)
                run_turns(act, turn)

            @block.vector
            def _(dve):
                def keep_low(now, bb):
                    d, batch, half = now
                    for c in range(NC):
                        dve.wait_ge(d_ready, 4 * d + 2 * c + 2)
                        dve.tensor_copy(xb[:, 1, c, half * EH:half * EH + EH, bb],
                                        ps_x[:, 1, 0:SLOTS // 2].rearrange("p (e s) -> p e s", s=CAP)
                                        ).then_inc(xb_lo, 1)

                def fill_slots(d, batch, half, parity, early=False):
                    if not early:
                        dve.wait_ge(d_ready, 4 * (d - 1))
                    dve.tensor_tensor(place[:, parity],
                                      iota[:].rearrange("p (n o s) -> p n o s", n=1, o=1).to_broadcast([P, NT, EH, CAP]),
                                      pos_slot[:, batch, :, half * EH:half * EH + EH]
                                      .rearrange("p j (e o) -> p j e o", o=1).to_broadcast([P, NT, EH, CAP]),
                                      ALU.is_equal).then_inc(placed, 1)

                def low_h(q, e, half, pair):
                    number = 2 * (E * q + e) + half
                    dve.wait_ge(relued, MH * number + 2 * pair + 2)
                    at = 2 * pair
                    dve.tensor_tensor(hs[:, half, 1, at:at + 2], relu[:, at:at + 2], hs[:, half, 0, at:at + 2],
                                      ALU.subtract).then_inc(h_lo, 1)

                def keep_y(q, e):
                    for t, (lo, hi) in enumerate(TILES):
                        u = NTI * (E * q + e) + t
                        dve.wait_ge(o_ready, u + 1)
                        if e or not first_batch(q):
                            dve.wait_ge(o_stored, NTI * 16 * (E * q + e))
                        dve.scalar_tensor_tensor(yo[0:hi - lo, t], ps_o[0:hi - lo, t, 0:C],
                                                 scales[0:hi - lo, DOWN_SC:DOWN_SC + 1], b2b[0:hi - lo, e],
                                                 ALU.mult, ALU.add).then_inc(o_kept, 1)

                def add_term(q, n):
                    bb, k = n // 2, n % 2
                    b = GB * q + bb
                    if k == 0:
                        dve.wait_ge(acc_landed, 16 * (b + 1))
                    else:
                        dve.wait_ge(summed, 8 * q + n)
                    dve.wait_ge(yg_landed[k], NT * 16 * (GB * q + bb + 1))
                    for j in range(NT):
                        last = dve.scalar_tensor_tensor(acc[:, j], yg[:, k, j], weight[:, k, b, j:j + 1], acc[:, j],
                                                        ALU.mult, ALU.add)
                    last.then_inc(summed, 1)

                def rows_for(q):
                    dve.tensor_copy(rows_q[:], row_of[:, :, bass.ds(GB * q, GB)]).then_inc(rows_made, 1)

                def turn(q, odd, first=False, last=False):
                    for e in range(E):
                        now = dispatched(q, e, last)
                        if e > 0:
                            keep_y(q, e - 1)
                        elif not first:
                            keep_y(q - 1, E - 1)
                            rows_for(q - 1)
                        if now:
                            keep_low(now, e % GB)
                        low_h(q, e, 1, 0)
                        nxt = dispatched(q, e + 2, last)
                        if nxt:
                            fill_slots(*nxt, e % 2)
                        low_h(q, e, 1, 1)
                        if not first:
                            add_term(q - 1, e)
                        for pair in range(MH // 2):
                            if e < E - 1:
                                low_h(q, e + 1, 0, pair)
                            elif not last:
                                low_h(q + 1, 0, 0, pair)

                dve.wait_ge(b_const, 16)
                fill_slots(0, 0, 0, 0, early=True)
                fill_slots(1, 1, 0, 1, early=True)
                for bb in range(GB):
                    keep_low((bb, bb, 0), bb)
                    d = bb + 2
                    fill_slots(d, d % GB, d // GB, d % 2)
                for pair in range(MH // 2):
                    low_h(0, 0, 0, pair)
                run_turns(dve, turn)
                keep_y(NQ - 1, E - 1)
                rows_for(NQ - 1)
                for n in range(2 * GB):
                    add_term(NQ - 1, n)

            @block.tensor
            def _(pe):
                def dispatch(d, parity, landed, c, first=False):
                    if c == 0:
                        pe.wait_ge(xg_landed[parity], landed)
                        pe.wait_ge(placed, d + 1)
                    for part in range(2):
                        if c or not first:
                            pe.wait_ge(xb_lo if part else xb_hi, 2 * d + c)
                        for j in range(NT):
                            last = pe.matmul(ps_x[:, part, 0:SLOTS // 2], xg[:, parity, j, part, c * P:(c + 1) * P],
                                             place[:, parity, j].rearrange("p e s -> p (e s)"),
                                             start=(j == 0), stop=(j == NT - 1))
                        last.then_inc(d_ready, 1)

                def up(q, e, half, k):
                    number = 2 * (E * q + e) + half
                    if e % EH == 0 and half == 0 and k == 0:
                        pe.wait_ge(xb_hi, 4 * GB * q + 2 * GB * (e // EH + 1))
                        pe.wait_ge(xb_lo, 4 * GB * q + 2 * GB * (e // EH + 1))
                    if k >= H_BANKS or half or e or not first_batch(q):
                        pe.wait_ge(relued, MH * number + k - H_BANKS + 1)
                    terms = [(l, r, c) for c in range(NC) for l, r in ((0, 0), (1, 0), (0, 1))]
                    at = (half * MH + k) * P
                    for n, (l, r, c) in enumerate(terms):
                        last = pe.matmul(ps_h[:, k % H_BANKS, 0:GS], w1s[:, l, c, e, at:at + P],
                                         xb[:, r, c, e].rearrange("p b s -> p (b s)"),
                                         start=(n == 0), stop=(n == len(terms) - 1))
                    last.then_inc(h_ready, 1)

                def down(q, e, half, k):
                    if k % 2 == 0:
                        pe.wait_ge(h_lo, 2 * (2 * (E * q + e) + half) + k // 2 + 1)
                    for t, (lo, hi) in enumerate(TILES):
                        if half == 0 and k == 0 and (e or not first_batch(q)):
                            pe.wait_ge(o_kept, NTI * (E * q + e - 1) + t + 1)
                        for n, (l, r) in enumerate(((0, 0), (0, 1), (1, 0))):
                            last = pe.matmul(ps_o[0:hi - lo, t, 0:C], hs[:, half, l, k, lo:hi],
                                             w2s[:, r, half * MH + k, e],
                                             start=(half == 0 and k == 0 and n == 0),
                                             stop=(half == 1 and k == MH - 1 and n == 2), skip_group_check=True)
                        if half == 1 and k == MH - 1:
                            last.then_inc(o_ready, 1)
                        if half == 0 and k == MH - 1 and t == NTI - 1:
                            last.then_inc(halves, 1)

                def turn(q, odd, first=False, last=False):
                    for e in range(E):
                        now = dispatched(q, e, last)
                        for k in range(MH):
                            if now and k in (0, 1):
                                dispatch(now[0], e % 2, 16 * (GB * q + GB // 2 + e // 2 + 1), k)
                            up(q, e, 1, k)
                            down(q, e, 0, k)
                        for k in range(MH):
                            if e < E - 1:
                                up(q, e + 1, 0, k)
                            elif not last:
                                up(q + 1, 0, 0, k)
                            down(q, e, 1, k)

                for bb in range(GB):
                    for c in range(NC):
                        dispatch(bb, bb % 2, 16 * (bb // 2 + 1), c, first=bb == 0)
                for k in range(MH):
                    up(0, 0, 0, k)
                run_turns(pe, turn)


def program(nc, x, waT, wpT, wr, w1, b1T, w2, b2, c_mask, c_kbias, c_ident, c_ident32, c_maskT, c_tri, c_erank, c_erow, c_brow,
            c_iota, out):
    NB = x.shape[0]
    xhl_dram = nc.dram_tensor("xhl_scratch", [NB, P, NT, 2, C], F16, kind="Internal").ap()
    acc_dram = nc.dram_tensor("acc_scratch", [NB, P, NT, C], F32, kind="Internal").ap()
    qk_dram = nc.dram_tensor("qk_scratch", [NB, 2, 2, 3, P, T], F16, kind="Internal").ap()
    y_dram = [nc.dram_tensor(f"y_scratch{n}", [E * GS, C], F32, kind="Internal").ap() for n in range(2)]
    with ExitStack() as top:
        def lasting(name, shape, dt):
            return top.enter_context(nc.sbuf_tensor(name, shape, dt))

        spare = lasting("spare", [P, max(NT * C, NB * NT * E)], F32)
        logits = spare[:, 0:NB * NT * E].rearrange("p (b j e) -> p b j e", b=NB, j=NT)
        scales = lasting("scales", [P, BOUND + 1], F32)
        attention_phase(nc, top, x, waT, wpT, wr, w1, w2, c_mask, c_kbias, c_ident, c_ident32, c_maskT, xhl_dram, acc_dram,
                        qk_dram, logits, scales)
        pos_slot = lasting("pos_slot", [P, NB, NT, E], F16)
        weight = lasting("weight", [P, 2, NB, NT], F32)
        row_of = lasting("row_of", [P, 2, NB, NT], I32)
        w1s = lasting("w1s", [P, 2, NC, E, HF], F16)
        w2s = lasting("w2s", [P, 2, NM, E, C], F16)
        b1s = lasting("b1s", [P, E, NM], F32)
        b2b = lasting("b2b", [P, E, C], F32)
        routing_phase(nc, top, w1, b1T, w2, b2, c_tri, c_erank, c_erow, c_brow, logits, scales, pos_slot, weight,
                      row_of, w1s, w2s, b1s, b2b)
        expert_phase(nc, top, c_iota, xhl_dram, acc_dram, y_dram, out, scales, spare, pos_slot, weight, row_of,
                     w1s, w2s, b1s, b2b)


def constants(nb):
    import numpy as np

    start = 2.0 ** (-0.5)
    slopes = np.array([start * start ** i for i in range(NH)], dtype=np.float32).astype(np.float64)
    keys = np.arange(T)
    rest = slopes[:, None] * keys[None, :] * ALIBI_UP
    parts = []
    for _ in range(3):
        part = rest.astype(np.float16)
        parts.append(part)
        rest = rest - part.astype(np.float64)
    mask_q = np.zeros((P, T), np.float32)
    mask_q[:, T - P:] = np.where(np.arange(P)[None, :] > np.arange(P)[:, None], -BIG, 0.0)
    mask_k = np.where(np.arange(P)[:, None] > np.arange(P)[None, :], -BIG, 0.0)

    def bf16_bits(a):
        return (np.asarray(a, np.float32).view(np.uint32) >> 16).astype(np.uint16)

    return {
        "c_mask": mask_q,
        "c_kbias": np.stack(parts),
        "c_ident": np.eye(P, dtype=np.float16),
        "c_ident32": np.eye(P, dtype=np.float32),
        "c_maskT": bf16_bits(np.stack([mask_k, np.eye(P)])),
        "c_tri": bf16_bits(np.stack([np.triu(np.ones((P, P)), 1), np.ones((P, P))])),
        "c_erank": np.tile(np.arange(E, 0, -1, dtype=np.float32), (P, 1)),
        "c_erow": np.tile(np.arange(E, dtype=np.float32) * GS, (P, 1)),
        "c_brow": np.tile(np.array([b % GB * CAP for b in range(nb)], np.float32), (P, 1)),
        "c_iota": np.tile(np.arange(CAP, dtype=np.float16), (P, 1)),
    }


def qkv_columns(w):
    import numpy as np

    qk = w[:2 * C].reshape(2, 2, HALF, HD, C).transpose(0, 1, 3, 2, 4).reshape(2 * C, C)
    return np.concatenate([qk, w[2 * C:]]).T


def kernel(L0_attn_x, L0_attn_w_attn, L0_attn_w_proj, L0_ffn_Wr, L0_ffn_W1, L0_ffn_b1, L0_ffn_W2, L0_ffn_b2):
    import numpy as np
    import concourse.bacc as bacc
    from concourse.bass_utils import run_bass_kernel_spmd

    x = np.ascontiguousarray(L0_attn_x)
    arrays = {
        "x": x,
        "waT": np.ascontiguousarray(qkv_columns(np.asarray(L0_attn_w_attn))),
        "wpT": np.ascontiguousarray(np.asarray(L0_attn_w_proj).T),
        "wr": np.ascontiguousarray(L0_ffn_Wr),
        "w1": np.ascontiguousarray(L0_ffn_W1),
        "b1T": np.ascontiguousarray(np.asarray(L0_ffn_b1).reshape(E, NM, P).transpose(2, 0, 1)),
        "w2": np.ascontiguousarray(L0_ffn_W2),
        "b2": np.ascontiguousarray(L0_ffn_b2),
        **constants(x.shape[0]),
    }
    nc = bacc.Bacc("TRN2", target_bir_lowering=False, num_devices=1)
    aps = {name: nc.dram_tensor(name, a.shape, mybir.dt.from_np(a.dtype), kind="ExternalInput").ap()
           for name, a in arrays.items()}
    out = nc.dram_tensor("out", x.shape, mybir.dt.from_np(x.dtype), kind="ExternalOutput").ap()
    program(nc, out=out, **aps)
    r = run_bass_kernel_spmd(nc, [arrays], core_ids=[0])
    return r.results[0]["out"]
```
